# Optimizing a Trainium2 kernel written in Bass

```python
import numpy as np
import jax
import jax.numpy as jnp

def _softmax(x, axis=-1):
    return jax.nn.softmax(x, axis=axis)

def _gelu(x):
    return jax.nn.gelu(x, approximate=True)

def _silu(x):
    return jax.nn.silu(x)

def _sigmoid(x):
    return jax.nn.sigmoid(x)

def _layernorm(x, axis=-1, eps=1e-05):
    m = jnp.mean(x, axis=axis, keepdims=True)
    v = jnp.var(x, axis=axis, keepdims=True)
    return (x - m) / jnp.sqrt(v + eps)

def _scatter_add(tgt, idx, src, axis=0):
    return tgt.at[idx].add(src)

def _segment_sum(src, seg, n):
    return jax.ops.segment_sum(src, seg, n)
kernel_name = 'mk_lm_tower_d2_tok_ids256_r4_e0a63b'

def setup_inputs(seed: int=0):
    np.random.seed(seed)
    _w = jnp.asarray

    def _rec_inputs():
        import jax
        import jax.numpy as jnp
        _rk = jax.random.key(seed)
        x = jax.random.randint(jax.random.fold_in(_rk, 1), (16, 1024), 0, 12564, jnp.int32)
        return x
    x = _rec_inputs()

    def _L0_tok_setup():
        import jax, jax.numpy as jnp
        import numpy as np
        INP_SIZE = 50257
        HIDDEN = 64
        KSIZE = 9
        B, T = (16, 1024)
        key = jax.random.key(seed)
        k1, k2, k3, k4 = jax.random.split(key, 4)
        x = jax.random.randint(k1, (B, T), 0, INP_SIZE, dtype=jnp.int64 if jax.config.jax_enable_x64 else jnp.int32)
        emb = jax.random.normal(k2, (INP_SIZE, HIDDEN), dtype=jnp.float32) * 0.02
        fan_in = HIDDEN * KSIZE
        bound = 1.0 / np.sqrt(fan_in)
        W = jax.random.uniform(k3, (HIDDEN, HIDDEN, KSIZE), dtype=jnp.float32, minval=-bound, maxval=bound)
        b = jax.random.uniform(k4, (HIDDEN,), dtype=jnp.float32, minval=-bound, maxval=bound)
        return {'x': x, 'emb': emb, 'W': W, 'b': b}
    _L0_tok_all = _L0_tok_setup()
    _L0_tok_in = {k: v for k, v in _L0_tok_all.items() if k in ('emb', 'W', 'b')}
    del _L0_tok_all

    def _L0_attn_setup():
        import jax, jax.numpy as jnp
        import numpy as np
        H, D = (8, 32)
        EPS = 1e-05
        key = jax.random.key(seed)
        ks = jax.random.split(key, 4)
        B, N, C = (2, 512, 64)
        inner = H * D
        return {'node_features': jax.random.normal(ks[0], (B, N, C), jnp.float32), 'ln_gamma': jnp.ones((C,), jnp.float32), 'ln_beta': jnp.zeros((C,), jnp.float32), 'W_qkv': jax.random.normal(ks[1], (3 * inner, C), jnp.float32) * 0.02, 'W_gate': jax.random.normal(ks[2], (inner, C), jnp.float32) * 0.02, 'b_gate': jnp.ones((inner,), jnp.float32), 'W_final': jax.random.normal(ks[3], (C, inner), jnp.float32) * 0.02, 'b_final': jnp.zeros((C,), jnp.float32)}
    _L0_attn_all = _L0_attn_setup()
    _L0_attn_in = {k: v for k, v in _L0_attn_all.items() if k in ('ln_gamma', 'ln_beta', 'W_qkv', 'W_gate', 'b_gate', 'W_final', 'b_final')}
    del _L0_attn_all

    def _L0_ffn_setup():
        import jax, jax.numpy as jnp
        import numpy as np
        TOP_K = 2
        LN_EPS = 1e-05
        key = jax.random.key(seed)
        ks = jax.random.split(key, 8)
        B, S, D, E, H = (16, 256, 64, 8, 256)
        x = jax.random.normal(ks[0], (B, S, D), dtype=jnp.float32)
        Wr = jax.random.normal(ks[1], (D, E), dtype=jnp.float32) * 0.1
        br = jnp.zeros((E,), dtype=jnp.float32)
        ln_g = jnp.ones((E, D), dtype=jnp.float32)
        ln_b = jnp.zeros((E, D), dtype=jnp.float32)
        W1 = jax.random.normal(ks[2], (E, D, H), dtype=jnp.float32) * (1.0 / np.sqrt(D))
        b1 = jnp.zeros((E, H), dtype=jnp.float32)
        W2 = jax.random.normal(ks[3], (E, H, D), dtype=jnp.float32) * (1.0 / np.sqrt(H))
        b2 = jnp.zeros((E, D), dtype=jnp.float32)
        return {'x': x, 'Wr': Wr, 'br': br, 'ln_g': ln_g, 'ln_b': ln_b, 'W1': W1, 'b1': b1, 'W2': W2, 'b2': b2}
    _L0_ffn_all = _L0_ffn_setup()
    _L0_ffn_in = {k: v for k, v in _L0_ffn_all.items() if k in ('Wr', 'br', 'ln_g', 'ln_b', 'W1', 'b1', 'W2', 'b2')}
    del _L0_ffn_all

    def _L1_attn_setup():
        import jax, jax.numpy as jnp
        import numpy as np
        B, N, D = (8, 512, 64)
        S = 128
        H = int(2.0 * D)
        EPS = 1e-05
        key = jax.random.key(seed)
        ks = jax.random.split(key, 4)
        x = jax.random.normal(ks[0], (B, N, D), dtype=jnp.float32)
        g = jnp.ones((), jnp.float32)
        W_uv = jax.random.normal(ks[1], (D, 2 * H + S), jnp.float32) * 0.02
        b_uv = jnp.zeros((2 * H + S,), jnp.float32)
        gamma = jnp.ones((2, S), jnp.float32)
        beta = jnp.zeros((2, S), jnp.float32)
        W_o = jax.random.normal(ks[2], (H, D), jnp.float32) * 0.02
        b_o = jnp.zeros((D,), jnp.float32)
        return {'x': x, 'g': g, 'W_uv': W_uv, 'b_uv': b_uv, 'gamma': gamma, 'beta': beta, 'W_o': W_o, 'b_o': b_o}
    _L1_attn_all = _L1_attn_setup()
    _L1_attn_in = {k: v for k, v in _L1_attn_all.items() if k in ('g', 'W_uv', 'b_uv', 'gamma', 'beta', 'W_o', 'b_o')}
    del _L1_attn_all

    def _L1_ffn_setup():
        import math
        import jax, jax.numpy as jnp
        import numpy as np
        CAPACITY_FACTOR = 1.25
        TOP_K = 2
        LN_EPS = 1e-05

        def _layer_norm(x, gamma, beta):
            mu = jnp.mean(x, axis=-1, keepdims=True)
            var = jnp.var(x, axis=-1, keepdims=True)
            return (x - mu) * jax.lax.rsqrt(var + LN_EPS) * gamma + beta
        key = jax.random.key(seed)
        ks = jax.random.split(key, 4)
        B, S, D, F, E = (8, 1024, 64, 128, 8)
        x = jax.random.normal(ks[0], (B, S, D), dtype=jnp.float32)
        Wr = jax.random.normal(ks[1], (D, E), dtype=jnp.float32) / np.sqrt(D)
        br = jnp.zeros((E,), jnp.float32)
        W1 = jax.random.normal(ks[2], (E, D, F), dtype=jnp.float32) / np.sqrt(D)
        b1 = jnp.zeros((E, F), jnp.float32)
        W2 = jax.random.normal(ks[3], (E, F, D), dtype=jnp.float32) / np.sqrt(F)
        b2 = jnp.zeros((E, D), jnp.float32)
        gamma = jnp.ones((D,), jnp.float32)
        beta = jnp.zeros((D,), jnp.float32)
        return {'x': x, 'Wr': Wr, 'br': br, 'W1': W1, 'b1': b1, 'W2': W2, 'b2': b2, 'gamma': gamma, 'beta': beta}
    _L1_ffn_all = _L1_ffn_setup()
    _L1_ffn_in = {k: v for k, v in _L1_ffn_all.items() if k in ('Wr', 'br', 'W1', 'b1', 'W2', 'b2', 'gamma', 'beta')}
    del _L1_ffn_all
    return {'x': x, 'L0_tok_emb': _L0_tok_in['emb'], 'L0_tok_W': _L0_tok_in['W'], 'L0_tok_b': _L0_tok_in['b'], 'L0_attn_ln_gamma': _L0_attn_in['ln_gamma'], 'L0_attn_ln_beta': _L0_attn_in['ln_beta'], 'L0_attn_W_qkv': _L0_attn_in['W_qkv'], 'L0_attn_W_gate': _L0_attn_in['W_gate'], 'L0_attn_b_gate': _L0_attn_in['b_gate'], 'L0_attn_W_final': _L0_attn_in['W_final'], 'L0_attn_b_final': _L0_attn_in['b_final'], 'L0_ffn_Wr': _L0_ffn_in['Wr'], 'L0_ffn_br': _L0_ffn_in['br'], 'L0_ffn_ln_g': _L0_ffn_in['ln_g'], 'L0_ffn_ln_b': _L0_ffn_in['ln_b'], 'L0_ffn_W1': _L0_ffn_in['W1'], 'L0_ffn_b1': _L0_ffn_in['b1'], 'L0_ffn_W2': _L0_ffn_in['W2'], 'L0_ffn_b2': _L0_ffn_in['b2'], 'L1_attn_g': _L1_attn_in['g'], 'L1_attn_W_uv': _L1_attn_in['W_uv'], 'L1_attn_b_uv': _L1_attn_in['b_uv'], 'L1_attn_gamma': _L1_attn_in['gamma'], 'L1_attn_beta': _L1_attn_in['beta'], 'L1_attn_W_o': _L1_attn_in['W_o'], 'L1_attn_b_o': _L1_attn_in['b_o'], 'L1_ffn_Wr': _L1_ffn_in['Wr'], 'L1_ffn_br': _L1_ffn_in['br'], 'L1_ffn_W1': _L1_ffn_in['W1'], 'L1_ffn_b1': _L1_ffn_in['b1'], 'L1_ffn_W2': _L1_ffn_in['W2'], 'L1_ffn_b2': _L1_ffn_in['b2'], 'L1_ffn_gamma': _L1_ffn_in['gamma'], 'L1_ffn_beta': _L1_ffn_in['beta']}

def reference(x, L0_tok_emb, L0_tok_W, L0_tok_b, L0_attn_ln_gamma, L0_attn_ln_beta, L0_attn_W_qkv, L0_attn_W_gate, L0_attn_b_gate, L0_attn_W_final, L0_attn_b_final, L0_ffn_Wr, L0_ffn_br, L0_ffn_ln_g, L0_ffn_ln_b, L0_ffn_W1, L0_ffn_b1, L0_ffn_W2, L0_ffn_b2, L1_attn_g, L1_attn_W_uv, L1_attn_b_uv, L1_attn_gamma, L1_attn_beta, L1_attn_W_o, L1_attn_b_o, L1_ffn_Wr, L1_ffn_br, L1_ffn_W1, L1_ffn_b1, L1_ffn_W2, L1_ffn_b2, L1_ffn_gamma, L1_ffn_beta):
    import jax
    import jax.numpy as jnp

    def _L0_tok_ref(x, emb, W, b):
        import jax, jax.numpy as jnp
        import numpy as np
        INP_SIZE = 50257
        HIDDEN = 64
        KSIZE = 9
        B, T = (16, 1024)
        offsets = jnp.arange(-(KSIZE // 2), KSIZE // 2 + 1)
        idx = jnp.clip(x[..., None] + offsets, 0, INP_SIZE - 1)
        gathered = emb[idx]
        out = jnp.einsum('btkh,ohk->bto', gathered, W) + b
        return out

    def _L0_attn_ref(node_features, ln_gamma, ln_beta, W_qkv, W_gate, b_gate, W_final, b_final):
        import jax, jax.numpy as jnp
        import numpy as np
        H, D = (8, 32)
        EPS = 1e-05
        x = node_features
        B, N, _ = x.shape
        mu = jnp.mean(x, axis=-1, keepdims=True)
        var = jnp.mean(jnp.square(x - mu), axis=-1, keepdims=True)
        normed = (x - mu) / jnp.sqrt(var + EPS) * ln_gamma + ln_beta
        qkv = normed @ W_qkv.T
        q, k, v = jnp.split(qkv, 3, axis=-1)

        def to_heads(t):
            return t.reshape(B, N, H, D).transpose(0, 2, 1, 3)
        q, k, v = (to_heads(q), to_heads(k), to_heads(v))
        gate = jax.nn.sigmoid(to_heads(x @ W_gate.T + b_gate))
        scores = jnp.einsum('bhid,bhjd->bhij', q, k) * D ** (-0.5)
        attn = jax.nn.softmax(scores, axis=-1)
        out = jnp.einsum('bhij,bhid->bhjd', attn, v) * gate
        out = out.transpose(0, 2, 1, 3).reshape(B, N, H * D)
        return x + out @ W_final.T + b_final

    def _L0_ffn_ref(x, Wr, br, ln_g, ln_b, W1, b1, W2, b2):
        import jax, jax.numpy as jnp
        import numpy as np
        TOP_K = 2
        LN_EPS = 1e-05
        B, S, D = x.shape
        N = B * S
        xt = x.reshape(N, D)
        logits = xt @ Wr + br
        probs = jax.nn.softmax(logits, axis=-1)
        top_p, top_idx = jax.lax.top_k(probs, TOP_K)
        weights = top_p / top_p.sum(axis=-1, keepdims=True)
        mu = xt.mean(axis=-1, keepdims=True)
        var = ((xt - mu) ** 2).mean(axis=-1, keepdims=True)
        xn = (xt - mu) * jax.lax.rsqrt(var + LN_EPS)
        xe = xn[None, :, :] * ln_g[:, None, :] + ln_b[:, None, :]
        h = jax.nn.gelu(jnp.einsum('end,edh->enh', xe, W1) + b1[:, None, :], approximate=False)
        y = jnp.einsum('enh,ehd->end', h, W2) + b2[:, None, :]
        y_tok = jnp.transpose(y, (1, 0, 2))
        sel = jnp.take_along_axis(y_tok, top_idx[:, :, None], axis=1)
        out = (weights[:, :, None] * sel).sum(axis=1)
        return out.reshape(B, S, D)

    def _L1_attn_ref(x, g, W_uv, b_uv, gamma, beta, W_o, b_o):
        import jax, jax.numpy as jnp
        import numpy as np
        B, N, D = (8, 512, 64)
        S = 128
        H = int(2.0 * D)
        EPS = 1e-05
        d = x.shape[-1]
        norm = jnp.linalg.norm(x, axis=-1, keepdims=True) * jax.lax.rsqrt(jnp.float32(d))
        xn = x / jnp.maximum(norm, EPS) * g
        uv = jax.nn.silu(jnp.einsum('bnd,de->bne', xn, W_uv) + b_uv)
        u = uv[..., :H]
        v = uv[..., H:2 * H]
        base = uv[..., 2 * H:]
        q = base * gamma[0] + beta[0]
        k = base * gamma[1] + beta[1]
        qk = jnp.einsum('bns,bms->bnm', q, k) * jax.lax.rsqrt(jnp.float32(S))
        attn = jnp.square(jax.nn.relu(qk))
        gated = u * jnp.einsum('bnm,bmh->bnh', attn, v)
        return jnp.einsum('bnh,hd->bnd', gated, W_o) + b_o

    def _L1_ffn_ref(x, Wr, br, W1, b1, W2, b2, gamma, beta):
        import math
        import jax, jax.numpy as jnp
        import numpy as np
        CAPACITY_FACTOR = 1.25
        TOP_K = 2
        LN_EPS = 1e-05

        def _layer_norm(x, gamma, beta):
            mu = jnp.mean(x, axis=-1, keepdims=True)
            var = jnp.var(x, axis=-1, keepdims=True)
            return (x - mu) * jax.lax.rsqrt(var + LN_EPS) * gamma + beta
        B, S, D = x.shape
        E = Wr.shape[1]
        N = B * S
        K = TOP_K
        logits = jnp.mean(x, axis=1) @ Wr + br
        routing_weights = jax.nn.softmax(logits, axis=-1)
        capacity = float(math.ceil(N * CAPACITY_FACTOR / E))
        expected_loads = routing_weights.sum(axis=0) * (N / B)
        scale = jnp.where(expected_loads > capacity, capacity / expected_loads, 1.0)
        routing_weights = jax.nn.softmax(routing_weights * scale, axis=-1)
        rw_tok = jnp.broadcast_to(routing_weights[:, None, :], (B, S, E)).reshape(N, E)
        top_w, top_i = jax.lax.top_k(rw_tok, K)
        top_w = jax.nn.softmax(top_w, axis=-1)
        xf = x.reshape(N, D)
        h = jax.nn.gelu(jnp.einsum('nd,edf->enf', xf, W1) + b1[:, None, :], approximate=False)
        y = jnp.einsum('enf,efd->end', h, W2) + b2[:, None, :]
        w_dense = jnp.zeros((N, E), x.dtype).at[jnp.arange(N)[:, None], top_i].add(top_w)
        out = jnp.einsum('ne,end->nd', w_dense, y).reshape(B, S, D)
        out = _layer_norm(out + x, gamma, beta)
        return out
    h = _L0_tok_ref(x, L0_tok_emb, L0_tok_W, L0_tok_b)
    h = h + _L0_attn_ref(_layernorm(h, axis=-1), L0_attn_ln_gamma, L0_attn_ln_beta, L0_attn_W_qkv, L0_attn_W_gate, L0_attn_b_gate, L0_attn_W_final, L0_attn_b_final)
    h = h + _L0_ffn_ref(_layernorm(h, axis=-1), L0_ffn_Wr, L0_ffn_br, L0_ffn_ln_g, L0_ffn_ln_b, L0_ffn_W1, L0_ffn_b1, L0_ffn_W2, L0_ffn_b2)
    h = h + _L1_attn_ref(_layernorm(h, axis=-1), L1_attn_g, L1_attn_W_uv, L1_attn_b_uv, L1_attn_gamma, L1_attn_beta, L1_attn_W_o, L1_attn_b_o)
    h = h + _L1_ffn_ref(_layernorm(h, axis=-1), L1_ffn_Wr, L1_ffn_br, L1_ffn_W1, L1_ffn_b1, L1_ffn_W2, L1_ffn_b2, L1_ffn_gamma, L1_ffn_beta)
    return h

_drawn_inputs = setup_inputs


def setup_inputs(seed=0):
    import zlib

    import numpy as np

    out = dict(_drawn_inputs(seed))
    spreads = {'L0_attn_ln_gamma': (1.0, 0.6),
     'L0_attn_ln_beta': (0.0, 0.8),
     'L0_attn_b_gate': (1.0, 0.6),
     'L0_attn_b_final': (0.0, 0.1),
     'L0_ffn_br': (0.0, 0.1),
     'L0_ffn_ln_g': (1.0, 0.2),
     'L0_ffn_ln_b': (0.0, 0.1),
     'L0_ffn_b1': (0.0, 0.1),
     'L0_ffn_b2': (0.0, 0.1),
     'L1_attn_b_uv': (0.0, 0.1),
     'L1_attn_gamma': (1.0, 0.6),
     'L1_attn_beta': (0.0, 0.8),
     'L1_attn_b_o': (0.0, 0.1),
     'L1_ffn_br': (0.0, 0.8),
     'L1_ffn_b1': (0.0, 0.413),
     'L1_ffn_b2': (0.0, 0.426),
     'L1_ffn_gamma': (1.0, 0.2),
     'L1_ffn_beta': (0.0, 0.298)}
    factors = {'L0_attn_W_gate': 8.0}
    for name, (base, spread) in spreads.items():
        noise = np.random.default_rng([zlib.crc32(name.encode()), seed]).standard_normal(out[name].shape)
        drawn = base * np.exp(spread * noise) if base else spread * noise
        out[name] = jnp.asarray(drawn.astype(out[name].dtype))
    for name, factor in factors.items():
        out[name] = (out[name] * factor).astype(out[name].dtype)
    return out
```

```python
from contextlib import ExitStack

import numpy as np

import concourse.bass as bass
from concourse import mybir

F32 = mybir.dt.float32
F16 = mybir.dt.float16
I32 = mybir.dt.int32
U32 = mybir.dt.uint32
ALU = mybir.AluOpType
ACT = mybir.ActivationFunctionType
AX = mybir.AxisListType

P = 128
NB, T, D = 16, 1024, 64
TILES = T // P
NT = NB * TILES
VOCAB, KS = 50257, 9
PAD = KS - 1
HEADS, DH = 8, 32
GROUPS, HG = 2, 4
SCALE0 = DH ** -0.5
EPS = 1e-5
HALF = 512


class Signal:

    def __init__(self, ctx, nc, name, credits=0):
        self.sem = ctx.enter_context(nc.semaphore(name))
        self.credits = credits
        self.taken = 0

    def open(self, eng):
        eng.sem_inc(self.sem, self.credits)

    def take(self, n=1):
        self.taken += n
        return self.taken

    def settle(self, eng):
        if self.taken:
            eng.sem_inc(self.sem, -self.taken)
        self.taken = 0


def batch(tensor, b):
    return tensor[:, bass.ds(b * TILES, TILES)]


def wide(ap, n):
    return ap.unsqueeze(2).to_broadcast([ap.shape[0], ap.shape[1], n])


def shared(ap, n):
    return ap.unsqueeze(1).to_broadcast([ap.shape[0], n, ap.shape[1]])


def emit_identity(nc, ctx, ident):
    with nc.semaphore("ident_zero") as zeroed, nc.Block() as block:
        @block.gpsimd
        def _(pool):
            pool.memset(ident[:, :], 0.0).then_inc(zeroed, 1)
            pool.wait_ge(zeroed, 1)
            pool.affine_select(out=ident[:, :], in_=ident[:, :], compare_op=ALU.not_equal, fill=1.0,
                               base=0, pattern=[[-1, P]], channel_multiplier=1)


def emit_embedding(nc, x, table, w, bias, h_sb, ident):
    WIN = KS * D
    CHUNKS = 5
    starts = [0, 128, 256, 384, WIN - P]
    with ExitStack() as ctx:
        sb = lambda name, shape, dt=F32: ctx.enter_context(nc.sbuf_tensor(name, shape, dt))
        xi = sb("xi", [P, NT], I32)
        rows = sb("rows", [P, NT], I32)
        idx = sb("idx", [P, 2, TILES], I32)
        win = sb("win", [P, TILES, WIN])
        winT = sb("winT", [P, 4, CHUNKS * P])
        w_sb = sb("conv_w", [P, CHUNKS, D])
        b_bc = sb("conv_b", [P, D])
        psT = [ctx.enter_context(nc.psum_tensor(f"psT{i}", [P, 2 * HALF], F32)) for i in range(2)]
        psO = [ctx.enter_context(nc.psum_tensor(f"psO{i}", [P, HALF], F32)) for i in range(2)]
        s = lambda name, credits=0: Signal(ctx, nc, name, credits)
        x_loaded = ctx.enter_context(nc.semaphore("x_loaded"))
        w_loaded = s("w_loaded")
        b_loaded = s("b_loaded")
        clipped = ctx.enter_context(nc.semaphore("clipped"))
        rows_ready = ctx.enter_context(nc.semaphore("rows_ready"))
        idx_copied = s("idx_copied")
        landed = [ctx.enter_context(nc.semaphore(f"win_landed{t}")) for t in range(TILES)]
        win_free = s("win_free", TILES)
        t_done_a = s("t_done_a")
        t_done_v = s("t_done_v")
        wT_a = s("wT_a")
        wT_v = s("wT_v")
        conv_done = s("conv_done")
        out_read = s("out_read", 2)
        block = ctx.enter_context(nc.Block())

        @block.sync
        def _(sp):
            sp.dma_start(xi[:, :].rearrange("p (b t) -> p b t", t=TILES),
                         x.rearrange("b (p t) -> p b t", t=TILES)).then_inc(x_loaded, 16)
            sp.dma_start(w_sb[:, 0:4, :], w[0:4 * P, :].rearrange("(c p) o -> p c o", p=P)).then_inc(w_loaded.sem, 16)
            sp.dma_start(w_sb[D:P, 4, :], w[4 * P:WIN, :]).then_inc(w_loaded.sem, 16)
            sp.dma_start(b_bc[:, :], bias.partition_broadcast(P)).then_inc(b_loaded.sem, 16)

        @block.gpsimd
        def _(pool):
            win_free.open(pool)
            pool.wait_ge(rows_ready, 1)
            with pool.Fori(0, NB // 2) as b2:
                for par in range(2):
                    pool.tensor_copy(idx[:, par, :], batch(rows, b2 * 2 + par)).then_inc(idx_copied.sem, 1)
                    pool.wait_ge(idx_copied.sem, idx_copied.take())
                    for t in range(TILES):
                        pool.wait_ge(win_free.sem, win_free.take())
                        pool.indirect_dma_start(
                            out=win[:, t, :], out_offset=None, in_=table[:, :],
                            in_offset=bass.IndirectOffsetOnAxis(ap=idx[:, par, t:t + 1], axis=0),
                        ).then_inc(landed[t], 16)
                idx_copied.settle(pool)
                win_free.settle(pool)

        @block.tensor
        def _(pe):
            out_read.open(pe)
            pe.wait_ge(w_loaded.sem, 32)

            def transpose(b, t):
                pe.wait_ge(landed[t], b * 16 + 16)
                for c in range(CHUNKS):
                    last = nc.tensor.transpose(psT[t % 2][:, c * P:(c + 1) * P],
                                               win[:, t, starts[c]:starts[c] + P], ident[:, :])
                last.then_inc(t_done_a.sem if t % 2 == 0 else t_done_v.sem, 1)

            def conv(t, o):
                read = wT_a if t % 2 == 0 else wT_v
                pe.wait_ge(read.sem, read.take())
                for c in range(CHUNKS):
                    lo = 0 if c < 4 else D
                    last = nc.tensor.matmul(psO[o][:, t * D:(t + 1) * D], winT[lo:P, t % 4, c * P:(c + 1) * P],
                                            w_sb[lo:P, c, :], start=(c == 0), stop=(c == CHUNKS - 1))
                return last

            with pe.Fori(0, NB // 2) as b2:
                for par in range(2):
                    transpose(b2 * 2 + par, 0)
                    for t in range(TILES):
                        if t == 0:
                            pe.wait_ge(out_read.sem, out_read.take())
                        if t + 1 < TILES:
                            transpose(b2 * 2 + par, t + 1)
                        last = conv(t, par)
                        if t < TILES - 1:
                            last.then_inc(win_free.sem, 1)
                    last.then_inc(conv_done.sem, 1)
                    pe.drain().then_inc(win_free.sem, 1)
                for q in (wT_a, wT_v, out_read):
                    q.settle(pe)

        @block.scalar
        def _(act):
            with act.Fori(0, NB // 2) as b2:
                for par in range(2):
                    for t in range(0, TILES, 2):
                        act.wait_ge(t_done_a.sem, t_done_a.take())
                        nc.scalar.activation(winT[:, t % 4, :], psT[0][:, 0:CHUNKS * P], ACT.Copy).then_inc(wT_a.sem, 1)
                t_done_a.settle(act)

        @block.vector
        def _(dve):
            dve.wait_ge(x_loaded, 16)
            nc.vector.tensor_scalar(rows[:, :], xi[:, :], float(-(KS // 2)), float(VOCAB - 1 + KS // 2),
                                    ALU.max, ALU.min).then_inc(clipped, 1)
            dve.wait_ge(clipped, 1)
            nc.vector.tensor_scalar(xi[:, :], rows[:, :], float(PAD - KS // 2), None, ALU.add).then_inc(clipped, 1)
            dve.wait_ge(clipped, 2)
            nc.vector.tensor_copy(rows[:, :], xi[:, :]).then_inc(rows_ready, 1)
            dve.wait_ge(b_loaded.sem, 16)
            with dve.Fori(0, NB // 2) as b2:
                for par in range(2):
                    for t in range(1, TILES, 2):
                        dve.wait_ge(t_done_v.sem, t_done_v.take())
                        nc.vector.tensor_copy(winT[:, t % 4, :], psT[1][:, 0:CHUNKS * P]).then_inc(wT_v.sem, 1)
                    dve.wait_ge(conv_done.sem, conv_done.take())
                    nc.vector.tensor_tensor(batch(h_sb, b2 * 2 + par),
                                            psO[par][:, :].rearrange("p (t d) -> p t d", d=D),
                                            shared(b_bc[:, :], TILES), ALU.add).then_inc(out_read.sem, 1)
                t_done_v.settle(dve)
                conv_done.settle(dve)


def emit_layernorm(nc, tag, h_sb, stats, kind, g=None):
    mean, var, r1, r2, s2 = (stats[:, i, :] for i in range(5))
    CH = 4
    n = NT // CH
    with ExitStack() as ctx:
        centred = ctx.enter_context(nc.sbuf_tensor(f"{tag}_centred", [P, 2, n, D], F32))
        g_sb = ctx.enter_context(nc.sbuf_tensor(f"{tag}_g", [P, 1], F32))
        sem = lambda name: ctx.enter_context(nc.semaphore(f"{tag}_{name}"))
        g_loaded = sem("g_loaded")
        summed, meaned, centred_done, squared, var_done, root, chain = (
            sem(x) for x in ("summed", "meaned", "centred", "squared", "var", "root", "chain"))
        block = ctx.enter_context(nc.Block())
        part = lambda t, c: t[:, c * n:(c + 1) * n]

        @block.sync
        def _(sp):
            if kind == "rms":
                sp.dma_start(g_sb[:, :], g.partition_broadcast(P)).then_inc(g_loaded, 16)

        @block.vector
        def _(dve):
            links = [0]

            def link(ins):
                links[0] += 1
                ins.then_inc(chain, 1)
                dve.wait_ge(chain, links[0])

            for c in range(CH):
                nc.vector.reduce_sum(part(mean, c), part(h_sb, c), AX.X).then_inc(summed, 1)
                dve.wait_ge(summed, c + 1)
                nc.vector.tensor_scalar(part(mean, c), part(mean, c), 1.0 / D, None, ALU.mult).then_inc(meaned, 1)
            for c in range(CH):
                dve.wait_ge(squared, c + 1)
                nc.vector.reduce_sum(part(var, c), centred[:, c % 2], AX.X).then_inc(var_done, 1)
            dve.wait_ge(var_done, CH)
            link(nc.vector.tensor_scalar(var, var, 1.0 / D, None, ALU.mult))
            nc.vector.tensor_scalar(r2, var, EPS, None, ALU.add).then_inc(root, 1)
            dve.wait_ge(root, 2)
            link(nc.vector.reciprocal(r1, s2))
            link(nc.vector.tensor_tensor(var, var, r1, ALU.mult))
            link(nc.vector.tensor_tensor(var, var, r1, ALU.mult))
            nc.vector.tensor_scalar(r2, var, EPS if kind == "norm" else 0.0, None, ALU.add).then_inc(root, 1)
            dve.wait_ge(root, 4)
            if kind == "rms":
                link(nc.vector.tensor_scalar(s2, s2, EPS, None, ALU.max))
            link(nc.vector.reciprocal(r2, s2))
            if kind == "rms":
                dve.wait_ge(g_loaded, 16)
                link(nc.vector.tensor_scalar(r2, r2, g_sb[:, :], None, ALU.mult))

        @block.gpsimd
        def _(pool):
            for c in range(CH):
                pool.wait_ge(meaned, c + 1)
                if c >= 2:
                    pool.wait_ge(var_done, c - 1)
                nc.gpsimd.tensor_tensor(centred[:, c % 2], part(h_sb, c), wide(part(mean, c), D),
                                        ALU.subtract).then_inc(centred_done, 1)

        @block.scalar
        def _(act):
            for c in range(CH):
                act.wait_ge(centred_done, c + 1)
                nc.scalar.activation(centred[:, c % 2], centred[:, c % 2], ACT.Square).then_inc(squared, 1)
            act.wait_ge(root, 1)
            nc.scalar.activation(s2, r2, ACT.Sqrt).then_inc(root, 1)
            act.wait_ge(root, 3)
            nc.scalar.activation(s2, r2, ACT.Sqrt).then_inc(root, 1)


RING = 3
EG = 4
UNITS = GROUPS * TILES * HG
LAG = 8
IN_RING = ("score", "xT", "q", "k", "v", "gate", "proj")


class Event:

    def __init__(self, kind, n=0, quarter=0):
        self.kind, self.n, self.quarter, self.slot = kind, n, quarter, None
        self.group, self.tile, self.head = n // (TILES * HG), n // HG % TILES, n % HG


def prep_events():
    return [Event("stage"), Event("base"), Event("xT", 0), Event("xT", 1), Event("q", 0), Event("split_q", 0), Event("k", 0),
            Event("split_k", 0), Event("v", 0), Event("gate", 0)]


def batch_events(has_prev, has_next):
    queries = GROUPS * TILES
    events = []
    for u in range(UNITS + (0 if has_next else LAG)):
        if u < UNITS:
            events.append(Event("score", u))
        k, c = (u - LAG) // HG, (u - LAG) % HG
        if (k, c) in ((0, 0), (TILES, 0)) and (k or has_prev):
            events.append(Event("out", 0 if k else 1))
        if k >= 0 or has_prev:
            events.append(Event("av", k % queries, c))
        if u % HG == 2 and (u > HG or has_prev):
            events.append(Event("values", (u // HG - 1) % queries))
        place = (u // (TILES * HG), u // HG % TILES, u % HG)
        if u < UNITS:
            for at, kind, n in (((0, 2, 2), "q", 1), ((0, 3, 2), "split_q", 1), ((0, 3, 2), "k", 1),
                                ((0, 4, 2), "split_k", 1), ((0, 4, 3), "v", 1), ((0, 5, 2), "gate", 1)):
                if at == place:
                    events.append(Event(kind, n))
            if place == (0, 6, 2) and has_prev:
                events.append(Event("proj"))
            if place == (0, 7, 2) and has_prev:
                events.append(Event("add", -1))
            if has_next:
                for at, kind, n in (((1, 0, 2), "stage", 0), ((1, 1, 2), "base", 0), ((1, 2, 2), "xT", 0), ((1, 2, 3), "xT", 1),
                                    ((1, 3, 3), "q", 0), ((1, 4, 2), "split_q", 0), ((1, 4, 3), "k", 0),
                                    ((1, 5, 2), "split_k", 0), ((1, 5, 3), "v", 0), ((1, 6, 2), "gate", 0)):
                    if at == place:
                        events.append(Event(kind, n))
    if not has_next:
        events += [Event("out", 1), Event("proj", 1), Event("add", 0)]
    return events


def attention_schedule():
    stretches = [prep_events(), batch_events(False, True), batch_events(True, True), batch_events(True, False)]
    at = 0
    for n, events in enumerate(stretches):
        start = at
        for e in events:
            if e.kind in IN_RING:
                e.slot = at % RING
                at += 1
        assert n != 2 or (at - start) % RING == 0, at - start
    return stretches


def emit_attention0(nc, h_sb, stats, ident, wqkv, wgate, bgate, wfin, bfin, gamma, beta):
    mean, r1, r2 = stats[:, 0, :], stats[:, 2, :], stats[:, 3, :]
    schedule = attention_schedule()
    with ExitStack() as ctx:
        sb = lambda name, shape, dt=F32: ctx.enter_context(nc.sbuf_tensor(name, shape, dt))
        w_n = sb("w_qkv", [P, 3 * HEADS * DH])
        w_y = sb("w_gate", [P, HEADS * DH])
        w_f = sb("w_fin", [P, GROUPS, D])
        b_g = sb("b_gate", [P, GROUPS])
        b_f = sb("b_fin", [P, D])
        aff = sb("aff", [P, 2])
        xT = sb("xT", [P, T])
        split_in = [sb(f"split_in{i}", [P, T]) for i in range(2)]
        yn = split_in[0][:, :].rearrange("p (t c) -> p t c", t=TILES)
        pr = split_in[1][:, 0:TILES * D].rearrange("p (t d) -> p t d", d=D)
        hi = [sb(f"split_hi{i}", [P, T], F16) for i in range(2)]
        lo = [sb(f"split_lo{i}", [P, T], F16) for i in range(2)]
        q_st = [sb(f"q_stack{g}", [3 * DH, HG, T], F16) for g in range(GROUPS)]
        k_st = [sb(f"k_stack{g}", [3 * DH, HG, T], F16) for g in range(GROUPS)]
        v_sb = [sb(f"v{g}", [P, TILES, HG * DH]) for g in range(GROUPS)]
        gate = [sb(f"gate{g}", [P, T]) for g in range(GROUPS)]
        gated = [sb(f"gated{g}", [P, T]) for g in range(GROUPS)]
        e_sb = sb("exps", [P, EG, HG, T])
        nmax = sb("nmax", [P, HG])
        zsum = sb("zsum", [P, EG, HG])
        rz = sb("rz", [P, EG, HG])
        vz = sb("vz", [P, EG, HG * DH])
        ring = [ctx.enter_context(nc.psum_tensor(f"ring{i}", [P, T], F32)) for i in range(RING)]
        outT = ctx.enter_context(nc.psum_tensor("outT", [P, T], F32))

        s = lambda name, credits=0: Signal(ctx, nc, name, credits)
        w_loaded = ctx.enter_context(nc.semaphore("w_loaded"))
        w_scaled = s("w_scaled")
        b_scaled = s("b_scaled")
        slot_free = s("slot_free", RING)
        score_done = s("score_done")
        max_done = s("max_done")
        item_done = s("item_done")
        exps_ended = s("exps_ended")
        sums_ended = s("sums_ended")
        rz_done = s("rz_done")
        vz_done = s("vz_done")
        e_free = s("e_free", EG)
        out_free = s("out_free", 1)
        staged = s("staged")
        copied = s("copied")
        projected = s("projected_done")
        split_done = s("split_done")
        stacked = [s(f"stacked{g}") for g in range(GROUPS)]
        pool_done = s("pool_done")
        block = ctx.enter_context(nc.Block())
        LOADS = 7
        STACK_DMAS = 2 * 3 * HG

        def turns(eng, body):
            body(None, 0, schedule[0])
            body(0, 1, schedule[1])
            with eng.Fori(1, NB - 1) as b:
                body(b, b + 1, schedule[2])
            body(NB - 1, None, schedule[3])

        @block.sync
        def _(sp):
            for dst, src in ((w_n[D:P, :], wqkv), (w_y[0:D, :], wgate),
                             (w_f[:, :, :], wfin.rearrange("(g p) o -> p g o", p=P)),
                             (b_g[:, :], bgate),
                             (b_f[:, :], bfin.partition_broadcast(P)),
                             (aff[D:P, 0:1], gamma.unsqueeze(1)), (aff[D:P, 1:2], beta.unsqueeze(1))):
                sp.dma_start(dst, src).then_inc(w_loaded, 16)

            def body(b, b_next, events):
                for e in events:
                    if e.kind not in ("split_q", "split_k"):
                        continue
                    i = 0 if e.kind == "split_q" else 1
                    stack = (q_st, k_st)[i][e.n]
                    parts = ((hi[0], lo[0], hi[0]), (hi[1], hi[1], lo[1]))[i]
                    sp.wait_ge(split_done.sem, split_done.take())
                    for n, part in enumerate(parts):
                        for h in range(HG):
                            sp.dma_start(stack[n * DH:(n + 1) * DH, h, :],
                                         part[h * DH:(h + 1) * DH, :]).then_inc(stacked[e.n].sem, 16)
                split_done.settle(sp)
            turns(sp, body)

        @block.tensor
        def _(pe):
            slot_free.open(pe)
            out_free.open(pe)
            pe.wait_ge(w_loaded, LOADS * 16)
            pe.wait_ge(w_scaled.sem, w_scaled.take())

            def body(b, b_next, events):
                for e in events:
                    if e.kind in IN_RING:
                        tile = ring[e.slot]
                        if e.kind == "score" and e.n % (TILES * HG) == 0:
                            stack = stacked[e.group]
                            pe.wait_ge(stack.sem, stack.take(STACK_DMAS * 16))
                        if e.kind == "xT" and e.n == 0:
                            pe.wait_ge(staged.sem, staged.take())
                        if e.kind == "proj" and e.n == 1:
                            pe.wait_ge(out_free.sem, out_free.take())
                        whole = RING - 1 if b is None and e.kind == "q" else 0
                        pe.wait_ge(slot_free.sem, slot_free.take() + whole)
                    if e.kind == "score":
                        for j in range(2):
                            last = nc.tensor.matmul(tile[:, j * HALF:(j + 1) * HALF],
                                                    q_st[e.group][:, e.head, e.tile * P:(e.tile + 1) * P],
                                                    k_st[e.group][:, e.head, j * HALF:(j + 1) * HALF],
                                                    start=True, stop=True)
                        last.then_inc(score_done.sem, 1)
                    elif e.kind == "av":
                        c, first = e.quarter, e.n % TILES == 0
                        if c == 0:
                            pe.wait_ge(vz_done.sem, vz_done.take())
                        if c == 0 and first:
                            pe.wait_ge(out_free.sem, out_free.take())
                        quarter = slice(c * T // 4, (c + 1) * T // 4)
                        for h in range(HG):
                            last = nc.tensor.matmul(outT[h * DH:(h + 1) * DH, quarter],
                                                    vz[:, e.n % EG, h * DH:(h + 1) * DH],
                                                    e_sb[:, e.n % EG, h, quarter], start=first and c % 2 == 0,
                                                    stop=e.n % TILES == TILES - 1, skip_group_check=True)
                        if c == 3:
                            last.then_inc(e_free.sem, 1)
                    elif e.kind == "xT":
                        for t in range(TILES // 2):
                            last = nc.tensor.transpose(tile[:, t * P:(t + 1) * P], yn[:, e.n * TILES // 2 + t, :],
                                                       ident[:, :])
                        last.then_inc(item_done.sem, 1)
                    elif e.kind in ("q", "k", "gate"):
                        col = e.n * P + (HEADS * DH if e.kind == "k" else 0)
                        w, rows = (w_y, slice(0, D)) if e.kind == "gate" else (w_n, slice(D, P))
                        for j in range(2):
                            last = nc.tensor.matmul(tile[:, j * HALF:(j + 1) * HALF], w[rows, col:col + P],
                                                    xT[rows, j * HALF:(j + 1) * HALF], start=True, stop=True)
                        last.then_inc(item_done.sem, 1)
                    elif e.kind == "v":
                        col = 2 * HEADS * DH + e.n * P
                        for t in range(TILES):
                            last = nc.tensor.matmul(tile[:, t * P:(t + 1) * P], xT[D:P, t * P:(t + 1) * P],
                                                    w_n[D:P, col:col + P], start=True, stop=True)
                        last.then_inc(item_done.sem, 1)
                    elif e.kind == "proj":
                        for t in range(TILES):
                            for g in range(GROUPS):
                                last = nc.tensor.matmul(tile[:, t * D:(t + 1) * D], gated[g][:, t * P:(t + 1) * P],
                                                        w_f[:, g, :], start=(g == 0), stop=(g == 1))
                        last.then_inc(item_done.sem, 1)
                    elif e.kind == "out" and b_next is None and e is events[-3]:
                        pe.drain().then_inc(sums_ended.sem, 1)
                for q in (w_scaled, slot_free, out_free, vz_done, staged, *stacked):
                    q.settle(pe)
            turns(pe, body)

        @block.vector
        def _(dve):
            dve.wait_ge(w_loaded, LOADS * 16)
            nc.vector.tensor_scalar(w_f[:, :, :], w_f[:, :, :], 0.5, None, ALU.mult).then_inc(w_scaled.sem, 1)
            nc.vector.tensor_scalar(b_g[:, :], b_g[:, :], 0.5, None, ALU.mult)
            nc.vector.memset(aff[0:D, 0:1], 1.0)
            nc.vector.memset(aff[0:D, 1:2], 0.0).then_inc(b_scaled.sem, 1)

            def body(b, b_next, events):
                for n, e in enumerate(events):
                    if e.kind == "score":
                        dve.wait_ge(score_done.sem, score_done.take())
                        nc.vector.tensor_reduce(nmax[:, e.head:e.head + 1], ring[e.slot][:, :], axis=AX.X,
                                                op=ALU.max, negate=True).then_inc(max_done.sem, 1)
                    elif e.kind == "values":
                        if b_next is None and e.n == GROUPS * TILES - 1 and n > len(events) // 2:
                            dve.wait_ge(exps_ended.sem, exps_ended.take())
                        nc.vector.reciprocal(rz[:, e.n % EG, :], zsum[:, e.n % EG, :]).then_inc(rz_done.sem, 1)
                    elif e.kind == "out":
                        if e is events[-3] and b_next is None:
                            dve.wait_ge(sums_ended.sem, sums_ended.take())
                        nc.vector.scalar_tensor_tensor(gated[e.n][:, :], gate[e.n][:, :], 1.0, outT[:, :],
                                                       ALU.add, ALU.mult).then_inc(out_free.sem, 1)
                for q in (score_done, exps_ended, sums_ended):
                    q.settle(dve)
            turns(dve, body)

        @block.scalar
        def _(act):
            e_free.open(act)
            act.wait_ge(w_loaded, LOADS * 16)
            act.wait_ge(b_scaled.sem, b_scaled.take())

            def body(b, b_next, events):
                for e in events:
                    if e.kind not in IN_RING:
                        continue
                    tile = ring[e.slot]
                    if e.kind == "score":
                        act.wait_ge(max_done.sem, max_done.take())
                        k = e.tile % EG
                        if e.head == 0:
                            act.wait_ge(e_free.sem, e_free.take())
                        nc.scalar.activation(e_sb[:, k, e.head, :], tile[:, :], ACT.Exp,
                                             bias=nmax[:, e.head:e.head + 1], scale=1.0,
                                             accum_out=zsum[:, k, e.head:e.head + 1]).then_inc(slot_free.sem, 1)
                        if e.n == UNITS - 1 and b_next is None:
                            act.drain().then_inc(exps_ended.sem, 1)
                        continue
                    act.wait_ge(item_done.sem, item_done.take())
                    if e.kind == "xT":
                        nc.scalar.activation(xT[:, e.n * HALF:(e.n + 1) * HALF], tile[:, 0:HALF], ACT.Identity,
                                             bias=aff[:, 1:2], scale=aff[:, 0:1]).then_inc(slot_free.sem, 1)
                    elif e.kind in ("q", "k"):
                        i = 0 if e.kind == "q" else 1
                        nc.scalar.activation(split_in[i][:, :], tile[:, :], ACT.Copy,
                                             scale=(SCALE0, 1.0)[i]).then_inc(slot_free.sem, 1)
                        act.drain().then_inc(copied.sem, 1)
                    elif e.kind == "v":
                        nc.scalar.activation(v_sb[e.n][:, :, :].rearrange("p t d -> p (t d)"), tile[:, :],
                                             ACT.Copy).then_inc(slot_free.sem, 1)
                    elif e.kind == "gate":
                        nc.scalar.activation(gate[e.n][:, :], tile[:, :], ACT.Tanh, bias=b_g[:, e.n:e.n + 1],
                                             scale=0.5).then_inc(slot_free.sem, 1)
                    elif e.kind == "proj":
                        nc.scalar.activation(split_in[1][:, 0:TILES * D], tile[:, 0:HALF],
                                             ACT.Copy).then_inc(slot_free.sem, 1)
                        act.drain().then_inc(projected.sem, 1)
                for q in (b_scaled, max_done, e_free, item_done):
                    q.settle(act)
            turns(act, body)

        @block.gpsimd
        def _(pool):
            pool.wait_ge(w_loaded, LOADS * 16)

            def body(b, b_next, events):
                for e in events:
                    if e.kind == "values":
                        pool.wait_ge(rz_done.sem, rz_done.take())
                        k = e.n % EG
                        v = v_sb[e.n // TILES][:, e.n % TILES, :].rearrange("p (h d) -> p h d", h=HG)
                        nc.gpsimd.tensor_tensor(vz[:, k, :].rearrange("p (h d) -> p h d", h=HG), v,
                                                wide(rz[:, k, :], DH), ALU.mult).then_inc(vz_done.sem, 1)
                    elif e.kind in ("split_q", "split_k"):
                        i = 0 if e.kind == "split_q" else 1
                        pool.wait_ge(copied.sem, copied.take())
                        nc.gpsimd.tensor_copy(hi[i][:, :], split_in[i][:, :]).then_inc(pool_done.sem, 1)
                        pool.wait_ge(pool_done.sem, pool_done.take())
                        nc.gpsimd.tensor_tensor(lo[i][:, :], split_in[i][:, :], hi[i][:, :],
                                                ALU.subtract).then_inc(split_done.sem, 1)
                    elif e.kind == "stage":
                        y = yn[:, :, 0:D]
                        for src, stat, op in ((batch(h_sb, b_next), mean, ALU.subtract), (y, r1, ALU.mult)):
                            nc.gpsimd.tensor_tensor(y, src, wide(batch(stat, b_next), D), op).then_inc(pool_done.sem, 1)
                            pool.wait_ge(pool_done.sem, pool_done.take())
                        nc.gpsimd.tensor_tensor(yn[:, :, D:2 * D], y, wide(batch(r2, b_next), D), ALU.mult)
                    elif e.kind == "base":
                        h = batch(h_sb, b_next)
                        nc.gpsimd.tensor_tensor(h, h, shared(b_f[:, :], TILES), ALU.add).then_inc(pool_done.sem, 1)
                        pool.wait_ge(pool_done.sem, pool_done.take())
                        nc.gpsimd.tensor_tensor(h, h, yn[:, :, 0:D], ALU.add).then_inc(staged.sem, 1)
                    elif e.kind == "add":
                        h = batch(h_sb, NB - 1 if e.n == 0 else b - 1)
                        pool.wait_ge(projected.sem, projected.take())
                        nc.gpsimd.tensor_tensor(h, h, pr, ALU.add).then_inc(pool_done.sem, 1)
                        pool.wait_ge(pool_done.sem, pool_done.take())
                for q in (rz_done, copied, projected, pool_done):
                    q.settle(pool)
            turns(pool, body)


EXPERTS, HID0 = 8, 256
HC = HID0 // P
HT = EXPERTS * HC
WS = 64.0


def emit_moe0(nc, h_sb, stats, ident, wr, br, lng, lnb, w1, b1, w2, b2):
    mean, r1, r2, s2 = (stats[:, i, :] for i in (0, 2, 3, 4))
    with ExitStack() as ctx:
        sb = lambda name, shape, dt=F32: ctx.enter_context(nc.sbuf_tensor(name, shape, dt))
        w1f = sb("w1f", [P, EXPERTS, HID0])
        w1h = sb("w1h", [P, HT, P], F16)
        w1l = sb("w1l", [P, HT, P], F16)
        lng_sb = sb("lng", [P, EXPERTS])
        lnb_sb = sb("lnb", [P, EXPERTS])
        wrf = sb("wrf", [P, EXPERTS])
        wrh = sb("wrh", [P, EXPERTS], F16)
        wrl = sb("wrl", [P, EXPERTS], F16)
        br_sb = sb("br", [P, EXPERTS])
        b1_sb = sb("b1", [P, HT])
        w2_sb = sb("w2", [P, HT, D])
        b2_sb = sb("b2", [P, EXPERTS, D])
        iota_i = sb("iota_i", [P, EXPERTS], I32)
        iota = sb("iota", [P, EXPERTS])
        euler = sb("euler", [P, TILES])
        xn = sb("xn", [P, TILES, 2 * D])
        xs = sb("xs", [P, T], F16)
        hid = [sb(f"hid{i}", [P, T]) for i in range(2)]
        logits = sb("logits", [P, TILES, EXPERTS])
        top = sb("top", [P, TILES, 8])
        top_i = sb("top_i", [P, TILES, 8], U32)
        top_f = sb("top_f", [P, 2, TILES])
        gap = sb("gap", [P, TILES])
        e2 = sb("e2", [P, TILES])
        tw = sb("tw", [P, 2, TILES])
        den = sb("den", [P, TILES])
        pick = sb("pick", [P, 2, TILES, EXPERTS])
        wt = sb("wt", [P, TILES, EXPERTS])
        biased = [sb(f"biased{i}", [P, TILES, D]) for i in range(2)]
        term = [sb(f"term{i}", [P, TILES, D]) for i in range(2)]
        hps = [ctx.enter_context(nc.psum_tensor(f"hps{i}", [P, T], F32)) for i in range(2)]
        yps = [ctx.enter_context(nc.psum_tensor(f"yps{i}", [P, HALF], F32)) for i in range(2)]
        xps = ctx.enter_context(nc.psum_tensor("xps", [P, T], F32))

        s = lambda name, credits=0: Signal(ctx, nc, name, credits)
        LOADS = 12
        loaded = ctx.enter_context(nc.semaphore("loaded"))
        consts = s("consts")
        folded_v = s("folded_v")
        w_ready = s("w_ready")
        b1_ready = s("b1_ready")
        xn_ready = s("xn_ready")
        x_done = s("x_done")
        xs_free = s("xs_free")
        xs_ready = s("xs_ready")
        r_done = s("r_done")
        r_read = s("r_read")
        h_done = s("h_done")
        gelu_done = s("gelu_done")
        y_done = s("y_done")
        y_free = s("y_free", 2)
        gap_ready = s("gap_ready")
        e2_ready = s("e2_ready")
        term_done = s("term_done")
        term_free = s("term_free", 2)
        chain = s("dve_chain")
        pool_done = s("pool_done0")
        block = ctx.enter_context(nc.Block())

        def turns(eng, body):
            with eng.Fori(0, NB - 1) as b:
                body(b, True)
            body(NB - 1, False)

        @block.sync
        def _(sp):
            for half in (slice(0, D), slice(D, P)):
                for dst, src in ((w1f[half, :, :], w1.rearrange("e d h -> d e h")), (lng_sb[half, :], lng),
                                 (lnb_sb[half, :], lnb), (wrf[half, :], wr)):
                    sp.dma_start(dst, src).then_inc(loaded, 16)
            for dst, src in ((br_sb[:, :], br.partition_broadcast(P)), (b1_sb[:, :], b1),
                             (w2_sb[:, :, :], w2.rearrange("e (c p) d -> p (e c) d", p=P)),
                             (b2_sb[:, :, :].rearrange("p e d -> p (e d)"), b2.partition_broadcast(P))):
                sp.dma_start(dst, src).then_inc(loaded, 16)

        @block.tensor
        def _(pe):
            y_free.open(pe)
            pe.wait_ge(loaded, LOADS * 16)

            def transpose():
                pe.wait_ge(xn_ready.sem, xn_ready.take())
                for t in range(TILES):
                    last = nc.tensor.transpose(xps[:, t * P:(t + 1) * P], xn[:, t, :], ident[:, :])
                last.then_inc(x_done.sem, 1)

            def layer1(ht):
                for j in range(2):
                    cols = slice(j * HALF, (j + 1) * HALF)
                    nc.tensor.matmul(hps[ht % 2][:, cols], w1h[:, ht, :], xs[:, cols], start=True, stop=False)
                    last = nc.tensor.matmul(hps[ht % 2][:, cols], w1l[0:D, ht, :], xs[0:D, cols],
                                            start=False, stop=True)
                last.then_inc(h_done.sem, 1)

            def layer2(ht):
                expert, chunk = divmod(ht, HC)
                pe.wait_ge(gelu_done.sem, gelu_done.take())
                if chunk == 0:
                    pe.wait_ge(y_free.sem, y_free.take())
                for t in range(TILES):
                    last = nc.tensor.matmul(yps[expert % 2][:, t * D:(t + 1) * D], hid[ht % 2][:, t * P:(t + 1) * P],
                                            w2_sb[:, ht, :], start=(chunk == 0 and t == 0), stop=(chunk == HC - 1),
                                            skip_group_check=True)
                    if ht == HT - 2 and t == 0:
                        last.then_inc(xs_free.sem, 1)
                if chunk == HC - 1:
                    last.then_inc(y_done.sem, 1)

            for ht in range(HT):
                expert, chunk = divmod(ht, HC)
                last = nc.tensor.matmul(hps[0][:, ht:ht + 1], w1f[0:D, expert, chunk * P:(chunk + 1) * P],
                                        lnb_sb[0:D, expert:expert + 1], start=True, stop=True)
            last.then_inc(folded_v.sem, 1)
            pe.wait_ge(w_ready.sem, w_ready.take())
            transpose()

            def body(b, has_next):
                pe.wait_ge(xs_ready.sem, xs_ready.take())
                for t in range(TILES):
                    out = xps[:, t * EXPERTS:(t + 1) * EXPERTS]
                    nc.tensor.matmul(out, xs[:, t * P:(t + 1) * P], wrh[:, :], start=True, stop=False)
                    last = nc.tensor.matmul(out, xs[0:D, t * P:(t + 1) * P], wrl[0:D, :], start=False, stop=True)
                last.then_inc(r_done.sem, 1)
                for ht in range(HT):
                    layer1(ht)
                    if ht:
                        layer2(ht - 1)
                    if ht == 12:
                        pe.wait_ge(r_read.sem, r_read.take())
                        if has_next:
                            transpose()
                layer2(HT - 1)
                for q in (xn_ready, w_ready, gelu_done, y_free, xs_ready, r_read):
                    q.settle(pe)
            for q in (xn_ready, w_ready):
                q.settle(pe)
            turns(pe, body)

        @block.scalar
        def _(act):
            act.wait_ge(b1_ready.sem, b1_ready.take())

            def body(b, has_next):
                for ht in range(HT):
                    act.wait_ge(h_done.sem, h_done.take())
                    nc.scalar.activation(hid[ht % 2][:, :], hps[ht % 2][:, :], ACT.Gelu, bias=b1_sb[:, ht:ht + 1],
                                         scale=1.0 / WS).then_inc(gelu_done.sem, 1)
                h_done.settle(act)
            turns(act, body)

        @block.gpsimd
        def _(pool):
            pool.memset(euler[:, :], float(np.e))
            pool.iota(iota_i[:, :], pattern=[[1, EXPERTS]], base=0, channel_multiplier=0).then_inc(consts.sem, 1)

            def stage(b):
                x = xn[:, :, 0:D]
                for src, stat, op in ((batch(h_sb, b), mean, ALU.subtract), (x, r1, ALU.mult), (x, r2, ALU.mult)):
                    nc.gpsimd.tensor_tensor(x, src, wide(batch(stat, b), D), op).then_inc(pool_done.sem, 1)
                    pool.wait_ge(pool_done.sem, pool_done.take())
                nc.gpsimd.tensor_copy(xn[:, :, D:2 * D], x).then_inc(xn_ready.sem, 1)

            stage(0)
            pool_done.settle(pool)

            def body(b, has_next):
                pool.wait_ge(gap_ready.sem, gap_ready.take())
                nc.gpsimd.tensor_tensor(e2[:, :], euler[:, :], gap[:, :], ALU.pow).then_inc(e2_ready.sem, 1)
                for e in range(EXPERTS):
                    pool.wait_ge(term_done.sem, term_done.take())
                    nc.gpsimd.tensor_tensor(batch(h_sb, b), batch(h_sb, b), term[e % 2][:, :, :],
                                            ALU.add).then_inc(pool_done.sem, 1)
                    pool.wait_ge(pool_done.sem, pool_done.take())
                    pool.sem_inc(term_free.sem, 1)
                    if e == 2 and has_next:
                        stage(b + 1)
                for q in (gap_ready, term_done, pool_done):
                    q.settle(pool)
            turns(pool, body)

        @block.vector
        def _(dve):
            term_free.open(dve)

            def link(ins):
                ins.then_inc(chain.sem, 1)
                dve.wait_ge(chain.sem, chain.take())

            def split_tokens():
                dve.wait_ge(x_done.sem, x_done.take())
                link(nc.vector.tensor_copy(xs[:, :], xps[:, :]))
                nc.vector.tensor_tensor(xs[D:P, :], xps[D:P, :], xs[D:P, :], ALU.subtract).then_inc(xs_ready.sem, 1)

            dve.wait_ge(loaded, LOADS * 16)
            dve.wait_ge(consts.sem, consts.take())
            link(nc.vector.tensor_copy(iota[:, :], iota_i[:, :]))
            dve.wait_ge(folded_v.sem, folded_v.take())
            nc.vector.tensor_tensor(b1_sb[:, :], b1_sb[:, :], hps[0][:, 0:HT], ALU.add).then_inc(b1_ready.sem, 1)
            for e in range(EXPERTS):
                last = nc.vector.tensor_scalar(w1f[:, e, :], w1f[:, e, :], lng_sb[:, e:e + 1], WS, ALU.mult, ALU.mult)
            link(last)
            link(nc.vector.tensor_scalar(wrf[:, :], wrf[:, :], WS, None, ALU.mult))
            w1_flat = w1f[:, :, :].rearrange("p e h -> p (e h)")
            flat = lambda w: w[:, :, :].rearrange("p t h -> p (t h)")
            link(nc.vector.tensor_copy(flat(w1h), w1_flat))
            nc.vector.tensor_tensor(flat(w1l), w1_flat, flat(w1h), ALU.subtract)
            link(nc.vector.tensor_copy(wrh[:, :], wrf[:, :]))
            nc.vector.tensor_tensor(wrl[:, :], wrf[:, :], wrh[:, :], ALU.subtract).then_inc(w_ready.sem, 1)
            split_tokens()
            for q in (consts, folded_v, chain, x_done):
                q.settle(dve)

            def body(b, has_next):
                dve.wait_ge(r_done.sem, r_done.take())
                nc.vector.tensor_tensor(logits[:, :, :],
                                        xps[:, 0:TILES * EXPERTS].rearrange("p (t e) -> p t e", e=EXPERTS),
                                        wide(batch(s2, b), EXPERTS), ALU.mult).then_inc(r_read.sem, 1)
                dve.drain()
                link(nc.vector.scalar_tensor_tensor(logits[:, :, :], logits[:, :, :], 1.0 / WS,
                                                    shared(br_sb[:, :], TILES), ALU.mult, ALU.add))
                for t in range(TILES):
                    last = nc.vector.max(top[:, t, :], logits[:, t, :])
                link(last)
                nc.vector.tensor_tensor(gap[:, :], top[:, :, 1], top[:, :, 0], ALU.subtract).then_inc(gap_ready.sem, 1)
                for t in range(TILES):
                    last = nc.vector.max_index(top_i[:, t, :], top[:, t, :], logits[:, t, :])
                link(last)
                link(nc.vector.tensor_copy(top_f[:, :, :], top_i[:, :, 0:2].rearrange("p t k -> p k t")))
                for k in range(2):
                    last = nc.vector.tensor_tensor(pick[:, k], shared(iota[:, :], TILES), wide(top_f[:, k, :], EXPERTS),
                                                   ALU.is_equal)
                link(last)
                dve.wait_ge(e2_ready.sem, e2_ready.take())
                link(nc.vector.tensor_scalar(den[:, :], e2[:, :], 1.0, None, ALU.add))
                link(nc.vector.reciprocal(tw[:, 0, :], den[:, :]))
                link(nc.vector.tensor_tensor(tw[:, 1, :], e2[:, :], tw[:, 0, :], ALU.mult))
                for k in range(2):
                    last = nc.vector.tensor_tensor(pick[:, k], pick[:, k], wide(tw[:, k, :], EXPERTS), ALU.mult)
                link(last)
                link(nc.vector.tensor_tensor(wt[:, :, :], pick[:, 0], pick[:, 1], ALU.add))
                for e in range(EXPERTS):
                    if e == EXPERTS - 1 and has_next:
                        dve.wait_ge(xs_free.sem, xs_free.take())
                        split_tokens()
                    dve.wait_ge(y_done.sem, y_done.take())
                    link(nc.vector.tensor_tensor(biased[e % 2][:, :, :],
                                                 yps[e % 2][:, :].rearrange("p (t d) -> p t d", d=D),
                                                 shared(b2_sb[:, e, :], TILES), ALU.add))
                    dve.sem_inc(y_free.sem, 1)
                    dve.wait_ge(term_free.sem, term_free.take())
                    nc.vector.tensor_tensor(term[e % 2][:, :, :], biased[e % 2][:, :, :], wide(wt[:, :, e], D),
                                            ALU.mult).then_inc(term_done.sem, 1)
                if not has_next:
                    dve.wait_ge(xs_free.sem, xs_free.take())
                for q in (r_done, e2_ready, xs_free, x_done, y_done, term_free, chain):
                    q.settle(dve)
            turns(dve, body)


S1 = 128


def emit_attention1(nc, h_sb, stats, ident, wuv, buv, gam, bet, wo, bo):
    mean, r1, r2 = (stats[:, i, :] for i in (0, 2, 3))
    with ExitStack() as ctx:
        sb = lambda name, shape, dt=F32: ctx.enter_context(nc.sbuf_tensor(name, shape, dt))
        w_sb = sb("wuv", [D + 1, 3 * S1])
        gb = sb("gb", [P, 4])
        wo_sb = sb("wo", [P, D])
        bo_sb = sb("bo", [P, D])
        xn = sb("xn1", [P, TILES, D])
        xT = sb("xT1", [D + 1, T])
        base = sb("base", [P, T])
        q_sb, k_sb, u_sb, v_sb = ([sb(f"{n}1_{i}", [P, T]) for i in range(2)] for n in "qkuv")
        a_sb = [sb(f"a1_{i}", [P, T]) for i in range(2)]
        gated = sb("a1_gated", [P, T])
        proj = sb("a1_proj", [P, TILES, D])
        sps = [ctx.enter_context(nc.psum_tensor(f"sps{i}", [P, T], F32)) for i in range(2)]
        ops_ = ctx.enter_context(nc.psum_tensor("ops", [P, T], F32))
        pps = ctx.enter_context(nc.psum_tensor("pps", [P, T], F32))

        s = lambda name, credits=0: Signal(ctx, nc, name, credits)
        LOADS = 6
        loaded = ctx.enter_context(nc.semaphore("loaded1"))
        scaled = s("scaled1")
        xn_ready = s("xn_ready1")
        xn_free = s("xn_free1", 1)
        p_done = s("p_done1")
        proj_done = s("proj_done1")
        p_free = s("p_free1", 1)
        base_done = s("base_done1")
        qk_ready = s("qk_ready1")
        s_done = s("s_done1")
        relu_done = s("relu_done1")
        a_ready = s("a_ready1")
        o_done = s("o_done1")
        gated_done = s("gated_done1", 1)
        chain = s("dve_chain1")
        pool_done = s("pool_done1")
        block = ctx.enter_context(nc.Block())

        def turns(eng, body):
            body(None, 1, False, True)
            body(0, 0, False, True)
            with eng.Fori(0, (NB - 2) // 2) as i:
                body(i * 2 + 1, 1, True, True, settle=False)
                body(i * 2 + 2, 0, True, True)
            body(NB - 1, 1, True, False)

        @block.sync
        def _(sp):
            for dst, src in ((w_sb[0:D, :], wuv), (w_sb[D:D + 1, :], buv.unsqueeze(0)), (gb[:, 0:2], gam),
                             (gb[:, 2:4], bet), (wo_sb[:, :], wo), (bo_sb[:, :], bo.partition_broadcast(P))):
                sp.dma_start(dst, src).then_inc(loaded, 16)

        @block.gpsimd
        def _(pool):
            xn_free.open(pool)

            def body(b, par, has_prev, has_next, settle=True):
                if has_next:
                    nxt = 0 if b is None else b + 1
                    pool.wait_ge(xn_free.sem, xn_free.take())
                    x = xn[:, :, :]
                    for n, (src, stat, op) in enumerate(((batch(h_sb, nxt), mean, ALU.subtract), (x, r1, ALU.mult),
                                                         (x, r2, ALU.mult))):
                        ins = nc.gpsimd.tensor_tensor(x, src, wide(batch(stat, nxt), D), op)
                        if n < 2:
                            ins.then_inc(pool_done.sem, 1)
                            pool.wait_ge(pool_done.sem, pool_done.take())
                    ins.then_inc(xn_ready.sem, 1)
                if settle:
                    for q in (xn_free, pool_done):
                        q.settle(pool)
            turns(pool, body)

        @block.tensor
        def _(pe):
            p_free.open(pe)
            gated_done.open(pe)
            pe.wait_ge(loaded, LOADS * 16)
            pe.wait_ge(scaled.sem, scaled.take())

            def scores(par, m):
                if m == 0:
                    pe.wait_ge(qk_ready.sem, qk_ready.take())
                for j in range(2):
                    cols = slice(j * HALF, (j + 1) * HALF)
                    last = nc.tensor.matmul(sps[m % 2][:, cols], k_sb[par][:, m * P:(m + 1) * P], q_sb[par][:, cols],
                                            start=True, stop=True)
                last.then_inc(s_done.sem, 1)

            def attend(par, m):
                pe.wait_ge(a_ready.sem, a_ready.take())
                if m == 0:
                    pe.wait_ge(gated_done.sem, gated_done.take())
                    pe.wait_ge(p_free.sem, p_free.taken + 1)
                for j in range(2):
                    cols = slice(j * HALF, (j + 1) * HALF)
                    last = nc.tensor.matmul(ops_[:, cols], v_sb[par][:, m * P:(m + 1) * P], a_sb[m % 2][:, cols],
                                            start=(m == 0), stop=(m == TILES - 1), skip_group_check=True)
                if m == TILES - 1:
                    last.then_inc(o_done.sem, 1)

            def operand(kind):
                if kind == "xT":
                    pe.wait_ge(xn_ready.sem, xn_ready.take())
                pe.wait_ge(p_free.sem, p_free.take())
                if kind == "xT":
                    for t in range(TILES):
                        last = nc.tensor.transpose(pps[0:D, t * P:(t + 1) * P], xn[:, t, :], ident[:, :])
                elif kind == "v":
                    for t in range(TILES):
                        last = nc.tensor.matmul(pps[:, t * P:(t + 1) * P], xT[:, t * P:(t + 1) * P],
                                                w_sb[:, S1:2 * S1], start=True, stop=True)
                else:
                    col = 0 if kind == "u" else 2 * S1
                    for j in range(2):
                        last = nc.tensor.matmul(pps[:, j * HALF:(j + 1) * HALF], w_sb[:, col:col + S1],
                                                xT[:, j * HALF:(j + 1) * HALF], start=True, stop=True)
                        if kind == "base" and j == 0:
                            last.then_inc(xn_free.sem, 1)
                last.then_inc(p_done.sem, 1)

            def project():
                pe.wait_ge(p_free.sem, p_free.take())
                for t in range(TILES):
                    last = nc.tensor.matmul(pps[:, t * D:(t + 1) * D], gated[:, t * P:(t + 1) * P], wo_sb[:, :],
                                            start=True, stop=True)
                last.then_inc(proj_done.sem, 1)

            def body(b, par, has_prev, has_next, settle=True):
                for m in range(TILES):
                    if b is not None:
                        scores(par, m)
                        if m:
                            attend(par, m - 1)
                        elif has_prev:
                            attend(1 - par, TILES - 1)
                    if has_next and 1 <= m <= 4:
                        operand(("xT", "base", "u", "v")[m - 1])
                    if m == 5 and has_prev:
                        project()
                if b is not None and not has_next:
                    attend(par, TILES - 1)
                    pe.wait_ge(gated_done.sem, gated_done.take())
                    project()
                if settle:
                    for q in (scaled, qk_ready, a_ready, gated_done, p_free, xn_ready):
                        q.settle(pe)

            turns(pe, body)

        @block.vector
        def _(dve):
            dve.wait_ge(loaded, LOADS * 16)
            nc.vector.tensor_scalar(gb[:, 0:4:2], gb[:, 0:4:2], S1 ** -0.5, None, ALU.mult)
            nc.vector.memset(xT[D:D + 1, :], 1.0).then_inc(scaled.sem, 1)

            def link(ins):
                ins.then_inc(chain.sem, 1)
                dve.wait_ge(chain.sem, chain.take())

            def gate_output(par):
                dve.wait_ge(o_done.sem, o_done.take())
                nc.vector.tensor_tensor(gated[:, :], ops_[:, :], u_sb[par][:, :], ALU.mult).then_inc(gated_done.sem, 1)

            def add_projection(b):
                dve.wait_ge(proj_done.sem, proj_done.take())
                link(nc.vector.tensor_tensor(proj[:, :, :], pps[:, 0:HALF].rearrange("p (t d) -> p t d", d=D),
                                             shared(bo_sb[:, :], TILES), ALU.add))
                nc.vector.tensor_tensor(batch(h_sb, b), batch(h_sb, b), proj[:, :, :], ALU.add).then_inc(p_free.sem, 1)

            def body(b, par, has_prev, has_next, settle=True):
                for m in range(TILES):
                    if b is not None:
                        dve.wait_ge(s_done.sem, s_done.take())
                        nc.vector.tensor_scalar(a_sb[m % 2][:, :], sps[m % 2][:, :], 0.0, None,
                                                ALU.max).then_inc(relu_done.sem, 1)
                    if m == 0 and has_prev:
                        gate_output(1 - par)
                    if m == 4 and has_next:
                        dve.wait_ge(base_done.sem, base_done.take())
                        nc.vector.tensor_scalar(q_sb[1 - par][:, :], base[:, :], gb[:, 0:1], gb[:, 2:3],
                                                ALU.mult, ALU.add)
                        nc.vector.tensor_scalar(k_sb[1 - par][:, :], base[:, :], gb[:, 1:2], gb[:, 3:4],
                                                ALU.mult, ALU.add).then_inc(qk_ready.sem, 1)
                    if m == 6 and has_prev:
                        add_projection(b - 1)
                if b is not None and not has_next:
                    gate_output(par)
                    add_projection(b)
                if settle:
                    for q in (chain, o_done, proj_done, s_done, base_done):
                        q.settle(dve)
            turns(dve, body)

        @block.scalar
        def _(act):
            act.wait_ge(loaded, LOADS * 16)

            def body(b, par, has_prev, has_next, settle=True):
                for m in range(TILES):
                    if has_next and 1 <= m <= 4:
                        act.wait_ge(p_done.sem, p_done.take())
                        if m == 1:
                            nc.scalar.activation(xT[0:D, :], pps[0:D, :], ACT.Copy).then_inc(p_free.sem, 1)
                        elif m == 2:
                            nc.scalar.activation(base[:, :], pps[:, :], ACT.Silu).then_inc(p_free.sem, 1)
                            act.drain().then_inc(base_done.sem, 1)
                        else:
                            nc.scalar.activation((u_sb if m == 3 else v_sb)[1 - par][:, :], pps[:, :],
                                                 ACT.Silu).then_inc(p_free.sem, 1)
                    if b is not None:
                        act.wait_ge(relu_done.sem, relu_done.take())
                        nc.scalar.activation(a_sb[m % 2][:, :], a_sb[m % 2][:, :],
                                             ACT.Square).then_inc(a_ready.sem, 1)
                if settle:
                    for q in (p_done, relu_done):
                        q.settle(act)
            turns(act, body)


HID1 = 128
ROW_W2, ROW_B2, ROW_B1 = HID1, HID1 + D, HID1 + 2 * D
ROW = HID1 + 2 * D + 1
CAPACITY = float(-(-NB * T * 5 // (4 * EXPERTS)))


def emit_routing(nc, h_sb, stats, ident, y_all, wr, br, route_i, route_w):
    mean, r1 = stats[:, 0, :], stats[:, 2, :]
    CH = 4
    n, nb = NT // CH, NB // CH
    with ExitStack() as ctx:
        sb = lambda name, shape, dt=F32: ctx.enter_context(nc.sbuf_tensor(name, shape, dt))
        ysum = sb("ysum", [P, NB, D])
        token_share = sb("token_share", [P, 1])
        ones = sb("ones", [NB, P])
        row_i = sb("row_i", [P, 1], I32)
        row_f = sb("row_f", [P, 1])
        wr_sb = sb("r_wr", [D, EXPERTS])
        br_sb = sb("r_br", [NB, EXPERTS])
        tokens_mean = sb("tokens_mean", [D, NB])
        logits, exps, probs, scale = (sb(f"r_{x}", [NB, EXPERTS]) for x in ("logits", "exps", "probs", "scale"))
        top = sb("r_top", [NB, 8])
        top_i = sb("r_top_i", [NB, 8], U32)
        nmax, total, gap, e2, den = (sb(f"r_{x}", [NB, 1]) for x in ("nmax", "total", "gap", "e2", "den"))
        four = sb("r_four", [NB, 4])
        four_diag = sb("r_four_diag", [NB, 4, NB])
        rows = sb("r_rows", [P, NB, 2])
        ps = [ctx.enter_context(nc.psum_tensor(f"r_ps{i}", [P, HALF], F32)) for i in range(4)]
        sem = lambda name: ctx.enter_context(nc.semaphore("r_" + name))
        loaded, consts, centred, scaled, summed, means_done, means_ready, logits_done, shifted, exped, \
            probs_ready, loads_done, gap_ready, e2_ready, four_ready, four_done, chain = (
                sem(x) for x in ("loaded", "consts", "centred", "scaled", "summed", "means_done", "means_ready",
                                 "logits_done", "shifted", "exped", "probs_ready", "loads_done", "gap_ready",
                                 "e2_ready", "four_ready", "four_done", "chain"))
        block = ctx.enter_context(nc.Block())
        part = lambda t, c: t[:, c * n:(c + 1) * n]

        @block.sync
        def _(sp):
            sp.dma_start(wr_sb[:, :], wr).then_inc(loaded, 16)
            sp.dma_start(br_sb[:, :], br.partition_broadcast(NB)).then_inc(loaded, 16)

        @block.gpsimd
        def _(pool):
            pool.memset(token_share[:, :], 1.0 / T)
            pool.memset(ones[:, :], 1.0)
            pool.iota(row_i[:, :], pattern=[[0, 1]], base=0, channel_multiplier=1).then_inc(consts, 1)
            for c in range(CH):
                pool.wait_ge(centred, c + 1)
                nc.gpsimd.tensor_tensor(part(y_all, c), part(y_all, c), wide(part(r1, c), D), ALU.mult).then_inc(scaled, 1)

        @block.tensor
        def _(pe):
            pe.wait_ge(consts, 1)
            pe.wait_ge(loaded, 32)
            for b in range(NB):
                if b % nb == 0:
                    pe.wait_ge(summed, b // nb + 1)
                last = nc.tensor.matmul(ps[0][0:D, b:b + 1], ysum[:, b, :], token_share[:, :], start=True, stop=True)
            last.then_inc(means_done, 1)
            pe.wait_ge(means_ready, 1)
            nc.tensor.matmul(ps[1][0:NB, 0:EXPERTS], tokens_mean[:, :], wr_sb[:, :], start=True,
                             stop=True).then_inc(logits_done, 1)
            pe.wait_ge(probs_ready, 1)
            nc.tensor.matmul(ps[2][0:NB, 0:EXPERTS], ones[:, 0:NB], probs[:, :], start=True,
                             stop=True).then_inc(loads_done, 1)
            pe.wait_ge(four_ready, 1)
            nc.tensor.matmul(ps[3][:, 0:4 * NB], ones[:, :], four_diag[:, :, :].rearrange("p k b -> p (k b)"),
                             start=True, stop=True).then_inc(four_done, 1)

        @block.scalar
        def _(act):
            for i in range(2):
                act.wait_ge(shifted, i + 1)
                nc.scalar.activation(exps[:, :], logits[:, :], ACT.Exp, bias=nmax[:, :], scale=1.0,
                                     accum_out=total[:, :])
                act.drain().then_inc(exped, 1)
            act.wait_ge(gap_ready, 1)
            nc.scalar.activation(e2[:, :], gap[:, :], ACT.Exp).then_inc(e2_ready, 1)

        @block.vector
        def _(dve):
            links = [0]

            def link(ins):
                links[0] += 1
                ins.then_inc(chain, 1)
                dve.wait_ge(chain, links[0])

            def softmax(i):
                nc.vector.tensor_reduce(nmax[:, :], logits[:, :], axis=AX.X, op=ALU.max, negate=True).then_inc(shifted, 1)
                dve.wait_ge(exped, i + 1)
                link(nc.vector.reciprocal(den[:, :], total[:, :]))
                return nc.vector.tensor_scalar(probs[:, :], exps[:, :], den[:, :], None, ALU.mult)

            def centre(c):
                nc.vector.tensor_tensor(part(y_all, c), part(h_sb, c), wide(part(mean, c), D),
                                        ALU.subtract).then_inc(centred, 1)

            centre(0)
            for c in range(CH):
                if c + 1 < CH:
                    centre(c + 1)
                dve.wait_ge(scaled, c + 1)
                nc.vector.reduce_sum(ysum[:, c * nb:(c + 1) * nb, :],
                                     part(y_all, c).rearrange("p (b t) d -> p b d t", t=TILES), AX.X).then_inc(summed, 1)
            dve.wait_ge(consts, 1)
            dve.wait_ge(loaded, 32)
            nc.vector.tensor_copy(row_f[:, :], row_i[:, :])
            dve.wait_ge(means_done, 1)
            nc.vector.tensor_copy(tokens_mean[:, :], ps[0][0:D, 0:NB]).then_inc(means_ready, 1)
            dve.wait_ge(logits_done, 1)
            link(nc.vector.tensor_tensor(logits[:, :], ps[1][0:NB, 0:EXPERTS], br_sb[:, :], ALU.add))
            softmax(0).then_inc(probs_ready, 1)
            dve.wait_ge(loads_done, 1)
            link(nc.vector.tensor_scalar(scale[:, :], ps[2][0:NB, 0:EXPERTS], float(T), CAPACITY, ALU.mult, ALU.max))
            link(nc.vector.reciprocal(scale[:, :], scale[:, :]))
            link(nc.vector.scalar_tensor_tensor(logits[:, :], scale[:, :], CAPACITY, probs[:, :], ALU.mult, ALU.mult))
            link(softmax(1))
            link(nc.vector.max(top[:, :], probs[:, :]))
            nc.vector.tensor_tensor(gap[:, :], top[:, 1:2], top[:, 0:1], ALU.subtract).then_inc(gap_ready, 1)
            link(nc.vector.max_index(top_i[:, :], top[:, :], probs[:, :]))
            nc.vector.tensor_copy(four[:, 0:2], top_i[:, 0:2])
            dve.wait_ge(e2_ready, 1)
            link(nc.vector.tensor_scalar(den[:, :], e2[:, :], 1.0, None, ALU.add))
            link(nc.vector.reciprocal(four[:, 2:3], den[:, :]))
            link(nc.vector.tensor_tensor(four[:, 3:4], e2[:, :], four[:, 2:3], ALU.mult))
            nc.vector.tensor_tensor(four_diag[:, :, :], wide(four[:, :], NB), shared(ident[0:NB, 0:NB], 4),
                                    ALU.mult).then_inc(four_ready, 1)
            dve.wait_ge(four_done, 1)
            four_all = ps[3][:, 0:4 * NB].rearrange("p (k b) -> p k b", b=NB)
            nc.vector.tensor_copy(route_w[:, :, :], four_all[:, 2:4, :])
            link(nc.vector.tensor_scalar(rows[:, :, :], four_all[:, 0:2, :].rearrange("p k b -> p b k"), float(P),
                                         row_f[:, :], ALU.mult, ALU.add))
            nc.vector.tensor_copy(route_i[:, :, :], rows[:, :, :])


def emit_moe1(nc, h_sb, stats, ident, wr, br, table, gamma, beta, out):
    with ExitStack() as outer:
        keep = lambda name, shape, dt=F32: outer.enter_context(nc.sbuf_tensor(name, shape, dt))
        y_all = keep("y_all", [P, NT, D])
        route_i = keep("route_i", [P, NB, 2], I32)
        route_w = keep("route_w", [P, 2, NB])
        emit_routing(nc, h_sb, stats, ident, y_all, wr, br, route_i, route_w)
        emit_experts(nc, h_sb, ident, y_all, route_i, route_w, table, gamma, beta, out)


def emit_experts(nc, h_sb, ident, y_all, route_i, route_w, table, gamma, beta, out):
    with ExitStack() as ctx:
        sb = lambda name, shape, dt=F32: ctx.enter_context(nc.sbuf_tensor(name, shape, dt))
        two = lambda name, shape, dt=F32: [sb(f"{name}_{i}", shape, dt) for i in range(2)]
        gam_sb = sb("m1_gamma", [P, D])
        bet_sb = sb("m1_beta", [P, D])
        idx = two("m1_idx", [P, 2], I32)
        w_g = two("m1_w", [P, 2, ROW])
        w2s = two("m1_w2s", [P, 2, D])
        b2s = two("m1_b2s", [P, 2, D])
        y_b = two("m1_y", [P, TILES, D])
        yT = two("m1_yT", [P, HALF])
        hid = two("m1_hid", [P, 2 * HALF])
        base = two("m1_base", [P, TILES, D])
        z = two("m1_z", [P, TILES, D])
        sq = sb("m1_sq", [P, TILES, D])
        zm = sb("m1_zm", [P, TILES])
        zv = two("m1_zv", [P, TILES])
        rstd = sb("m1_rstd", [P, TILES])
        half = sb("m1_half", [P, TILES])
        yps = [ctx.enter_context(nc.psum_tensor(f"m1_yps{i}", [P, HALF], F32)) for i in range(2)]
        hps = [ctx.enter_context(nc.psum_tensor(f"m1_hps{i}", [P, 2 * HALF], F32)) for i in range(2)]
        xps = ctx.enter_context(nc.psum_tensor("m1_xps", [P, HALF], F32))

        s = lambda name, credits=0: Signal(ctx, nc, "m1_" + name, credits)
        loaded = ctx.enter_context(nc.semaphore("m1_loaded"))
        stored = ctx.enter_context(nc.semaphore("m1_stored"))
        landed = [ctx.enter_context(nc.semaphore(f"m1_landed{i}")) for i in range(2)]
        idx_copied = s("idx_copied")
        w_free = s("w_free", 2)
        y_ready = s("y_ready")
        x_done = s("x_done")
        yT_ready = s("yT_ready")
        w_ready = s("w_ready")
        b2_ready = s("b2_ready")
        base_ready = s("base_ready")
        h_done = s("h_done")
        gelu_done = s("gelu_done")
        out_done = s("out_done")
        centred = s("centred")
        squared = s("squared")
        var_ready = s("var_ready")
        rstd_ready = s("rstd_ready")
        z_ready = s("z_ready")
        h_ready = s("h_ready")
        chain = s("chain")
        pool_done = s("pool_done")
        block = ctx.enter_context(nc.Block())

        def turns(eng, body):
            body(-1, 1, 1, False, False, True)
            body(0, 0, 1, False, True, True)
            with eng.Fori(0, NB // 2 - 1) as r:
                body(r * 2 + 1, 1, r + 2, True, True, True, settle=False)
                body(r * 2 + 2, 0, r + 2, True, True, True)
            body(NB - 1, 1, None, True, True, False)
            body(NB, 0, None, True, False, False)

        @block.sync
        def _(sp):
            sp.dma_start(gam_sb[:, :], gamma.partition_broadcast(P)).then_inc(loaded, 16)
            sp.dma_start(bet_sb[:, :], beta.partition_broadcast(P)).then_inc(loaded, 16)

            def body(i, par, count, has_prev, has_this, has_next, settle=True):
                if has_prev:
                    sp.wait_ge(h_ready.sem, h_ready.take())
                    sp.dma_start(out[bass.ds(i - 1, 1)].rearrange("b (p t) d -> p (b t) d", t=TILES),
                                 batch(h_sb, i - 1)).then_inc(stored, 16)
                if settle:
                    h_ready.settle(sp)
            turns(sp, body)
            sp.wait_ge(stored, NB * 16)

        @block.gpsimd
        def _(pool):
            w_free.open(pool)
            pool.memset(half[:, :], -0.5).then_inc(pool_done.sem, 1)
            pool.wait_ge(pool_done.sem, pool_done.take())

            def step(ins):
                ins.then_inc(pool_done.sem, 1)
                pool.wait_ge(pool_done.sem, pool_done.take())

            def body(i, par, count, has_prev, has_this, has_next, settle=True):
                nxt = 1 - par
                if has_next:
                    nc.gpsimd.tensor_copy(idx[nxt][:, :], route_i[:, i + 1, :] if isinstance(i, int) else
                                          route_i[:, bass.ds(i + 1, 1), :].rearrange("p b k -> p (b k)")
                                          ).then_inc(idx_copied.sem, 1)
                    pool.wait_ge(idx_copied.sem, idx_copied.take())
                    pool.wait_ge(w_free.sem, w_free.take())
                    for k in range(2):
                        pool.indirect_dma_start(
                            out=w_g[nxt][:, k, :], out_offset=None, in_=table[:, :],
                            in_offset=bass.IndirectOffsetOnAxis(ap=idx[nxt][:, k:k + 1], axis=0),
                        ).then_inc(landed[nxt], 16)
                    nc.gpsimd.tensor_copy(y_b[nxt][:, :, :], batch(y_all, i + 1)).then_inc(y_ready.sem, 1)
                if has_prev:
                    pool.wait_ge(var_ready.sem, var_ready.take())
                    nc.gpsimd.tensor_tensor(rstd[:, :], zv[nxt][:, :], half[:, :], ALU.pow).then_inc(rstd_ready.sem, 1)
                    step(nc.gpsimd.tensor_tensor(batch(h_sb, i - 1), batch(h_sb, i - 1),
                                                 shared(bet_sb[:, :], TILES), ALU.add))
                    pool.wait_ge(z_ready.sem, z_ready.take())
                    nc.gpsimd.tensor_tensor(batch(h_sb, i - 1), batch(h_sb, i - 1), z[nxt][:, :, :],
                                            ALU.add).then_inc(h_ready.sem, 1)
                if has_next:
                    pool.wait_ge(b2_ready.sem, b2_ready.take())
                    step(nc.gpsimd.tensor_tensor(base[nxt][:, :, :], batch(y_all, i + 1),
                                                 shared(b2s[nxt][:, 0, :], TILES), ALU.add))
                    nc.gpsimd.tensor_tensor(base[nxt][:, :, :], base[nxt][:, :, :],
                                            shared(b2s[nxt][:, 1, :], TILES), ALU.add).then_inc(base_ready.sem, 1)
                if settle:
                    for q in (idx_copied, w_free, var_ready, z_ready, b2_ready, pool_done):
                        q.settle(pool)
            pool.wait_ge(loaded, 32)
            turns(pool, body)

        @block.tensor
        def _(pe):
            def body(i, par, count, has_prev, has_this, has_next, settle=True):
                nxt = 1 - par
                if has_next:
                    pe.wait_ge(y_ready.sem, y_ready.take())
                    if has_this:
                        pe.wait_ge(yT_ready.sem, yT_ready.take())
                    for j in range(TILES // 2):
                        last = nc.tensor.transpose(xps[:, j * P:(j + 1) * P],
                                                   y_b[nxt][:, 2 * j:2 * j + 2, :].rearrange("p t d -> p (t d)"),
                                                   ident[:, :])
                    last.then_inc(x_done.sem, 1)
                if has_this:
                    if not has_next:
                        pe.wait_ge(yT_ready.sem, yT_ready.take())
                    pe.wait_ge(w_ready.sem, w_ready.take())
                    for k in range(2):
                        for odd in range(2):
                            rows = slice(odd * D, (odd + 1) * D)
                            last = nc.tensor.matmul(hps[k][:, odd * HALF:(odd + 1) * HALF], w_g[par][rows, k, 0:HID1],
                                                    yT[par][rows, :], start=True, stop=True)
                        last.then_inc(h_done.sem, 1)
                    for k in range(2):
                        pe.wait_ge(gelu_done.sem, gelu_done.take())
                        for t in range(TILES):
                            at = t % 2 * HALF + t // 2 * P
                            last = nc.tensor.matmul(yps[par][:, t * D:(t + 1) * D], hid[k][:, at:at + P],
                                                    w2s[par][:, k, :], start=(k == 0 and t == 0), stop=(k == 1),
                                                    skip_group_check=True)
                    last.then_inc(out_done.sem, 1)
                if settle:
                    for q in (y_ready, yT_ready, w_ready, gelu_done):
                        q.settle(pe)
            turns(pe, body)

        @block.scalar
        def _(act):
            def body(i, par, count, has_prev, has_this, has_next, settle=True):
                nxt = 1 - par
                if has_next:
                    act.wait_ge(x_done.sem, x_done.take())
                    nc.scalar.activation(yT[nxt][:, :], xps[:, :], ACT.Copy).then_inc(yT_ready.sem, 1)
                for k in range(2):
                    if has_this:
                        act.wait_ge(h_done.sem, h_done.take())
                        nc.scalar.activation(hid[k][:, :], hps[k][:, :], ACT.Gelu,
                                             bias=w_g[par][:, k, ROW_B1:ROW_B1 + 1], scale=1.0).then_inc(gelu_done.sem, 1)
                    if k == 0 and has_prev:
                        act.wait_ge(centred.sem, centred.take())
                        nc.scalar.activation(sq[:, :, :], z[nxt][:, :, :], ACT.Square).then_inc(squared.sem, 1)
                if has_this:
                    act.drain().then_inc(w_free.sem, 1)
                if settle:
                    for q in (x_done, h_done, centred):
                        q.settle(act)
            turns(act, body)

        @block.vector
        def _(dve):
            dve.wait_ge(loaded, 32)

            def link(ins):
                ins.then_inc(chain.sem, 1)
                dve.wait_ge(chain.sem, chain.take())

            def body(i, par, count, has_prev, has_this, has_next, settle=True):
                nxt = 1 - par
                if has_prev:
                    zb, mb = z[nxt][:, :, :], zm[:, :]
                    dve.wait_ge(base_ready.sem, base_ready.take())
                    dve.wait_ge(out_done.sem, out_done.take())
                    link(nc.vector.tensor_tensor(zb, yps[nxt][:, :].rearrange("p (t d) -> p t d", d=D),
                                                 base[nxt][:, :, :], ALU.add))
                    link(nc.vector.reduce_sum(mb, zb, AX.X))
                    link(nc.vector.tensor_scalar(mb, mb, 1.0 / D, None, ALU.mult))
                    nc.vector.tensor_tensor(zb, zb, wide(mb, D), ALU.subtract).then_inc(centred.sem, 1)
                if has_next:
                    dve.wait_ge(landed[nxt], count * 32)
                    for k in range(2):
                        w = route_w[:, k, i + 1:i + 2] if isinstance(i, int) else route_w[:, k, bass.ds(i + 1, 1)]
                        nc.vector.tensor_scalar(b2s[nxt][:, k, :], w_g[nxt][:, k, ROW_B2:ROW_B2 + D], w, None, ALU.mult)
                        last = nc.vector.tensor_scalar(w2s[nxt][:, k, :], w_g[nxt][:, k, ROW_W2:ROW_W2 + D], w, None,
                                                       ALU.mult)
                    last.then_inc(w_ready.sem, 1)
                    dve.drain().then_inc(b2_ready.sem, 1)
                if has_prev:
                    dve.wait_ge(squared.sem, squared.take())
                    link(nc.vector.reduce_sum(zv[nxt][:, :], sq[:, :, :], AX.X))
                    nc.vector.tensor_scalar(zv[nxt][:, :], zv[nxt][:, :], 1.0 / D, EPS, ALU.mult,
                                            ALU.add).then_inc(var_ready.sem, 1)
                    link(nc.vector.tensor_tensor(zb, zb, shared(gam_sb[:, :], TILES), ALU.mult))
                    dve.wait_ge(rstd_ready.sem, rstd_ready.take())
                    nc.vector.tensor_tensor(zb, zb, wide(rstd[:, :], D), ALU.mult).then_inc(z_ready.sem, 1)
                if settle:
                    for q in (base_ready, out_done, squared, rstd_ready, chain):
                        q.settle(dve)
            turns(dve, body)


INS = {
    "x": ((NB, T), I32), "table": ((VOCAB + 2 * PAD, D), F32), "conv_w": ((KS * D, D), F32), "conv_b": ((D,), F32),
    "qkv_w": ((D, 3 * HEADS * DH), F32), "gate_w": ((D, HEADS * DH), F32), "gate_b": ((P, GROUPS), F32),
    "fin_w": ((HEADS * DH, D), F32), "fin_b": ((D,), F32), "ln_gamma": ((D,), F32), "ln_beta": ((D,), F32),
    "m0_wr": ((D, EXPERTS), F32), "m0_br": ((EXPERTS,), F32), "m0_lng": ((D, EXPERTS), F32),
    "m0_lnb": ((D, EXPERTS), F32), "m0_w1": ((EXPERTS, D, HID0), F32), "m0_b1": ((P, HT), F32),
    "m0_w2": ((EXPERTS, HID0, D), F32), "m0_b2": ((EXPERTS * D,), F32),
    "a1_g": ((1,), F32), "a1_wuv": ((D, 3 * S1), F32), "a1_buv": ((3 * S1,), F32), "a1_gamma": ((S1, 2), F32),
    "a1_beta": ((S1, 2), F32), "a1_wo": ((S1, D), F32), "a1_bo": ((D,), F32),
    "m1_wr": ((D, EXPERTS), F32), "m1_br": ((EXPERTS,), F32), "m1_table": ((EXPERTS * P, ROW), F32),
    "m1_gamma": ((D,), F32), "m1_beta": ((D,), F32),
}


def build(nc, a, out):
    with ExitStack() as ctx:
        h_sb = ctx.enter_context(nc.sbuf_tensor("h", [P, NT, D], F32))
        stats = ctx.enter_context(nc.sbuf_tensor("stats", [P, 5, NT], F32))
        ident = ctx.enter_context(nc.sbuf_tensor("ident", [P, P], F32))
        emit_identity(nc, ctx, ident)
        emit_embedding(nc, a["x"], a["table"], a["conv_w"], a["conv_b"], h_sb, ident)
        emit_layernorm(nc, "ln1", h_sb, stats, "norm")
        emit_attention0(nc, h_sb, stats, ident, a["qkv_w"], a["gate_w"], a["gate_b"], a["fin_w"], a["fin_b"],
                        a["ln_gamma"], a["ln_beta"])
        emit_layernorm(nc, "ln2", h_sb, stats, "norm")
        emit_moe0(nc, h_sb, stats, ident, *(a["m0_" + n] for n in ("wr", "br", "lng", "lnb", "w1", "b1", "w2", "b2")))
        emit_layernorm(nc, "ln3", h_sb, stats, "rms", a["a1_g"])
        emit_attention1(nc, h_sb, stats, ident, *(a["a1_" + n] for n in ("wuv", "buv", "gamma", "beta", "wo", "bo")))
        emit_layernorm(nc, "ln4", h_sb, stats, "norm")
        emit_moe1(nc, h_sb, stats, ident, *(a["m1_" + n] for n in ("wr", "br", "table", "gamma", "beta")), out)


def kernel(**inputs):
    import concourse.bacc as bacc
    from concourse.bass_utils import run_bass_kernel_spmd

    g = {k: np.asarray(v) for k, v in inputs.items()}
    arrays = {
        "x": g["x"], "table": np.pad(g["L0_tok_emb"], ((PAD, PAD), (0, 0)), mode="edge"),
        "conv_w": g["L0_tok_W"].transpose(2, 1, 0).reshape(KS * D, D), "conv_b": g["L0_tok_b"],
        "qkv_w": g["L0_attn_W_qkv"].T, "gate_w": g["L0_attn_W_gate"].T, "gate_b": g["L0_attn_b_gate"].reshape(GROUPS, P).T,
        "fin_w": g["L0_attn_W_final"].T, "fin_b": g["L0_attn_b_final"], "ln_gamma": g["L0_attn_ln_gamma"],
        "ln_beta": g["L0_attn_ln_beta"],
        "m0_wr": g["L0_ffn_Wr"], "m0_br": g["L0_ffn_br"], "m0_lng": g["L0_ffn_ln_g"].T, "m0_lnb": g["L0_ffn_ln_b"].T,
        "m0_w1": g["L0_ffn_W1"], "m0_b1": g["L0_ffn_b1"].reshape(HT, P).T, "m0_w2": g["L0_ffn_W2"],
        "m0_b2": g["L0_ffn_b2"].reshape(-1),
        "a1_g": g["L1_attn_g"].reshape(1), "a1_wuv": g["L1_attn_W_uv"], "a1_buv": g["L1_attn_b_uv"],
        "a1_gamma": g["L1_attn_gamma"].T, "a1_beta": g["L1_attn_beta"].T, "a1_wo": g["L1_attn_W_o"],
        "a1_bo": g["L1_attn_b_o"],
        "m1_wr": g["L1_ffn_Wr"], "m1_br": g["L1_ffn_br"], "m1_gamma": g["L1_ffn_gamma"], "m1_beta": g["L1_ffn_beta"],
        "m1_table": np.concatenate([
            np.tile(g["L1_ffn_W1"], (1, P // D, 1)), g["L1_ffn_W2"],
            np.broadcast_to(g["L1_ffn_b2"][:, None, :], (EXPERTS, P, D)), g["L1_ffn_b1"][:, :, None],
        ], axis=2).reshape(EXPERTS * P, ROW),
    }
    nc = bacc.Bacc("TRN2", target_bir_lowering=False, num_devices=1)
    aps = {n: nc.dram_tensor(f"in_{n}", shape, dt, kind="ExternalInput").ap() for n, (shape, dt) in INS.items()}
    out = nc.dram_tensor("out_h", (NB, T, D), F32, kind="ExternalOutput").ap()
    build(nc, aps, out)
    r = run_bass_kernel_spmd(nc, [{f"in_{n}": np.ascontiguousarray(arrays[n]) for n in INS}], core_ids=[0])
    return r.results[0]["out_h"]
```

```python
from contextlib import ExitStack

import numpy as np

import concourse.bass as bass
from concourse import mybir

F32 = mybir.dt.float32
F16 = mybir.dt.float16
I32 = mybir.dt.int32
U32 = mybir.dt.uint32
ALU = mybir.AluOpType
ACT = mybir.ActivationFunctionType
AX = mybir.AxisListType

P = 128
NB, T, D = 16, 1024, 64
TILES = T // P
NT = NB * TILES
VOCAB, KS = 50257, 9
PAD = KS - 1
HEADS, DH = 8, 32
GROUPS, HG = 2, 4
SCALE0 = DH ** -0.5
EPS = 1e-5
HALF = 512


class Signal:

    def __init__(self, ctx, nc, name, credits=0):
        self.sem = ctx.enter_context(nc.semaphore(name))
        self.credits = credits
        self.taken = 0

    def open(self, eng):
        eng.sem_inc(self.sem, self.credits)

    def take(self, n=1):
        self.taken += n
        return self.taken

    def settle(self, eng):
        if self.taken:
            eng.sem_inc(self.sem, -self.taken)
        self.taken = 0


def batch(tensor, b):
    return tensor[:, bass.ds(b * TILES, TILES)]


def wide(ap, n):
    return ap.unsqueeze(2).to_broadcast([ap.shape[0], ap.shape[1], n])


def shared(ap, n):
    return ap.unsqueeze(1).to_broadcast([ap.shape[0], n, ap.shape[1]])


def emit_identity(nc, ctx, ident):
    with nc.semaphore("ident_zero") as zeroed, nc.Block() as block:
        @block.gpsimd
        def _(pool):
            pool.memset(ident[:, :], 0.0).then_inc(zeroed, 1)
            pool.wait_ge(zeroed, 1)
            pool.affine_select(out=ident[:, :], in_=ident[:, :], compare_op=ALU.not_equal, fill=1.0,
                               base=0, pattern=[[-1, P]], channel_multiplier=1)


def emit_embedding(nc, x, table, w, bias, h_sb, ident):
    WIN = KS * D
    CHUNKS = 5
    starts = [0, 128, 256, 384, WIN - P]
    with ExitStack() as ctx:
        sb = lambda name, shape, dt=F32: ctx.enter_context(nc.sbuf_tensor(name, shape, dt))
        xi = sb("xi", [P, NT], I32)
        rows = sb("rows", [P, NT], I32)
        idx = sb("idx", [P, 2, TILES], I32)
        win = sb("win", [P, TILES, WIN])
        winT = sb("winT", [P, 4, CHUNKS * P])
        w_sb = sb("conv_w", [P, CHUNKS, D])
        b_bc = sb("conv_b", [P, D])
        psT = [ctx.enter_context(nc.psum_tensor(f"psT{i}", [P, 2 * HALF], F32)) for i in range(2)]
        psO = [ctx.enter_context(nc.psum_tensor(f"psO{i}", [P, HALF], F32)) for i in range(2)]
        s = lambda name, credits=0: Signal(ctx, nc, name, credits)
        x_loaded = ctx.enter_context(nc.semaphore("x_loaded"))
        w_loaded = s("w_loaded")
        b_loaded = s("b_loaded")
        clipped = ctx.enter_context(nc.semaphore("clipped"))
        rows_ready = ctx.enter_context(nc.semaphore("rows_ready"))
        idx_copied = s("idx_copied")
        landed = [ctx.enter_context(nc.semaphore(f"win_landed{t}")) for t in range(TILES)]
        win_free = s("win_free", TILES)
        t_done_a = s("t_done_a")
        t_done_v = s("t_done_v")
        wT_a = s("wT_a")
        wT_v = s("wT_v")
        conv_done = s("conv_done")
        out_read = s("out_read", 2)
        block = ctx.enter_context(nc.Block())

        @block.sync
        def _(sp):
            sp.dma_start(xi[:, :].rearrange("p (b t) -> p b t", t=TILES),
                         x.rearrange("b (p t) -> p b t", t=TILES)).then_inc(x_loaded, 16)
            sp.dma_start(w_sb[:, 0:4, :], w[0:4 * P, :].rearrange("(c p) o -> p c o", p=P)).then_inc(w_loaded.sem, 16)
            sp.dma_start(w_sb[D:P, 4, :], w[4 * P:WIN, :]).then_inc(w_loaded.sem, 16)
            sp.dma_start(b_bc[:, :], bias.partition_broadcast(P)).then_inc(b_loaded.sem, 16)

        @block.gpsimd
        def _(pool):
            win_free.open(pool)
            pool.wait_ge(rows_ready, 1)
            with pool.Fori(0, NB // 2) as b2:
                for par in range(2):
                    pool.tensor_copy(idx[:, par, :], batch(rows, b2 * 2 + par)).then_inc(idx_copied.sem, 1)
                    pool.wait_ge(idx_copied.sem, idx_copied.take())
                    for t in range(TILES):
                        pool.wait_ge(win_free.sem, win_free.take())
                        pool.indirect_dma_start(
                            out=win[:, t, :], out_offset=None, in_=table[:, :],
                            in_offset=bass.IndirectOffsetOnAxis(ap=idx[:, par, t:t + 1], axis=0),
                        ).then_inc(landed[t], 16)
                idx_copied.settle(pool)
                win_free.settle(pool)

        @block.tensor
        def _(pe):
            out_read.open(pe)
            pe.wait_ge(w_loaded.sem, 32)

            def transpose(b, t):
                pe.wait_ge(landed[t], b * 16 + 16)
                for c in range(CHUNKS):
                    last = nc.tensor.transpose(psT[t % 2][:, c * P:(c + 1) * P],
                                               win[:, t, starts[c]:starts[c] + P], ident[:, :])
                last.then_inc(t_done_a.sem if t % 2 == 0 else t_done_v.sem, 1)

            def conv(t, o):
                read = wT_a if t % 2 == 0 else wT_v
                pe.wait_ge(read.sem, read.take())
                for c in range(CHUNKS):
                    lo = 0 if c < 4 else D
                    last = nc.tensor.matmul(psO[o][:, t * D:(t + 1) * D], winT[lo:P, t % 4, c * P:(c + 1) * P],
                                            w_sb[lo:P, c, :], start=(c == 0), stop=(c == CHUNKS - 1))
                return last

            with pe.Fori(0, NB // 2) as b2:
                for par in range(2):
                    transpose(b2 * 2 + par, 0)
                    for t in range(TILES):
                        if t == 0:
                            pe.wait_ge(out_read.sem, out_read.take())
                        if t + 1 < TILES:
                            transpose(b2 * 2 + par, t + 1)
                        last = conv(t, par)
                        if t < TILES - 1:
                            last.then_inc(win_free.sem, 1)
                    last.then_inc(conv_done.sem, 1)
                    pe.drain().then_inc(win_free.sem, 1)
                for q in (wT_a, wT_v, out_read):
                    q.settle(pe)

        @block.scalar
        def _(act):
            with act.Fori(0, NB // 2) as b2:
                for par in range(2):
                    for t in range(0, TILES, 2):
                        act.wait_ge(t_done_a.sem, t_done_a.take())
                        nc.scalar.activation(winT[:, t % 4, :], psT[0][:, 0:CHUNKS * P], ACT.Copy).then_inc(wT_a.sem, 1)
                t_done_a.settle(act)

        @block.vector
        def _(dve):
            dve.wait_ge(x_loaded, 16)
            nc.vector.tensor_scalar(rows[:, :], xi[:, :], float(-(KS // 2)), float(VOCAB - 1 + KS // 2),
                                    ALU.max, ALU.min).then_inc(clipped, 1)
            dve.wait_ge(clipped, 1)
            nc.vector.tensor_scalar(xi[:, :], rows[:, :], float(PAD - KS // 2), None, ALU.add).then_inc(clipped, 1)
            dve.wait_ge(clipped, 2)
            nc.vector.tensor_copy(rows[:, :], xi[:, :]).then_inc(rows_ready, 1)
            dve.wait_ge(b_loaded.sem, 16)
            with dve.Fori(0, NB // 2) as b2:
                for par in range(2):
                    for t in range(1, TILES, 2):
                        dve.wait_ge(t_done_v.sem, t_done_v.take())
                        nc.vector.tensor_copy(winT[:, t % 4, :], psT[1][:, 0:CHUNKS * P]).then_inc(wT_v.sem, 1)
                    dve.wait_ge(conv_done.sem, conv_done.take())
                    nc.vector.tensor_tensor(batch(h_sb, b2 * 2 + par),
                                            psO[par][:, :].rearrange("p (t d) -> p t d", d=D),
                                            shared(b_bc[:, :], TILES), ALU.add).then_inc(out_read.sem, 1)
                t_done_v.settle(dve)
                conv_done.settle(dve)


def emit_layernorm(nc, tag, h_sb, stats, kind, g=None):
    mean, var, r1, r2, s2 = (stats[:, i, :] for i in range(5))
    CH = 4
    n = NT // CH
    with ExitStack() as ctx:
        centred = ctx.enter_context(nc.sbuf_tensor(f"{tag}_centred", [P, 2, n, D], F32))
        g_sb = ctx.enter_context(nc.sbuf_tensor(f"{tag}_g", [P, 1], F32))
        sem = lambda name: ctx.enter_context(nc.semaphore(f"{tag}_{name}"))
        g_loaded = sem("g_loaded")
        summed, meaned, centred_done, squared, var_done, root, chain = (
            sem(x) for x in ("summed", "meaned", "centred", "squared", "var", "root", "chain"))
        block = ctx.enter_context(nc.Block())
        part = lambda t, c: t[:, c * n:(c + 1) * n]

        @block.sync
        def _(sp):
            if kind == "rms":
                sp.dma_start(g_sb[:, :], g.partition_broadcast(P)).then_inc(g_loaded, 16)

        @block.vector
        def _(dve):
            links = [0]

            def link(ins):
                links[0] += 1
                ins.then_inc(chain, 1)
                dve.wait_ge(chain, links[0])

            for c in range(CH):
                nc.vector.reduce_sum(part(mean, c), part(h_sb, c), AX.X).then_inc(summed, 1)
                dve.wait_ge(summed, c + 1)
                nc.vector.tensor_scalar(part(mean, c), part(mean, c), 1.0 / D, None, ALU.mult).then_inc(meaned, 1)
            for c in range(CH):
                dve.wait_ge(squared, c + 1)
                nc.vector.reduce_sum(part(var, c), centred[:, c % 2], AX.X).then_inc(var_done, 1)
            dve.wait_ge(var_done, CH)
            link(nc.vector.tensor_scalar(var, var, 1.0 / D, None, ALU.mult))
            nc.vector.tensor_scalar(r2, var, EPS, None, ALU.add).then_inc(root, 1)
            dve.wait_ge(root, 2)
            link(nc.vector.reciprocal(r1, s2))
            link(nc.vector.tensor_tensor(var, var, r1, ALU.mult))
            link(nc.vector.tensor_tensor(var, var, r1, ALU.mult))
            nc.vector.tensor_scalar(r2, var, EPS if kind == "norm" else 0.0, None, ALU.add).then_inc(root, 1)
            dve.wait_ge(root, 4)
            if kind == "rms":
                link(nc.vector.tensor_scalar(s2, s2, EPS, None, ALU.max))
            link(nc.vector.reciprocal(r2, s2))
            if kind == "rms":
                dve.wait_ge(g_loaded, 16)
                link(nc.vector.tensor_scalar(r2, r2, g_sb[:, :], None, ALU.mult))

        @block.gpsimd
        def _(pool):
            for c in range(CH):
                pool.wait_ge(meaned, c + 1)
                if c >= 2:
                    pool.wait_ge(var_done, c - 1)
                nc.gpsimd.tensor_tensor(centred[:, c % 2], part(h_sb, c), wide(part(mean, c), D),
                                        ALU.subtract).then_inc(centred_done, 1)

        @block.scalar
        def _(act):
            for c in range(CH):
                act.wait_ge(centred_done, c + 1)
                nc.scalar.activation(centred[:, c % 2], centred[:, c % 2], ACT.Square).then_inc(squared, 1)
            act.wait_ge(root, 1)
            nc.scalar.activation(s2, r2, ACT.Sqrt).then_inc(root, 1)
            act.wait_ge(root, 3)
            nc.scalar.activation(s2, r2, ACT.Sqrt).then_inc(root, 1)


RING = 3
EG = 4
UNITS = GROUPS * TILES * HG
LAG = 8


READER = {"score": "act", "q": "act", "k": "act", "gate": "act", "xT": "dve", "v": "dve", "proj": "dve"}
OWN = {8: ("q", 1), 11: ("split_q", 1), 17: ("k", 1), 19: ("split_k", 1), 24: ("v", 1), 29: ("gate", 1)}
PREV = {13: ("proj", 0), 20: ("proj", 1)}
NEXT = {23: ("stage", 0), 27: ("base", 0), 35: ("xT", 0), 40: ("q", 0), 43: ("split_q", 0),
        46: ("k", 0), 51: ("split_k", 0), 54: ("v", 0), 59: ("gate", 0)}


class Event:

    def __init__(self, kind, n=0, quarter=0, final=False):
        self.kind, self.n, self.quarter, self.final, self.slot = kind, n, quarter, final, None
        self.group, self.tile, self.head = n // (TILES * HG), n // HG % TILES, n % HG
        self.slot_reader = None


def prep_events():
    return [Event("stage"), Event("base"), Event("xT"), Event("q", 0), Event("split_q", 0), Event("k", 0),
            Event("split_k", 0), Event("v", 0), Event("gate", 0)]


def batch_events(has_prev, has_next):
    queries = GROUPS * TILES
    events = []
    for u in range(UNITS + (0 if has_next else LAG)):
        if u < UNITS:
            events.append(Event("score", u))
        k, c = (u - LAG) // HG, (u - LAG) % HG
        if (k, c) in ((0, 0), (TILES, 0)) and (k or has_prev):
            events.append(Event("out", 0 if k else 1))
        if k in (0, TILES):
            quarters = {0: (), 1: (), 2: (0, 1), 3: (2, 3)}[c]
        else:
            quarters = (c,) if k >= 0 or has_prev else ()
        events += [Event("av", k % queries, quarter) for quarter in quarters]
        if u % HG == 2 and (u > HG or has_prev):
            events.append(Event("values", (u // HG - 1) % queries))
        for table, wanted in ((OWN, u < UNITS), (PREV, has_prev), (NEXT, has_next)):
            if u in table and wanted:
                events.append(Event(*table[u]))
    if not has_next:
        events += [Event("out", 1, final=True), Event("proj", 0, final=True), Event("proj", 1)]
    return events


def attention_schedule():
    stretches = [prep_events(), batch_events(False, True), batch_events(True, True), batch_events(True, False)]
    at = 0
    readers = ["act"] * RING
    for n, events in enumerate(stretches):
        start = at
        if n >= 2:
            assert readers == ["act"] * RING
        for e in events:
            if e.kind in READER:
                e.slot = at % RING
                e.slot_reader, readers[e.slot] = readers[e.slot], READER[e.kind]
                at += 1
        assert n != 2 or (at - start) % RING == 0, at - start
    return stretches


def emit_attention0(nc, h_sb, stats, ident, wqkv, wgate, bgate, wfin, bfin, gamma, beta):
    mean, r1, r2 = stats[:, 0, :], stats[:, 2, :], stats[:, 3, :]
    schedule = attention_schedule()
    with ExitStack() as ctx:
        sb = lambda name, shape, dt=F32: ctx.enter_context(nc.sbuf_tensor(name, shape, dt))
        w_n = sb("w_qkv", [P, 3 * HEADS * DH])
        w_y = sb("w_gate", [P, HEADS * DH])
        w_f = sb("w_fin", [P, GROUPS, D])
        b_g = sb("b_gate", [P, GROUPS])
        b_f = sb("b_fin", [P, D])
        aff = sb("aff", [P, 2])
        xT = sb("xT", [P, T])
        split_in = [sb(f"split_in{i}", [P, T]) for i in range(2)]
        yn = split_in[0][:, :].rearrange("p (t c) -> p t c", t=TILES)
        hi = [sb(f"split_hi{i}", [P, T], F16) for i in range(2)]
        lo = [sb(f"split_lo{i}", [P, T], F16) for i in range(2)]
        q_st = [sb(f"q_stack{g}", [3 * DH, HG, T], F16) for g in range(GROUPS)]
        k_st = [sb(f"k_stack{g}", [3 * DH, HG, T], F16) for g in range(GROUPS)]
        v_sb = [sb(f"v{g}", [P, TILES, HG * DH]) for g in range(GROUPS)]
        gate = [sb(f"gate{g}", [P, T]) for g in range(GROUPS)]
        gated = [sb(f"gated{g}", [P, T]) for g in range(GROUPS)]
        e_sb = sb("exps", [P, EG, HG, T])
        nmax = sb("nmax", [P, HG])
        zsum = sb("zsum", [P, EG, HG])
        rz = sb("rz", [P, EG, HG])
        vz = sb("vz", [P, EG, HG * DH])
        ring = [ctx.enter_context(nc.psum_tensor(f"ring{i}", [P, T], F32)) for i in range(RING)]
        outT = ctx.enter_context(nc.psum_tensor("outT", [P, T], F32))

        s = lambda name, credits=0: Signal(ctx, nc, name, credits)
        w_loaded = ctx.enter_context(nc.semaphore("w_loaded"))
        w_scaled = s("w_scaled")
        b_scaled = s("b_scaled")
        slot_free = {"act": s("slot_free_a", RING),
                     "dve": s("slot_free_v")}
        score_done = s("score_done")
        max_done = s("max_done")
        item_done = {"act": s("item_done_a"),
                     "dve": s("item_done_v")}
        exps_ended = s("exps_ended")
        sums_ended = s("sums_ended")
        rz_done = s("rz_done")
        vz_done = s("vz_done")
        e_free = s("e_free", EG)
        out_free = s("out_free", 1)
        staged = s("staged")
        copied = s("copied")
        split_done = s("split_done")
        stacked = [s(f"stacked{g}") for g in range(GROUPS)]
        pool_done = s("pool_done")
        block = ctx.enter_context(nc.Block())
        LOADS = 7
        STACK_DMAS = 2 * 3 * HG

        def turns(eng, body):
            body(None, 0, schedule[0])
            body(0, 1, schedule[1])
            with eng.Fori(1, NB - 1) as b:
                body(b, b + 1, schedule[2])
            body(NB - 1, None, schedule[3])

        @block.sync
        def _(sp):
            for dst, src in ((w_n[D:P, :], wqkv), (w_y[0:D, :], wgate),
                             (w_f[:, :, :], wfin.rearrange("(g p) o -> p g o", p=P)),
                             (b_g[:, :], bgate),
                             (b_f[:, :], bfin.partition_broadcast(P)),
                             (aff[D:P, 0:1], gamma.unsqueeze(1)), (aff[D:P, 1:2], beta.unsqueeze(1))):
                sp.dma_start(dst, src).then_inc(w_loaded, 16)

            def body(b, b_next, events):
                for e in events:
                    if e.kind not in ("split_q", "split_k"):
                        continue
                    i = 0 if e.kind == "split_q" else 1
                    stack = (q_st, k_st)[i][e.n]
                    parts = ((hi[0], lo[0], hi[0]), (hi[1], hi[1], lo[1]))[i]
                    sp.wait_ge(split_done.sem, split_done.take())
                    for n, part in enumerate(parts):
                        for h in range(HG):
                            sp.dma_start(stack[n * DH:(n + 1) * DH, h, :],
                                         part[h * DH:(h + 1) * DH, :]).then_inc(stacked[e.n].sem, 16)
                split_done.settle(sp)
            turns(sp, body)

        @block.tensor
        def _(pe):
            slot_free["act"].open(pe)
            out_free.open(pe)
            pe.wait_ge(w_loaded, LOADS * 16)
            pe.wait_ge(w_scaled.sem, w_scaled.take())

            def body(b, b_next, events):
                unread = 0
                for e in events:
                    if e.kind in READER:
                        tile = ring[e.slot]
                        if e.kind == "score" and e.n % (TILES * HG) == 0:
                            stack = stacked[e.group]
                            pe.wait_ge(stack.sem, stack.take(STACK_DMAS * 16))
                        if e.kind == "xT":
                            pe.wait_ge(staged.sem, staged.take())
                        if e.kind == "proj" and e.final:
                            pe.wait_ge(out_free.sem, out_free.take())
                        free = slot_free[e.slot_reader]
                        unread += (READER[e.kind] == "dve") - (e.slot_reader == "dve")
                        pe.wait_ge(free.sem, free.take())
                        if e.kind == "q" and e.n == 0 and unread:
                            xT_read = slot_free["dve"]
                            pe.wait_ge(xT_read.sem, xT_read.taken + unread)
                    if e.kind == "score":
                        for j in range(2):
                            last = nc.tensor.matmul(tile[:, j * HALF:(j + 1) * HALF],
                                                    q_st[e.group][:, e.head, e.tile * P:(e.tile + 1) * P],
                                                    k_st[e.group][:, e.head, j * HALF:(j + 1) * HALF],
                                                    start=True, stop=True)
                        last.then_inc(score_done.sem, 1)
                    elif e.kind == "av":
                        c, first = e.quarter, e.n % TILES == 0
                        if c == 0:
                            pe.wait_ge(vz_done.sem, vz_done.take())
                        if c == 0 and first:
                            pe.wait_ge(out_free.sem, out_free.take())
                        quarter = slice(c * T // 4, (c + 1) * T // 4)
                        for h in range(HG):
                            last = nc.tensor.matmul(outT[h * DH:(h + 1) * DH, quarter],
                                                    vz[:, e.n % EG, h * DH:(h + 1) * DH],
                                                    e_sb[:, e.n % EG, h, quarter], start=first and c % 2 == 0,
                                                    stop=e.n % TILES == TILES - 1, skip_group_check=True)
                        if c == 3:
                            last.then_inc(e_free.sem, 1)
                    elif e.kind == "xT":
                        for t in range(TILES):
                            last = nc.tensor.transpose(tile[:, t * P:(t + 1) * P], yn[:, t, :], ident[:, :])
                        last.then_inc(item_done["dve"].sem, 1)
                    elif e.kind in ("q", "k", "gate"):
                        col = e.n * P + (HEADS * DH if e.kind == "k" else 0)
                        w, rows = (w_y, slice(0, D)) if e.kind == "gate" else (w_n, slice(D, P))
                        for j in range(2):
                            last = nc.tensor.matmul(tile[:, j * HALF:(j + 1) * HALF], w[rows, col:col + P],
                                                    xT[rows, j * HALF:(j + 1) * HALF], start=True, stop=True)
                        last.then_inc(item_done["act"].sem, 1)
                    elif e.kind == "v":
                        col = 2 * HEADS * DH + e.n * P
                        for t in range(TILES):
                            last = nc.tensor.matmul(tile[:, t * P:(t + 1) * P], xT[D:P, t * P:(t + 1) * P],
                                                    w_n[D:P, col:col + P], start=True, stop=True)
                        last.then_inc(item_done["dve"].sem, 1)
                    elif e.kind == "proj":
                        for i in range(TILES // 2):
                            t = e.n * TILES // 2 + i
                            for g in range(GROUPS):
                                last = nc.tensor.matmul(tile[:, i * D:(i + 1) * D], gated[g][:, t * P:(t + 1) * P],
                                                        w_f[:, g, :], start=(g == 0), stop=(g == 1))
                        last.then_inc(item_done["dve"].sem, 1)
                    elif e.kind == "out" and e.final:
                        pe.drain().then_inc(sums_ended.sem, 1)
                for q in (w_scaled, *slot_free.values(), out_free, vz_done, staged, *stacked):
                    q.settle(pe)
            turns(pe, body)

        @block.vector
        def _(dve):
            dve.wait_ge(w_loaded, LOADS * 16)
            nc.vector.memset(aff[0:D, 0:1], 1.0)
            nc.vector.memset(aff[0:D, 1:2], 0.0)
            nc.vector.tensor_scalar(b_g[:, :], b_g[:, :], 0.5, None, ALU.mult).then_inc(b_scaled.sem, 1)
            nc.vector.tensor_scalar(w_f[:, :, :], w_f[:, :, :], 0.5, None, ALU.mult).then_inc(w_scaled.sem, 1)

            def body(b, b_next, events):
                for n, e in enumerate(events):
                    if e.kind == "score":
                        dve.wait_ge(score_done.sem, score_done.take())
                        nc.vector.tensor_reduce(nmax[:, e.head:e.head + 1], ring[e.slot][:, :], axis=AX.X,
                                                op=ALU.max, negate=True).then_inc(max_done.sem, 1)
                    elif e.kind == "values":
                        if b_next is None and e.n == GROUPS * TILES - 1 and n > len(events) // 2:
                            dve.wait_ge(exps_ended.sem, exps_ended.take())
                        nc.vector.reciprocal(rz[:, e.n % EG, :], zsum[:, e.n % EG, :]).then_inc(rz_done.sem, 1)
                    elif e.kind == "out":
                        if e.final:
                            dve.wait_ge(sums_ended.sem, sums_ended.take())
                        nc.vector.scalar_tensor_tensor(gated[e.n][:, :], gate[e.n][:, :], 1.0, outT[:, :],
                                                       ALU.add, ALU.mult).then_inc(out_free.sem, 1)
                    elif READER.get(e.kind) == "dve":
                        done, free, tile = item_done["dve"], slot_free["dve"], ring[e.slot]
                        dve.wait_ge(done.sem, done.take())
                        if e.kind == "xT":
                            nc.vector.tensor_scalar(xT[:, :], tile[:, :], aff[:, 0:1], aff[:, 1:2], ALU.mult,
                                                    ALU.add).then_inc(free.sem, 1)
                        elif e.kind == "v":
                            nc.vector.tensor_copy(v_sb[e.n][:, :, :].rearrange("p t d -> p (t d)"),
                                                  tile[:, :]).then_inc(free.sem, 1)
                        elif e.kind == "proj":
                            last_batch = b_next is None and n >= len(events) - 2
                            half = TILES // 2
                            at = NB - 1 if last_batch else b - 1
                            h = h_sb[:, bass.ds(at * TILES + e.n * half, half)]
                            nc.vector.tensor_tensor(h, h, tile[:, 0:half * D].rearrange("p (t d) -> p t d", d=D),
                                                    ALU.add).then_inc(free.sem, 1)
                for q in (score_done, item_done["dve"], exps_ended, sums_ended):
                    q.settle(dve)
            turns(dve, body)

        @block.scalar
        def _(act):
            e_free.open(act)
            act.wait_ge(w_loaded, LOADS * 16)
            act.wait_ge(b_scaled.sem, b_scaled.take())

            def body(b, b_next, events):
                for e in events:
                    if READER.get(e.kind) != "act":
                        continue
                    tile, free, done = ring[e.slot], slot_free["act"], item_done["act"]
                    if e.kind == "score":
                        act.wait_ge(max_done.sem, max_done.take())
                        k = e.tile % EG
                        if e.head == 0:
                            act.wait_ge(e_free.sem, e_free.take())
                        nc.scalar.activation(e_sb[:, k, e.head, :], tile[:, :], ACT.Exp,
                                             bias=nmax[:, e.head:e.head + 1], scale=1.0,
                                             accum_out=zsum[:, k, e.head:e.head + 1]).then_inc(free.sem, 1)
                        if e.n == UNITS - 1 and b_next is None:
                            act.drain().then_inc(exps_ended.sem, 1)
                        continue
                    act.wait_ge(done.sem, done.take())
                    if e.kind in ("q", "k"):
                        i = 0 if e.kind == "q" else 1
                        nc.scalar.activation(hi[i][:, :], tile[:, :], ACT.Copy, scale=(SCALE0, 1.0)[i])
                        nc.scalar.activation(split_in[i][:, :], tile[:, :], ACT.Copy,
                                             scale=(SCALE0, 1.0)[i]).then_inc(free.sem, 1)
                        act.drain().then_inc(copied.sem, 1)
                    elif e.kind == "gate":
                        nc.scalar.activation(gate[e.n][:, :], tile[:, :], ACT.Tanh, bias=b_g[:, e.n:e.n + 1],
                                             scale=0.5).then_inc(free.sem, 1)
                for q in (b_scaled, max_done, e_free, item_done["act"]):
                    q.settle(act)
            turns(act, body)

        @block.gpsimd
        def _(pool):
            pool.wait_ge(w_loaded, LOADS * 16)

            def body(b, b_next, events):
                for e in events:
                    if e.kind == "values":
                        pool.wait_ge(rz_done.sem, rz_done.take())
                        k = e.n % EG
                        v = v_sb[e.n // TILES][:, e.n % TILES, :].rearrange("p (h d) -> p h d", h=HG)
                        nc.gpsimd.tensor_tensor(vz[:, k, :].rearrange("p (h d) -> p h d", h=HG), v,
                                                wide(rz[:, k, :], DH), ALU.mult).then_inc(vz_done.sem, 1)
                    elif e.kind in ("split_q", "split_k"):
                        i = 0 if e.kind == "split_q" else 1
                        pool.wait_ge(copied.sem, copied.take())
                        nc.gpsimd.tensor_tensor(lo[i][:, :], split_in[i][:, :], hi[i][:, :],
                                                ALU.subtract).then_inc(split_done.sem, 1)
                    elif e.kind == "stage":
                        y = yn[:, :, 0:D]
                        for src, stat, op in ((batch(h_sb, b_next), mean, ALU.subtract), (y, r1, ALU.mult)):
                            nc.gpsimd.tensor_tensor(y, src, wide(batch(stat, b_next), D), op).then_inc(pool_done.sem, 1)
                            pool.wait_ge(pool_done.sem, pool_done.take())
                        nc.gpsimd.tensor_tensor(yn[:, :, D:2 * D], y, wide(batch(r2, b_next), D), ALU.mult)
                    elif e.kind == "base":
                        h = batch(h_sb, b_next)
                        nc.gpsimd.tensor_tensor(h, h, shared(b_f[:, :], TILES), ALU.add).then_inc(pool_done.sem, 1)
                        pool.wait_ge(pool_done.sem, pool_done.take())
                        nc.gpsimd.tensor_tensor(h, h, yn[:, :, 0:D], ALU.add).then_inc(staged.sem, 1)
                for q in (rz_done, copied, pool_done):
                    q.settle(pool)
            turns(pool, body)


EXPERTS, HID0 = 8, 256
HC = HID0 // P
HT = EXPERTS * HC
WS = 64.0
TE = TILES * EXPERTS
SIDE = {2: ("back", 0), 4: ("tokens", 0), 5: ("tokens", 1), 7: ("router", 0), 12: ("weights", 0)}


def emit_moe0(nc, h_sb, stats, ident, wr, br, lng, lnb, w1, b1, w2, b2):
    mean, r1, r2, s2 = (stats[:, i, :] for i in (0, 2, 3, 4))
    with ExitStack() as ctx:
        sb = lambda name, shape, dt=F32: ctx.enter_context(nc.sbuf_tensor(name, shape, dt))
        w1f = sb("w1f", [P, EXPERTS, HID0])
        w1h = sb("w1h", [P, HT, P], F16)
        w1l = sb("w1l", [P, HT, P], F16)
        lng_sb = sb("lng", [P, EXPERTS])
        lnb_sb = sb("lnb", [P, EXPERTS])
        wrf = sb("wrf", [P, EXPERTS])
        wrh = sb("wrh", [P, EXPERTS], F16)
        wrl = sb("wrl", [P, EXPERTS], F16)
        br_sb = sb("br", [P, EXPERTS])
        b1_sb = sb("b1", [P, HT])
        w2_sb = sb("w2", [P, HT, D])
        b2_sb = sb("b2", [P, EXPERTS])
        iota_i = sb("iota_i", [P, EXPERTS], I32)
        iota = sb("iota", [P, EXPERTS])
        euler = sb("euler", [P, TILES])
        select = sb("select", [P, TE, D], F16)
        xn = sb("xn", [P, TILES, 2 * D])
        xs = [sb(f"xs{i}", [P, T], F16) for i in range(2)]
        hid = [sb(f"hid{i}", [P, T]) for i in range(2)]
        logits = sb("logits", [P, TILES, EXPERTS])
        top = sb("top", [P, TILES, 8])
        top_i = sb("top_i", [P, TILES, 8], U32)
        top_f = sb("top_f", [P, 2, TILES])
        gap = sb("gap", [P, TILES])
        e2 = sb("e2", [P, TILES])
        tw = sb("tw", [P, 2, TILES])
        den = sb("den", [P, TILES])
        pick = sb("pick", [P, 2, TILES, EXPERTS])
        wt = sb("wt", [P, 2, TE])
        wts = [sb(f"wts{i}", [P, P], F16) for i in range(2)]
        acc = sb("acc", [P, HALF])
        wb = [sb(f"wb{i}", [P, HALF]) for i in range(2)]
        term = [sb(f"term{i}", [P, HALF]) for i in range(2)]
        hps = [ctx.enter_context(nc.psum_tensor(f"hps{i}", [P, T], F32)) for i in range(2)]
        yps = [ctx.enter_context(nc.psum_tensor(f"yps{i}", [P, HALF], F32)) for i in range(2)]
        wps = ctx.enter_context(nc.psum_tensor("wps", [P, HALF], F32))
        side = ctx.enter_context(nc.psum_tensor("side", [P, HALF], F32))

        s = lambda name, credits=0: Signal(ctx, nc, name, credits)
        LOADS = 13
        loaded = ctx.enter_context(nc.semaphore("loaded"))
        consts = s("consts")
        folded_v = s("folded_v")
        w_ready = s("w_ready")
        b1_ready = s("b1_ready")
        xn_ready = s("xn_ready")
        side_done = s("side_done")
        side_read = s("side_read", 1)
        xs_ready = s("xs_ready")
        wt_ready = s("wt_ready")
        wts_ready = s("wts_ready")
        h_done = s("h_done")
        gelu_done = s("gelu_done")
        wps_done = s("wps_done")
        wps_read = s("wps_read", 1)
        wb_ready = s("wb_ready")
        y_done = s("y_done")
        y_read = s("y_read", 1)
        gap_ready = s("gap_ready")
        e2_ready = s("e2_ready")
        term_done = s("term_done")
        term_free = s("term_free", 2)
        acc_ready = s("acc_ready")
        chain = s("dve_chain")
        pool_done = s("pool_done0")
        block = ctx.enter_context(nc.Block())

        def turns(eng, body):
            body(0, 0, prev=False)
            with eng.Fori(0, (NB - 2) // 2) as r:
                body(r * 2 + 1, 1, settle=False)
                body(r * 2 + 2, 0)
            body(NB - 1, 1, next=False)

        def due(ht, prev, next):
            kind, n = SIDE.get(ht, (None, 0))
            return (kind, n) if (prev if kind == "back" else next) else (None, 0)

        @block.sync
        def _(sp):
            for half in (slice(0, D), slice(D, P)):
                for dst, src in ((w1f[half, :, :], w1.rearrange("e d h -> d e h")), (lng_sb[half, :], lng),
                                 (lnb_sb[half, :], lnb), (wrf[half, :], wr), (b2_sb[half, :], b2)):
                    sp.dma_start(dst, src).then_inc(loaded, 16)
            for dst, src in ((br_sb[:, :], br.partition_broadcast(P)), (b1_sb[:, :], b1),
                             (w2_sb[:, :, :], w2.rearrange("e (c p) d -> p (e c) d", p=P))):
                sp.dma_start(dst, src).then_inc(loaded, 16)

        @block.tensor
        def _(pe):
            side_read.open(pe)
            y_read.open(pe)
            wps_read.open(pe)
            pe.wait_ge(loaded, LOADS * 16)

            def fill_side(kind, n, par):
                if kind is None:
                    return
                if kind == "back":
                    pe.wait_ge(acc_ready.sem, acc_ready.take())
                if kind == "tokens" and n == 0:
                    pe.wait_ge(xn_ready.sem, xn_ready.take())
                if kind == "router":
                    pe.wait_ge(xs_ready.sem, xs_ready.take())
                if kind == "weights":
                    pe.wait_ge(wt_ready.sem, wt_ready.take())
                pe.wait_ge(side_read.sem, side_read.take())
                if kind == "back":
                    for j in range(TILES // 2):
                        last = nc.tensor.transpose(side[:, j * P:(j + 1) * P], acc[:, j * P:(j + 1) * P], ident[:, :])
                elif kind == "tokens":
                    for j in range(TILES // 2):
                        last = nc.tensor.transpose(side[:, j * P:(j + 1) * P], xn[:, n * TILES // 2 + j, :], ident[:, :])
                elif kind == "router":
                    for t in range(TILES):
                        out = side[:, t * EXPERTS:(t + 1) * EXPERTS]
                        nc.tensor.matmul(out, xs[par][:, t * P:(t + 1) * P], wrh[:, :], start=True, stop=False)
                        last = nc.tensor.matmul(out, xs[par][0:D, t * P:(t + 1) * P], wrl[0:D, :], start=False, stop=True)
                else:
                    last = nc.tensor.transpose(side[:, 0:P], wt[:, :, :].rearrange("p k i -> p (k i)"), ident[:, :])
                last.then_inc(side_done.sem, 1)

            def layer1(ht, par):
                for j in range(2):
                    cols = slice(j * HALF, (j + 1) * HALF)
                    nc.tensor.matmul(hps[ht % 2][:, cols], w1h[:, ht, :], xs[par][:, cols], start=True, stop=False)
                    last = nc.tensor.matmul(hps[ht % 2][:, cols], w1l[0:D, ht, :], xs[par][0:D, cols],
                                            start=False, stop=True)
                last.then_inc(h_done.sem, 1)

            def layer2(ht, par):
                expert, chunk = divmod(ht, HC)
                if chunk == 0:
                    if expert == 0:
                        pe.wait_ge(wts_ready.sem, wts_ready.take())
                    pe.wait_ge(wps_read.sem, wps_read.take())
                    for t in range(TILES):
                        half, j = divmod(t, TILES // 2)
                        last = nc.tensor.matmul(wps[half * D:(half + 1) * D, j * P:(j + 1) * P],
                                                select[:, t * EXPERTS + expert, :], wts[par][:, :], start=True,
                                                stop=True)
                    last.then_inc(wps_done.sem, 1)
                if chunk == HC - 1:
                    pe.wait_ge(y_read.sem, y_read.take())
                pe.wait_ge(gelu_done.sem, gelu_done.take())
                for half in range(2):
                    last = nc.tensor.matmul(yps[expert % 2][half * D:(half + 1) * D, :], w2_sb[:, ht, :],
                                            hid[ht % 2][:, half * HALF:(half + 1) * HALF], start=(chunk == 0),
                                            stop=(chunk == HC - 1), skip_group_check=True)
                if chunk == HC - 1:
                    last.then_inc(y_done.sem, 1)

            for ht in range(HT):
                expert, chunk = divmod(ht, HC)
                last = nc.tensor.matmul(hps[0][:, ht:ht + 1], w1f[0:D, expert, chunk * P:(chunk + 1) * P],
                                        lnb_sb[0:D, expert:expert + 1], start=True, stop=True)
            last.then_inc(folded_v.sem, 1)
            pe.wait_ge(w_ready.sem, w_ready.take())

            def settle_all():
                for q in (xn_ready, w_ready, gelu_done, y_read, wps_read, xs_ready, side_read, wt_ready, wts_ready, acc_ready):
                    q.settle(pe)

            for kind, n in SIDE.values():
                if kind != "back":
                    fill_side(kind, n, 0)

            def body(b, par, prev=True, next=True, settle=True):
                for ht in range(HT + 1):
                    if ht < HT:
                        layer1(ht, par)
                    fill_side(*due(ht, prev, next), 1 - par)
                    if ht:
                        layer2(ht - 1, par)
                if settle:
                    settle_all()
            turns(pe, body)
            fill_side("back", 0, 0)

        @block.scalar
        def _(act):
            act.wait_ge(b1_ready.sem, b1_ready.take())

            def body(b, par, prev=True, next=True, settle=True):
                for ht in range(HT):
                    act.wait_ge(h_done.sem, h_done.take())
                    nc.scalar.activation(hid[ht % 2][:, :], hps[ht % 2][:, :], ACT.Gelu, bias=b1_sb[:, ht:ht + 1],
                                         scale=1.0 / WS).then_inc(gelu_done.sem, 1)
                    if ht % HC == HC - 1:
                        e = ht // HC
                        act.wait_ge(wps_done.sem, wps_done.take())
                        nc.scalar.activation(wb[e % 2][:, :], wps[:, :], ACT.Copy).then_inc(wps_read.sem, 1)
                        act.drain().then_inc(wb_ready.sem, 1)
                if settle:
                    h_done.settle(act)
                    wps_done.settle(act)
            turns(act, body)

        @block.gpsimd
        def _(pool):
            pool.memset(euler[:, :], float(np.e))
            pool.iota(iota_i[:, :], pattern=[[1, EXPERTS]], base=0, channel_multiplier=0).then_inc(consts.sem, 1)

            def step(ins):
                ins.then_inc(pool_done.sem, 1)
                pool.wait_ge(pool_done.sem, pool_done.take())

            def stage(b):
                x = xn[:, :, 0:D]
                for src, stat, op in ((batch(h_sb, b), mean, ALU.subtract), (x, r1, ALU.mult), (x, r2, ALU.mult)):
                    step(nc.gpsimd.tensor_tensor(x, src, wide(batch(stat, b), D), op))
                nc.gpsimd.tensor_copy(xn[:, :, D:2 * D], x).then_inc(xn_ready.sem, 1)

            def exp_gap():
                pool.wait_ge(gap_ready.sem, gap_ready.take())
                nc.gpsimd.tensor_tensor(e2[:, :], euler[:, :], gap[:, :], ALU.pow).then_inc(e2_ready.sem, 1)

            def settle_all():
                for q in (gap_ready, term_done, pool_done):
                    q.settle(pool)

            stage(0)
            exp_gap()

            def body(b, par, prev=True, next=True, settle=True):
                if next:
                    stage(b + 1)
                pool.wait_ge(term_done.sem, term_done.take())
                for e in range(1, EXPERTS):
                    if e == 3 and next:
                        exp_gap()
                    pool.wait_ge(term_done.sem, term_done.take())
                    step(nc.gpsimd.tensor_tensor(acc[:, :], acc[:, :], term[e % 2][:, :], ALU.add))
                    pool.sem_inc(term_free.sem, 1)
                pool.sem_inc(acc_ready.sem, 1)
                if settle:
                    settle_all()
            turns(pool, body)

        @block.vector
        def _(dve):
            term_free.open(dve)

            def link(ins):
                ins.then_inc(chain.sem, 1)
                dve.wait_ge(chain.sem, chain.take())

            def read_side(kind, n, par, b):
                if kind is None:
                    return
                dve.wait_ge(side_done.sem, side_done.take())
                if kind == "back":
                    h = batch(h_sb, b).rearrange("p (g j) d -> p g j d", g=2)
                    nc.vector.tensor_tensor(h, h, side[:, :].rearrange("p (j g d) -> p g j d", g=2, d=D),
                                            ALU.add).then_inc(side_read.sem, 1)
                elif kind == "tokens":
                    x = xs[par][:, n * HALF:(n + 1) * HALF]
                    link(nc.vector.tensor_copy(x, side[:, :]))
                    nc.vector.tensor_tensor(x[D:P], side[D:P, :], x[D:P], ALU.subtract).then_inc(side_read.sem, 1)
                    if n == 1:
                        dve.drain().then_inc(xs_ready.sem, 1)
                elif kind == "router":
                    route_logits(b)
                else:
                    link(nc.vector.tensor_copy(wts[par][:, :], side[:, 0:P]))
                    nc.vector.tensor_tensor(wts[par][TE:P, :], side[TE:P, 0:P], wts[par][TE:P, :],
                                            ALU.subtract).then_inc(side_read.sem, 1)
                    dve.drain().then_inc(wts_ready.sem, 1)

            def route_logits(b):
                nc.vector.tensor_tensor(logits[:, :, :], side[:, 0:TE].rearrange("p (t e) -> p t e", e=EXPERTS),
                                        wide(batch(s2, b), EXPERTS), ALU.mult).then_inc(side_read.sem, 1)
                dve.drain()
                link(nc.vector.scalar_tensor_tensor(logits[:, :, :], logits[:, :, :], 1.0 / WS,
                                                    shared(br_sb[:, :], TILES), ALU.mult, ALU.add))
                for t in range(TILES):
                    last = nc.vector.max(top[:, t, :], logits[:, t, :])
                link(last)
                nc.vector.tensor_tensor(gap[:, :], top[:, :, 1], top[:, :, 0], ALU.subtract).then_inc(gap_ready.sem, 1)
                for t in range(TILES):
                    last = nc.vector.max_index(top_i[:, t, :], top[:, t, :], logits[:, t, :])
                link(last)
                link(nc.vector.tensor_copy(top_f[:, :, :], top_i[:, :, 0:2].rearrange("p t k -> p k t")))
                for k in range(2):
                    last = nc.vector.tensor_tensor(pick[:, k], shared(iota[:, :], TILES), wide(top_f[:, k, :], EXPERTS),
                                                   ALU.is_equal)
                link(last)

            def route_weights():
                dve.wait_ge(e2_ready.sem, e2_ready.take())
                link(nc.vector.tensor_scalar(den[:, :], e2[:, :], 1.0, None, ALU.add))
                link(nc.vector.reciprocal(tw[:, 0, :], den[:, :]))
                link(nc.vector.tensor_tensor(tw[:, 1, :], e2[:, :], tw[:, 0, :], ALU.mult))
                for k in range(2):
                    last = nc.vector.tensor_tensor(pick[:, k], pick[:, k], wide(tw[:, k, :], EXPERTS), ALU.mult)
                link(last)
                for k in range(2):
                    last = nc.vector.tensor_tensor(wt[:, k, :].rearrange("p (t e) -> p t e", e=EXPERTS), pick[:, 0],
                                                   pick[:, 1], ALU.add)
                last.then_inc(wt_ready.sem, 1)

            dve.wait_ge(loaded, LOADS * 16)
            dve.wait_ge(consts.sem, consts.take())
            link(nc.vector.tensor_copy(iota[:, :], iota_i[:, :]))
            dve.wait_ge(folded_v.sem, folded_v.take())
            nc.vector.tensor_tensor(b1_sb[:, :], b1_sb[:, :], hps[0][:, 0:HT], ALU.add).then_inc(b1_ready.sem, 1)
            for e in range(EXPERTS):
                last = nc.vector.tensor_scalar(w1f[:, e, :], w1f[:, e, :], lng_sb[:, e:e + 1], WS, ALU.mult, ALU.mult)
            link(last)
            link(nc.vector.tensor_scalar(wrf[:, :], wrf[:, :], WS, None, ALU.mult))
            for rows in (slice(0, TE), slice(TE, P)):
                nc.vector.tensor_copy(select[rows, :, :], wide(ident[rows, rows], D))
            w1_flat = w1f[:, :, :].rearrange("p e h -> p (e h)")
            flat = lambda w: w[:, :, :].rearrange("p t h -> p (t h)")
            link(nc.vector.tensor_copy(flat(w1h), w1_flat))
            nc.vector.tensor_tensor(flat(w1l), w1_flat, flat(w1h), ALU.subtract)
            link(nc.vector.tensor_copy(wrh[:, :], wrf[:, :]))
            nc.vector.tensor_tensor(wrl[:, :], wrf[:, :], wrh[:, :], ALU.subtract).then_inc(w_ready.sem, 1)
            for kind, n in SIDE.values():
                if kind != "back":
                    read_side(kind, n, 0, 0)
                if kind == "router":
                    route_weights()

            def settle_all():
                for q in (consts, folded_v, side_done, e2_ready, wb_ready, y_done, term_free, chain):
                    q.settle(dve)
            settle_all()

            def body(b, par, prev=True, next=True, settle=True):
                for ht in range(1, HT + 1):
                    kind, n = due(ht, prev, next)
                    read_side(kind, n, 1 - par, b - 1 if kind == "back" else b + 1)
                    if ht == 10 and next:
                        route_weights()
                    if ht % HC == 0:
                        e = ht // HC - 1
                        dve.wait_ge(wb_ready.sem, wb_ready.take())
                        dve.wait_ge(y_done.sem, y_done.take())
                        if e:
                            dve.wait_ge(term_free.sem, term_free.take())
                        nc.vector.scalar_tensor_tensor(term[e % 2][:, :] if e else acc[:, :], yps[e % 2][:, :],
                                                       b2_sb[:, e:e + 1], wb[e % 2][:, :], ALU.add,
                                                       ALU.mult).then_inc(term_done.sem, 1)
                        dve.drain().then_inc(y_read.sem, 1)
                if settle:
                    settle_all()
            turns(dve, body)
            read_side("back", 0, 0, NB - 1)


S1 = 128


def emit_attention1(nc, h_sb, stats, ident, wuv, buv, gam, bet, wo, bo):
    mean, r1, r2 = (stats[:, i, :] for i in (0, 2, 3))
    with ExitStack() as ctx:
        sb = lambda name, shape, dt=F32: ctx.enter_context(nc.sbuf_tensor(name, shape, dt))
        w_sb = sb("wuv", [D + 1, 3 * S1])
        gb = sb("gb", [P, 4])
        wo_sb = sb("wo", [P, D])
        bo_sb = sb("bo", [P, D])
        xn = sb("xn1", [P, TILES, D])
        xT = sb("xT1", [D + 1, T])
        base = sb("base", [P, T])
        q_sb, k_sb, u_sb, v_sb = ([sb(f"{n}1_{i}", [P, T]) for i in range(2)] for n in "qkuv")
        a_sb = [sb(f"a1_{i}", [P, T]) for i in range(2)]
        gated = sb("a1_gated", [P, T])
        proj = sb("a1_proj", [P, TILES, D])
        sps = [ctx.enter_context(nc.psum_tensor(f"sps{i}", [P, T], F32)) for i in range(2)]
        ops_ = ctx.enter_context(nc.psum_tensor("ops", [P, T], F32))
        pps = ctx.enter_context(nc.psum_tensor("pps", [P, T], F32))

        s = lambda name, credits=0: Signal(ctx, nc, name, credits)
        LOADS = 6
        loaded = ctx.enter_context(nc.semaphore("loaded1"))
        scaled = s("scaled1")
        xn_ready = s("xn_ready1")
        xn_free = s("xn_free1", 1)
        p_done = s("p_done1")
        proj_done = s("proj_done1")
        p_free = s("p_free1", 1)
        base_done = s("base_done1")
        qk_ready = s("qk_ready1")
        s_done = s("s_done1")
        relu_done = s("relu_done1")
        a_ready = s("a_ready1")
        o_done = s("o_done1")
        gated_done = s("gated_done1", 1)
        chain = s("dve_chain1")
        pool_done = s("pool_done1")
        block = ctx.enter_context(nc.Block())

        def turns(eng, body):
            body(None, 1, False, True)
            body(0, 0, False, True)
            with eng.Fori(0, (NB - 2) // 2) as i:
                body(i * 2 + 1, 1, True, True, settle=False)
                body(i * 2 + 2, 0, True, True)
            body(NB - 1, 1, True, False)

        @block.sync
        def _(sp):
            for dst, src in ((w_sb[0:D, :], wuv), (w_sb[D:D + 1, :], buv.unsqueeze(0)), (gb[:, 0:2], gam),
                             (gb[:, 2:4], bet), (wo_sb[:, :], wo), (bo_sb[:, :], bo.partition_broadcast(P))):
                sp.dma_start(dst, src).then_inc(loaded, 16)

        @block.gpsimd
        def _(pool):
            xn_free.open(pool)

            def body(b, par, has_prev, has_next, settle=True):
                if has_next:
                    nxt = 0 if b is None else b + 1
                    pool.wait_ge(xn_free.sem, xn_free.take())
                    x = xn[:, :, :]
                    for n, (src, stat, op) in enumerate(((batch(h_sb, nxt), mean, ALU.subtract), (x, r1, ALU.mult),
                                                         (x, r2, ALU.mult))):
                        ins = nc.gpsimd.tensor_tensor(x, src, wide(batch(stat, nxt), D), op)
                        if n < 2:
                            ins.then_inc(pool_done.sem, 1)
                            pool.wait_ge(pool_done.sem, pool_done.take())
                    ins.then_inc(xn_ready.sem, 1)
                if settle:
                    for q in (xn_free, pool_done):
                        q.settle(pool)
            turns(pool, body)

        @block.tensor
        def _(pe):
            p_free.open(pe)
            gated_done.open(pe)
            pe.wait_ge(loaded, LOADS * 16)
            pe.wait_ge(scaled.sem, scaled.take())

            def scores(par, m):
                if m == 0:
                    pe.wait_ge(qk_ready.sem, qk_ready.take())
                for j in range(2):
                    cols = slice(j * HALF, (j + 1) * HALF)
                    last = nc.tensor.matmul(sps[m % 2][:, cols], k_sb[par][:, m * P:(m + 1) * P], q_sb[par][:, cols],
                                            start=True, stop=True)
                last.then_inc(s_done.sem, 1)

            def attend(par, m):
                pe.wait_ge(a_ready.sem, a_ready.take())
                if m == 0:
                    pe.wait_ge(gated_done.sem, gated_done.take())
                    pe.wait_ge(p_free.sem, p_free.taken + 1)
                for j in range(2):
                    cols = slice(j * HALF, (j + 1) * HALF)
                    last = nc.tensor.matmul(ops_[:, cols], v_sb[par][:, m * P:(m + 1) * P], a_sb[m % 2][:, cols],
                                            start=(m == 0), stop=(m == TILES - 1), skip_group_check=True)
                if m == TILES - 1:
                    last.then_inc(o_done.sem, 1)

            def operand(kind):
                if kind == "xT":
                    pe.wait_ge(xn_ready.sem, xn_ready.take())
                pe.wait_ge(p_free.sem, p_free.take())
                if kind == "xT":
                    for t in range(TILES):
                        last = nc.tensor.transpose(pps[0:D, t * P:(t + 1) * P], xn[:, t, :], ident[:, :])
                elif kind == "v":
                    for t in range(TILES):
                        last = nc.tensor.matmul(pps[:, t * P:(t + 1) * P], xT[:, t * P:(t + 1) * P],
                                                w_sb[:, S1:2 * S1], start=True, stop=True)
                else:
                    col = 0 if kind == "u" else 2 * S1
                    for j in range(2):
                        last = nc.tensor.matmul(pps[:, j * HALF:(j + 1) * HALF], w_sb[:, col:col + S1],
                                                xT[:, j * HALF:(j + 1) * HALF], start=True, stop=True)
                        if kind == "base" and j == 0:
                            last.then_inc(xn_free.sem, 1)
                last.then_inc(p_done.sem, 1)

            def project():
                pe.wait_ge(p_free.sem, p_free.take())
                for t in range(TILES):
                    last = nc.tensor.matmul(pps[:, t * D:(t + 1) * D], gated[:, t * P:(t + 1) * P], wo_sb[:, :],
                                            start=True, stop=True)
                last.then_inc(proj_done.sem, 1)

            def body(b, par, has_prev, has_next, settle=True):
                for m in range(TILES):
                    if b is not None:
                        scores(par, m)
                        if m:
                            attend(par, m - 1)
                        elif has_prev:
                            attend(1 - par, TILES - 1)
                    if has_next and 1 <= m <= 4:
                        operand(("xT", "base", "u", "v")[m - 1])
                    if m == 5 and has_prev:
                        project()
                if b is not None and not has_next:
                    attend(par, TILES - 1)
                    pe.wait_ge(gated_done.sem, gated_done.take())
                    project()
                if settle:
                    for q in (scaled, qk_ready, a_ready, gated_done, p_free, xn_ready):
                        q.settle(pe)

            turns(pe, body)

        @block.vector
        def _(dve):
            dve.wait_ge(loaded, LOADS * 16)
            nc.vector.tensor_scalar(gb[:, 0:4:2], gb[:, 0:4:2], S1 ** -0.5, None, ALU.mult)
            nc.vector.memset(xT[D:D + 1, :], 1.0).then_inc(scaled.sem, 1)

            def link(ins):
                ins.then_inc(chain.sem, 1)
                dve.wait_ge(chain.sem, chain.take())

            def gate_output(par):
                dve.wait_ge(o_done.sem, o_done.take())
                nc.vector.tensor_tensor(gated[:, :], ops_[:, :], u_sb[par][:, :], ALU.mult).then_inc(gated_done.sem, 1)

            def add_projection(b):
                dve.wait_ge(proj_done.sem, proj_done.take())
                link(nc.vector.tensor_tensor(proj[:, :, :], pps[:, 0:HALF].rearrange("p (t d) -> p t d", d=D),
                                             shared(bo_sb[:, :], TILES), ALU.add))
                nc.vector.tensor_tensor(batch(h_sb, b), batch(h_sb, b), proj[:, :, :], ALU.add).then_inc(p_free.sem, 1)

            def body(b, par, has_prev, has_next, settle=True):
                for m in range(TILES):
                    if b is not None:
                        dve.wait_ge(s_done.sem, s_done.take())
                        nc.vector.tensor_scalar(a_sb[m % 2][:, :], sps[m % 2][:, :], 0.0, None,
                                                ALU.max).then_inc(relu_done.sem, 1)
                    if m == 0 and has_prev:
                        gate_output(1 - par)
                    if m == 4 and has_next:
                        dve.wait_ge(base_done.sem, base_done.take())
                        nc.vector.tensor_scalar(q_sb[1 - par][:, :], base[:, :], gb[:, 0:1], gb[:, 2:3],
                                                ALU.mult, ALU.add)
                        nc.vector.tensor_scalar(k_sb[1 - par][:, :], base[:, :], gb[:, 1:2], gb[:, 3:4],
                                                ALU.mult, ALU.add).then_inc(qk_ready.sem, 1)
                    if m == 6 and has_prev:
                        add_projection(b - 1)
                if b is not None and not has_next:
                    gate_output(par)
                    add_projection(b)
                if settle:
                    for q in (chain, o_done, proj_done, s_done, base_done):
                        q.settle(dve)
            turns(dve, body)

        @block.scalar
        def _(act):
            act.wait_ge(loaded, LOADS * 16)

            def body(b, par, has_prev, has_next, settle=True):
                for m in range(TILES):
                    if has_next and 1 <= m <= 4:
                        act.wait_ge(p_done.sem, p_done.take())
                        if m == 1:
                            nc.scalar.activation(xT[0:D, :], pps[0:D, :], ACT.Copy).then_inc(p_free.sem, 1)
                        elif m == 2:
                            nc.scalar.activation(base[:, :], pps[:, :], ACT.Silu).then_inc(p_free.sem, 1)
                            act.drain().then_inc(base_done.sem, 1)
                        else:
                            nc.scalar.activation((u_sb if m == 3 else v_sb)[1 - par][:, :], pps[:, :],
                                                 ACT.Silu).then_inc(p_free.sem, 1)
                    if b is not None:
                        act.wait_ge(relu_done.sem, relu_done.take())
                        nc.scalar.activation(a_sb[m % 2][:, :], a_sb[m % 2][:, :],
                                             ACT.Square).then_inc(a_ready.sem, 1)
                if settle:
                    for q in (p_done, relu_done):
                        q.settle(act)
            turns(act, body)


HID1 = 128
ROW_W2, ROW_B2, ROW_B1 = HID1, HID1 + D, HID1 + 2 * D
ROW = HID1 + 2 * D + 1
CAPACITY = float(-(-NB * T * 5 // (4 * EXPERTS)))


def emit_routing(nc, h_sb, stats, ident, y_all, wr, br, route_i, route_w):
    mean, r1 = stats[:, 0, :], stats[:, 2, :]
    CH = 4
    n, nb = NT // CH, NB // CH
    with ExitStack() as ctx:
        sb = lambda name, shape, dt=F32: ctx.enter_context(nc.sbuf_tensor(name, shape, dt))
        ysum = sb("ysum", [P, NB, D])
        token_share = sb("token_share", [P, 1])
        ones = sb("ones", [NB, P])
        row_i = sb("row_i", [P, 1], I32)
        row_f = sb("row_f", [P, 1])
        wr_sb = sb("r_wr", [D, EXPERTS])
        br_sb = sb("r_br", [NB, EXPERTS])
        tokens_mean = sb("tokens_mean", [D, NB])
        logits, exps, probs, scale = (sb(f"r_{x}", [NB, EXPERTS]) for x in ("logits", "exps", "probs", "scale"))
        top = sb("r_top", [NB, 8])
        top_i = sb("r_top_i", [NB, 8], U32)
        nmax, total, gap, e2, den = (sb(f"r_{x}", [NB, 1]) for x in ("nmax", "total", "gap", "e2", "den"))
        four = sb("r_four", [NB, 4])
        four_diag = sb("r_four_diag", [NB, 4, NB])
        rows = sb("r_rows", [P, NB, 2])
        ps = [ctx.enter_context(nc.psum_tensor(f"r_ps{i}", [P, HALF], F32)) for i in range(4)]
        sem = lambda name: ctx.enter_context(nc.semaphore("r_" + name))
        loaded, consts, centred, scaled, summed, means_done, means_ready, logits_done, shifted, exped, \
            probs_ready, loads_done, gap_ready, e2_ready, four_ready, four_done, chain = (
                sem(x) for x in ("loaded", "consts", "centred", "scaled", "summed", "means_done", "means_ready",
                                 "logits_done", "shifted", "exped", "probs_ready", "loads_done", "gap_ready",
                                 "e2_ready", "four_ready", "four_done", "chain"))
        block = ctx.enter_context(nc.Block())
        part = lambda t, c: t[:, c * n:(c + 1) * n]

        @block.sync
        def _(sp):
            sp.dma_start(wr_sb[:, :], wr).then_inc(loaded, 16)
            sp.dma_start(br_sb[:, :], br.partition_broadcast(NB)).then_inc(loaded, 16)

        @block.gpsimd
        def _(pool):
            pool.memset(token_share[:, :], 1.0 / T)
            pool.memset(ones[:, :], 1.0)
            pool.iota(row_i[:, :], pattern=[[0, 1]], base=0, channel_multiplier=1).then_inc(consts, 1)
            for c in range(CH):
                pool.wait_ge(centred, c + 1)
                nc.gpsimd.tensor_tensor(part(y_all, c), part(y_all, c), wide(part(r1, c), D), ALU.mult).then_inc(scaled, 1)

        @block.tensor
        def _(pe):
            pe.wait_ge(consts, 1)
            pe.wait_ge(loaded, 32)
            for b in range(NB):
                if b % nb == 0:
                    pe.wait_ge(summed, b // nb + 1)
                last = nc.tensor.matmul(ps[0][0:D, b:b + 1], ysum[:, b, :], token_share[:, :], start=True, stop=True)
            last.then_inc(means_done, 1)
            pe.wait_ge(means_ready, 1)
            nc.tensor.matmul(ps[1][0:NB, 0:EXPERTS], tokens_mean[:, :], wr_sb[:, :], start=True,
                             stop=True).then_inc(logits_done, 1)
            pe.wait_ge(probs_ready, 1)
            nc.tensor.matmul(ps[2][0:NB, 0:EXPERTS], ones[:, 0:NB], probs[:, :], start=True,
                             stop=True).then_inc(loads_done, 1)
            pe.wait_ge(four_ready, 1)
            nc.tensor.matmul(ps[3][:, 0:4 * NB], ones[:, :], four_diag[:, :, :].rearrange("p k b -> p (k b)"),
                             start=True, stop=True).then_inc(four_done, 1)

        @block.scalar
        def _(act):
            for i in range(2):
                act.wait_ge(shifted, i + 1)
                nc.scalar.activation(exps[:, :], logits[:, :], ACT.Exp, bias=nmax[:, :], scale=1.0,
                                     accum_out=total[:, :])
                act.drain().then_inc(exped, 1)
            act.wait_ge(gap_ready, 1)
            nc.scalar.activation(e2[:, :], gap[:, :], ACT.Exp).then_inc(e2_ready, 1)

        @block.vector
        def _(dve):
            links = [0]

            def link(ins):
                links[0] += 1
                ins.then_inc(chain, 1)
                dve.wait_ge(chain, links[0])

            def softmax(i):
                nc.vector.tensor_reduce(nmax[:, :], logits[:, :], axis=AX.X, op=ALU.max, negate=True).then_inc(shifted, 1)
                dve.wait_ge(exped, i + 1)
                link(nc.vector.reciprocal(den[:, :], total[:, :]))
                return nc.vector.tensor_scalar(probs[:, :], exps[:, :], den[:, :], None, ALU.mult)

            def centre(c):
                nc.vector.tensor_tensor(part(y_all, c), part(h_sb, c), wide(part(mean, c), D),
                                        ALU.subtract).then_inc(centred, 1)

            centre(0)
            for c in range(CH):
                if c + 1 < CH:
                    centre(c + 1)
                dve.wait_ge(scaled, c + 1)
                nc.vector.reduce_sum(ysum[:, c * nb:(c + 1) * nb, :],
                                     part(y_all, c).rearrange("p (b t) d -> p b d t", t=TILES), AX.X).then_inc(summed, 1)
            dve.wait_ge(consts, 1)
            dve.wait_ge(loaded, 32)
            nc.vector.tensor_copy(row_f[:, :], row_i[:, :])
            dve.wait_ge(means_done, 1)
            nc.vector.tensor_copy(tokens_mean[:, :], ps[0][0:D, 0:NB]).then_inc(means_ready, 1)
            dve.wait_ge(logits_done, 1)
            link(nc.vector.tensor_tensor(logits[:, :], ps[1][0:NB, 0:EXPERTS], br_sb[:, :], ALU.add))
            softmax(0).then_inc(probs_ready, 1)
            dve.wait_ge(loads_done, 1)
            link(nc.vector.tensor_scalar(scale[:, :], ps[2][0:NB, 0:EXPERTS], float(T), CAPACITY, ALU.mult, ALU.max))
            link(nc.vector.reciprocal(scale[:, :], scale[:, :]))
            link(nc.vector.scalar_tensor_tensor(logits[:, :], scale[:, :], CAPACITY, probs[:, :], ALU.mult, ALU.mult))
            link(softmax(1))
            link(nc.vector.max(top[:, :], probs[:, :]))
            nc.vector.tensor_tensor(gap[:, :], top[:, 1:2], top[:, 0:1], ALU.subtract).then_inc(gap_ready, 1)
            link(nc.vector.max_index(top_i[:, :], top[:, :], probs[:, :]))
            nc.vector.tensor_copy(four[:, 0:2], top_i[:, 0:2])
            dve.wait_ge(e2_ready, 1)
            link(nc.vector.tensor_scalar(den[:, :], e2[:, :], 1.0, None, ALU.add))
            link(nc.vector.reciprocal(four[:, 2:3], den[:, :]))
            link(nc.vector.tensor_tensor(four[:, 3:4], e2[:, :], four[:, 2:3], ALU.mult))
            nc.vector.tensor_tensor(four_diag[:, :, :], wide(four[:, :], NB), shared(ident[0:NB, 0:NB], 4),
                                    ALU.mult).then_inc(four_ready, 1)
            dve.wait_ge(four_done, 1)
            four_all = ps[3][:, 0:4 * NB].rearrange("p (k b) -> p k b", b=NB)
            nc.vector.tensor_copy(route_w[:, :, :], four_all[:, 2:4, :])
            link(nc.vector.tensor_scalar(rows[:, :, :], four_all[:, 0:2, :].rearrange("p k b -> p b k"), float(P),
                                         row_f[:, :], ALU.mult, ALU.add))
            nc.vector.tensor_copy(route_i[:, :, :], rows[:, :, :])


def emit_moe1(nc, h_sb, stats, ident, wr, br, table, gamma, beta, out):
    with ExitStack() as outer:
        keep = lambda name, shape, dt=F32: outer.enter_context(nc.sbuf_tensor(name, shape, dt))
        y_all = keep("y_all", [P, NT, D])
        route_i = keep("route_i", [P, NB, 2], I32)
        route_w = keep("route_w", [P, 2, NB])
        emit_routing(nc, h_sb, stats, ident, y_all, wr, br, route_i, route_w)
        emit_experts(nc, h_sb, ident, y_all, route_i, route_w, table, gamma, beta, out)


def emit_experts(nc, h_sb, ident, y_all, route_i, route_w, table, gamma, beta, out):
    with ExitStack() as ctx:
        sb = lambda name, shape, dt=F32: ctx.enter_context(nc.sbuf_tensor(name, shape, dt))
        two = lambda name, shape, dt=F32: [sb(f"{name}_{i}", shape, dt) for i in range(2)]
        gam_sb = sb("m1_gamma", [P, D])
        bet_sb = sb("m1_beta", [P, D])
        idx = two("m1_idx", [P, 2], I32)
        w_g = two("m1_w", [P, 2, ROW])
        w1s = two("m1_w1s", [P, 2, HID1])
        b1s = two("m1_b1s", [P, 2])
        w2s = two("m1_w2s", [P, 2, D])
        b2w = two("m1_b2w", [P, D])
        b2s = two("m1_b2s", [P, D])
        y_b = two("m1_y", [P, TILES, D])
        yT = two("m1_yT", [P, HALF])
        hid = two("m1_hid", [P, 2 * HALF])
        oT = sb("m1_oT", [P, HALF])
        base = two("m1_base", [P, TILES, D])
        z = two("m1_z", [P, TILES, D])
        sq = sb("m1_sq", [P, TILES, D])
        zm = sb("m1_zm", [P, TILES])
        zv = two("m1_zv", [P, TILES])
        rstd = sb("m1_rstd", [P, TILES])
        half = sb("m1_half", [P, TILES])
        yps = [ctx.enter_context(nc.psum_tensor(f"m1_yps{i}", [P, HALF], F32)) for i in range(2)]
        hps = [ctx.enter_context(nc.psum_tensor(f"m1_hps{i}", [P, 2 * HALF], F32)) for i in range(2)]
        oTps = ctx.enter_context(nc.psum_tensor("m1_oTps", [P, HALF], F32))
        xps = ctx.enter_context(nc.psum_tensor("m1_xps", [P, HALF], F32))

        s = lambda name, credits=0: Signal(ctx, nc, "m1_" + name, credits)
        loaded = ctx.enter_context(nc.semaphore("m1_loaded"))
        stored = ctx.enter_context(nc.semaphore("m1_stored"))
        landed = [ctx.enter_context(nc.semaphore(f"m1_landed{i}")) for i in range(2)]
        idx_copied = s("idx_copied")
        y_ready = s("y_ready")
        x_done = s("x_done")
        yT_ready = s("yT_ready")
        w_ready = s("w_ready")
        b2_ready = s("b2_ready")
        base_ready = s("base_ready")
        h_done = s("h_done")
        gelu_done = s("gelu_done")
        oT_done = s("oT_done")
        oT_ready = s("oT_ready")
        out_done = s("out_done")
        centred = s("centred")
        squared = s("squared")
        var_ready = s("var_ready")
        rstd_ready = s("rstd_ready")
        z_ready = s("z_ready")
        h_ready = s("h_ready")
        chain = s("chain")
        pool_done = s("pool_done")
        block = ctx.enter_context(nc.Block())

        def turns(eng, body):
            body(-1, 1, 1, prev=False, this=False)
            body(0, 0, 1, prev=False)
            with eng.Fori(0, NB // 2 - 2) as r:
                body(r * 2 + 1, 1, r + 2, settle=False)
                body(r * 2 + 2, 0, r + 2)
            body(NB - 3, 1, NB // 2)
            body(NB - 2, 0, NB // 2, ahead=False)
            body(NB - 1, 1, None, next=False, ahead=False)
            body(NB, 0, None, this=False, next=False, ahead=False, settle=False)

        @block.sync
        def _(sp):
            sp.dma_start(gam_sb[:, :], gamma.partition_broadcast(P)).then_inc(loaded, 16)
            sp.dma_start(bet_sb[:, :], beta.partition_broadcast(P)).then_inc(loaded, 16)

            def body(i, par, count, prev=True, this=True, next=True, ahead=True, settle=True):
                if prev:
                    sp.wait_ge(h_ready.sem, h_ready.take())
                    sp.dma_start(out[bass.ds(i - 1, 1)].rearrange("b (p t) d -> p (b t) d", t=TILES),
                                 batch(h_sb, i - 1)).then_inc(stored, 16)
                if settle:
                    h_ready.settle(sp)
            turns(sp, body)
            sp.wait_ge(stored, NB * 16)

        @block.gpsimd
        def _(pool):
            pool.memset(half[:, :], -0.5).then_inc(pool_done.sem, 1)
            pool.wait_ge(pool_done.sem, pool_done.take())

            def gather(buf, b):
                nc.gpsimd.tensor_copy(idx[buf][:, :], route_i[:, bass.ds(b, 1), :].rearrange("p b k -> p (b k)")
                                      ).then_inc(idx_copied.sem, 1)
                pool.wait_ge(idx_copied.sem, idx_copied.take())
                for k in range(2):
                    pool.indirect_dma_start(
                        out=w_g[buf][:, k, :], out_offset=None, in_=table[:, :],
                        in_offset=bass.IndirectOffsetOnAxis(ap=idx[buf][:, k:k + 1], axis=0),
                    ).then_inc(landed[buf], 16)

            gather(0, 0)

            def body(i, par, count, prev=True, this=True, next=True, ahead=True, settle=True):
                nxt = 1 - par
                if ahead:
                    gather(par, i + 2)
                if prev:
                    pool.wait_ge(var_ready.sem, var_ready.take())
                    nc.gpsimd.tensor_tensor(rstd[:, :], zv[nxt][:, :], half[:, :], ALU.pow).then_inc(rstd_ready.sem, 1)
                    pool.wait_ge(z_ready.sem, z_ready.take())
                    nc.gpsimd.tensor_tensor(batch(h_sb, i - 1), batch(h_sb, i - 1), z[nxt][:, :, :],
                                            ALU.add).then_inc(h_ready.sem, 1)
                if next:
                    pool.wait_ge(b2_ready.sem, b2_ready.take())
                    nc.gpsimd.tensor_tensor(base[nxt][:, :, :], batch(y_all, i + 1), shared(b2s[nxt][:, :], TILES),
                                            ALU.add).then_inc(base_ready.sem, 1)
                if settle:
                    for q in (idx_copied, var_ready, z_ready, b2_ready, pool_done):
                        q.settle(pool)
            pool.wait_ge(loaded, 32)
            turns(pool, body)

        @block.tensor
        def _(pe):
            def body(i, par, count, prev=True, this=True, next=True, ahead=True, settle=True):
                nxt = 1 - par
                if next:
                    pe.wait_ge(y_ready.sem, y_ready.take())
                    if this:
                        pe.wait_ge(yT_ready.sem, yT_ready.take())
                    for j in range(TILES // 2):
                        last = nc.tensor.transpose(xps[:, j * P:(j + 1) * P],
                                                   y_b[nxt][:, 2 * j:2 * j + 2, :].rearrange("p t d -> p (t d)"),
                                                   ident[:, :])
                    last.then_inc(x_done.sem, 1)
                if this and not next:
                    pe.wait_ge(yT_ready.sem, yT_ready.take())
                for k in range(2):
                    if this:
                        if k == 0:
                            pe.wait_ge(w_ready.sem, w_ready.take())
                        for odd in range(2):
                            rows = slice(odd * D, (odd + 1) * D)
                            last = nc.tensor.matmul(hps[k][:, odd * HALF:(odd + 1) * HALF], w1s[par][rows, k, :],
                                                    yT[par][rows, :], start=True, stop=True)
                        last.then_inc(h_done.sem, 1)
                    if k == 0 and prev:
                        if not this:
                            pe.drain()
                        pe.wait_ge(oT_ready.sem, oT_ready.take())
                        for j in range(TILES // 2):
                            last = nc.tensor.transpose(yps[nxt][:, j * P:(j + 1) * P], oT[:, j * P:(j + 1) * P],
                                                       ident[:, :])
                        last.then_inc(out_done.sem, 1)
                if this:
                    for k in range(2):
                        pe.wait_ge(gelu_done.sem, gelu_done.take())
                        for odd in range(2):
                            last = nc.tensor.matmul(oTps[odd * D:(odd + 1) * D, :], w2s[par][:, k, :],
                                                    hid[k][:, odd * HALF:(odd + 1) * HALF], start=(k == 0), stop=(k == 1),
                                                    skip_group_check=True)
                    last.then_inc(oT_done.sem, 1)
                if settle:
                    for q in (y_ready, yT_ready, w_ready, gelu_done, oT_ready):
                        q.settle(pe)
            turns(pe, body)

        @block.scalar
        def _(act):
            nc.scalar.activation(y_b[0][:, :, :], batch(y_all, 0), ACT.Copy).then_inc(y_ready.sem, 1)

            def body(i, par, count, prev=True, this=True, next=True, ahead=True, settle=True):
                nxt = 1 - par
                if prev:
                    act.wait_ge(oT_done.sem, oT_done.take())
                    nc.scalar.activation(oT[:, :], oTps[:, :], ACT.Copy).then_inc(oT_ready.sem, 1)
                if next:
                    act.wait_ge(x_done.sem, x_done.take())
                    nc.scalar.activation(yT[nxt][:, :], xps[:, :], ACT.Copy).then_inc(yT_ready.sem, 1)
                if this:
                    for k in range(2):
                        act.wait_ge(h_done.sem, h_done.take())
                        nc.scalar.activation(hid[k][:, :], hps[k][:, :], ACT.Gelu,
                                             bias=b1s[par][:, k:k + 1], scale=1.0).then_inc(gelu_done.sem, 1)
                if prev:
                    act.wait_ge(centred.sem, centred.take())
                    nc.scalar.activation(sq[:, :, :], z[nxt][:, :, :], ACT.Square).then_inc(squared.sem, 1)
                if ahead:
                    nc.scalar.activation(y_b[par][:, :, :], batch(y_all, i + 2), ACT.Copy).then_inc(y_ready.sem, 1)
                if settle:
                    for q in (x_done, h_done, centred, oT_done):
                        q.settle(act)
            turns(act, body)

        @block.vector
        def _(dve):
            dve.wait_ge(loaded, 32)

            def link(ins):
                ins.then_inc(chain.sem, 1)
                dve.wait_ge(chain.sem, chain.take())

            def body(i, par, count, prev=True, this=True, next=True, ahead=True, settle=True):
                nxt = 1 - par
                if prev:
                    zb, mb = z[nxt][:, :, :], zm[:, :]
                    dve.wait_ge(base_ready.sem, base_ready.take())
                    dve.wait_ge(out_done.sem, out_done.take())
                    link(nc.vector.tensor_tensor(zb, yps[nxt][:, :].rearrange("p (t d) -> p t d", d=D),
                                                 base[nxt][:, :, :], ALU.add))
                    link(nc.vector.reduce_sum(mb, zb, AX.X))
                    link(nc.vector.tensor_scalar(mb, mb, 1.0 / D, None, ALU.mult))
                    nc.vector.tensor_tensor(zb, zb, wide(mb, D), ALU.subtract).then_inc(centred.sem, 1)
                if next:
                    dve.wait_ge(landed[nxt], count * 32)
                    w = [route_w[:, k, bass.ds(i + 1, 1)] for k in range(2)]
                    nc.vector.tensor_scalar(b2w[nxt][:, :], w_g[nxt][:, 0, ROW_B2:ROW_B2 + D], w[0], None, ALU.mult)
                    nc.vector.tensor_copy(w1s[nxt][:, :, :], w_g[nxt][:, :, 0:HID1])
                    nc.vector.tensor_copy(b1s[nxt][:, :], w_g[nxt][:, :, ROW_B1])
                    for k in range(2):
                        last = nc.vector.tensor_scalar(w2s[nxt][:, k, :], w_g[nxt][:, k, ROW_W2:ROW_W2 + D], w[k], None,
                                                       ALU.mult)
                    last.then_inc(w_ready.sem, 1)
                    link(dve.drain())
                    nc.vector.scalar_tensor_tensor(b2s[nxt][:, :], w_g[nxt][:, 1, ROW_B2:ROW_B2 + D], w[1], b2w[nxt][:, :],
                                                   ALU.mult, ALU.add).then_inc(b2_ready.sem, 1)
                if prev:
                    dve.wait_ge(squared.sem, squared.take())
                    link(nc.vector.reduce_sum(zv[nxt][:, :], sq[:, :, :], AX.X))
                    nc.vector.tensor_scalar(zv[nxt][:, :], zv[nxt][:, :], 1.0 / D, EPS, ALU.mult,
                                            ALU.add).then_inc(var_ready.sem, 1)
                    link(nc.vector.tensor_tensor(zb, zb, shared(gam_sb[:, :], TILES), ALU.mult))
                    dve.wait_ge(rstd_ready.sem, rstd_ready.take())
                    link(nc.vector.tensor_tensor(zb, zb, wide(rstd[:, :], D), ALU.mult))
                    nc.vector.tensor_tensor(zb, zb, shared(bet_sb[:, :], TILES), ALU.add).then_inc(z_ready.sem, 1)
                if settle:
                    for q in (base_ready, out_done, squared, rstd_ready, chain):
                        q.settle(dve)
            turns(dve, body)


INS = {
    "x": ((NB, T), I32), "table": ((VOCAB + 2 * PAD, D), F32), "conv_w": ((KS * D, D), F32), "conv_b": ((D,), F32),
    "qkv_w": ((D, 3 * HEADS * DH), F32), "gate_w": ((D, HEADS * DH), F32), "gate_b": ((P, GROUPS), F32),
    "fin_w": ((HEADS * DH, D), F32), "fin_b": ((D,), F32), "ln_gamma": ((D,), F32), "ln_beta": ((D,), F32),
    "m0_wr": ((D, EXPERTS), F32), "m0_br": ((EXPERTS,), F32), "m0_lng": ((D, EXPERTS), F32),
    "m0_lnb": ((D, EXPERTS), F32), "m0_w1": ((EXPERTS, D, HID0), F32), "m0_b1": ((P, HT), F32),
    "m0_w2": ((EXPERTS, HID0, D), F32), "m0_b2": ((D, EXPERTS), F32),
    "a1_g": ((1,), F32), "a1_wuv": ((D, 3 * S1), F32), "a1_buv": ((3 * S1,), F32), "a1_gamma": ((S1, 2), F32),
    "a1_beta": ((S1, 2), F32), "a1_wo": ((S1, D), F32), "a1_bo": ((D,), F32),
    "m1_wr": ((D, EXPERTS), F32), "m1_br": ((EXPERTS,), F32), "m1_table": ((EXPERTS * P, ROW), F32),
    "m1_gamma": ((D,), F32), "m1_beta": ((D,), F32),
}


def build(nc, a, out):
    with ExitStack() as ctx:
        h_sb = ctx.enter_context(nc.sbuf_tensor("h", [P, NT, D], F32))
        stats = ctx.enter_context(nc.sbuf_tensor("stats", [P, 5, NT], F32))
        ident = ctx.enter_context(nc.sbuf_tensor("ident", [P, P], F32))
        emit_identity(nc, ctx, ident)
        emit_embedding(nc, a["x"], a["table"], a["conv_w"], a["conv_b"], h_sb, ident)
        emit_layernorm(nc, "ln1", h_sb, stats, "norm")
        emit_attention0(nc, h_sb, stats, ident, a["qkv_w"], a["gate_w"], a["gate_b"], a["fin_w"], a["fin_b"],
                        a["ln_gamma"], a["ln_beta"])
        emit_layernorm(nc, "ln2", h_sb, stats, "norm")
        emit_moe0(nc, h_sb, stats, ident, *(a["m0_" + n] for n in ("wr", "br", "lng", "lnb", "w1", "b1", "w2", "b2")))
        emit_layernorm(nc, "ln3", h_sb, stats, "rms", a["a1_g"])
        emit_attention1(nc, h_sb, stats, ident, *(a["a1_" + n] for n in ("wuv", "buv", "gamma", "beta", "wo", "bo")))
        emit_layernorm(nc, "ln4", h_sb, stats, "norm")
        emit_moe1(nc, h_sb, stats, ident, *(a["m1_" + n] for n in ("wr", "br", "table", "gamma", "beta")), out)


def kernel(**inputs):
    import concourse.bacc as bacc
    from concourse.bass_utils import run_bass_kernel_spmd

    g = {k: np.asarray(v) for k, v in inputs.items()}
    arrays = {
        "x": g["x"], "table": np.pad(g["L0_tok_emb"], ((PAD, PAD), (0, 0)), mode="edge"),
        "conv_w": g["L0_tok_W"].transpose(2, 1, 0).reshape(KS * D, D), "conv_b": g["L0_tok_b"],
        "qkv_w": g["L0_attn_W_qkv"].T, "gate_w": g["L0_attn_W_gate"].T, "gate_b": g["L0_attn_b_gate"].reshape(GROUPS, P).T,
        "fin_w": g["L0_attn_W_final"].T, "fin_b": g["L0_attn_b_final"], "ln_gamma": g["L0_attn_ln_gamma"],
        "ln_beta": g["L0_attn_ln_beta"],
        "m0_wr": g["L0_ffn_Wr"], "m0_br": g["L0_ffn_br"], "m0_lng": g["L0_ffn_ln_g"].T, "m0_lnb": g["L0_ffn_ln_b"].T,
        "m0_w1": g["L0_ffn_W1"], "m0_b1": g["L0_ffn_b1"].reshape(HT, P).T, "m0_w2": g["L0_ffn_W2"],
        "m0_b2": g["L0_ffn_b2"].T,
        "a1_g": g["L1_attn_g"].reshape(1), "a1_wuv": g["L1_attn_W_uv"], "a1_buv": g["L1_attn_b_uv"],
        "a1_gamma": g["L1_attn_gamma"].T, "a1_beta": g["L1_attn_beta"].T, "a1_wo": g["L1_attn_W_o"],
        "a1_bo": g["L1_attn_b_o"],
        "m1_wr": g["L1_ffn_Wr"], "m1_br": g["L1_ffn_br"], "m1_gamma": g["L1_ffn_gamma"], "m1_beta": g["L1_ffn_beta"],
        "m1_table": np.concatenate([
            np.tile(g["L1_ffn_W1"], (1, P // D, 1)), g["L1_ffn_W2"],
            np.broadcast_to(g["L1_ffn_b2"][:, None, :], (EXPERTS, P, D)), g["L1_ffn_b1"][:, :, None],
        ], axis=2).reshape(EXPERTS * P, ROW),
    }
    nc = bacc.Bacc("TRN2", target_bir_lowering=False, num_devices=1)
    aps = {n: nc.dram_tensor(f"in_{n}", shape, dt, kind="ExternalInput").ap() for n, (shape, dt) in INS.items()}
    out = nc.dram_tensor("out_h", (NB, T, D), F32, kind="ExternalOutput").ap()
    build(nc, aps, out)
    r = run_bass_kernel_spmd(nc, [{f"in_{n}": np.ascontiguousarray(arrays[n]) for n in INS}], core_ids=[0])
    return r.results[0]["out_h"]
```

```python
from contextlib import ExitStack

import numpy as np

import concourse.bass as bass
from concourse import mybir

F32 = mybir.dt.float32
F16 = mybir.dt.float16
I32 = mybir.dt.int32
U32 = mybir.dt.uint32
ALU = mybir.AluOpType
ACT = mybir.ActivationFunctionType
AX = mybir.AxisListType

P = 128
NB, T, D = 16, 1024, 64
TILES = T // P
NT = NB * TILES
VOCAB, KS = 50257, 9
PAD = KS - 1
HEADS, DH = 8, 32
GROUPS, HG = 2, 4
SCALE0 = DH ** -0.5
EPS = 1e-5
HALF = 512
EXPERTS, HID0 = 8, 256
HC = HID0 // P
HT = EXPERTS * HC
S1 = 128


class Signal:

    def __init__(self, ctx, nc, name, credits=0):
        self.sem = ctx.enter_context(nc.semaphore(name))
        self.credits = credits
        self.taken = 0

    def open(self, eng):
        eng.sem_inc(self.sem, self.credits)

    def take(self, n=1):
        self.taken += n
        return self.taken

    def settle(self, eng):
        if self.taken:
            eng.sem_inc(self.sem, -self.taken)
        self.taken = 0


class Weights:

    def __init__(self, ctx, nc, name):
        self.ctx, self.nc, self.dmas = ctx, nc, []
        self.loaded = ctx.enter_context(nc.semaphore(name + "_loaded"))

    def tensor(self, name, shape, *dmas):
        t = self.ctx.enter_context(self.nc.sbuf_tensor(name, shape, F32))
        self.dmas += [(part(t), src) for part, src in dmas]
        return t

    def start(self, sp):
        for dst, src in self.dmas:
            sp.dma_start(dst, src).then_inc(self.loaded, 16)

    def wait(self, eng):
        eng.wait_ge(self.loaded, 16 * len(self.dmas))


UPPER, LOWER = slice(0, D), slice(D, P)
whole = lambda t: t[:]


def attention0_weights(ctx, nc, wqkv, wgate, bgate, wfin, bfin, gamma, beta):
    w = Weights(ctx, nc, "a0")
    w.w_n = w.tensor("w_qkv", [P, 3 * HEADS * DH], (lambda t: t[LOWER, :], wqkv))
    w.w_y = w.tensor("w_gate", [P, HEADS * DH], (lambda t: t[UPPER, :], wgate))
    w.w_f = w.tensor("w_fin", [P, GROUPS, D], (whole, wfin.rearrange("(g p) o -> p g o", p=P)))
    w.b_g = w.tensor("b_gate", [P, GROUPS], (whole, bgate))
    w.b_f = w.tensor("b_fin", [P, D], (whole, bfin.partition_broadcast(P)))
    w.aff = w.tensor("aff", [P, 2], (lambda t: t[LOWER, 0:1], gamma.unsqueeze(1)),
                     (lambda t: t[LOWER, 1:2], beta.unsqueeze(1)))
    return w


def moe0_weights(ctx, nc, wr, br, lng, lnb, w1, b1, w2, b2):
    w = Weights(ctx, nc, "m0")
    twice = lambda src: [((lambda t, half=half: t[half]), src) for half in (UPPER, LOWER)]
    w.w1 = w.tensor("w1f", [P, EXPERTS, HID0], *twice(w1.rearrange("e d h -> d e h")))
    w.lng = w.tensor("lng", [P, EXPERTS], *twice(lng))
    w.lnb = w.tensor("lnb", [P, EXPERTS], *twice(lnb))
    w.wr = w.tensor("wrf", [P, EXPERTS], *twice(wr))
    w.b2 = w.tensor("b2", [P, EXPERTS], *twice(b2))
    w.br = w.tensor("br", [P, EXPERTS], (whole, br.partition_broadcast(P)))
    w.b1 = w.tensor("b1", [P, HT], (whole, b1))
    w.w2 = w.tensor("w2", [P, HT, D], (whole, w2.rearrange("e (c p) d -> p (e c) d", p=P)))
    return w


def attention1_weights(ctx, nc, wuv, buv, gam, bet, wo, bo):
    w = Weights(ctx, nc, "a1")
    w.uv = w.tensor("wuv", [D + 1, 3 * S1], (lambda t: t[0:D, :], wuv), (lambda t: t[D:D + 1, :], buv.unsqueeze(0)))
    w.gb = w.tensor("gb", [P, 4], (lambda t: t[:, 0:2], gam), (lambda t: t[:, 2:4], bet))
    w.wo = w.tensor("wo", [P, D], (whole, wo))
    w.bo = w.tensor("bo", [P, D], (whole, bo.partition_broadcast(P)))
    return w


def moe1_weights(ctx, nc, wr, br, gamma, beta):
    w = Weights(ctx, nc, "m1")
    w.wr = w.tensor("m1_wr", [D, EXPERTS], (whole, wr))
    w.br = w.tensor("m1_br", [NB, EXPERTS], (whole, br.partition_broadcast(NB)))
    w.gamma = w.tensor("m1_gamma", [P, D], (whole, gamma.partition_broadcast(P)))
    w.beta = w.tensor("m1_beta", [P, D], (whole, beta.partition_broadcast(P)))
    return w


def batch(tensor, b):
    return tensor[:, bass.ds(b * TILES, TILES)]


def wide(ap, n):
    return ap.unsqueeze(2).to_broadcast([ap.shape[0], ap.shape[1], n])


def shared(ap, n):
    return ap.unsqueeze(1).to_broadcast([ap.shape[0], n, ap.shape[1]])


def emit_identity(nc, ctx, ident):
    with nc.semaphore("ident_zero") as zeroed, nc.Block() as block:
        @block.gpsimd
        def _(pool):
            pool.memset(ident[:, :], 0.0).then_inc(zeroed, 1)
            pool.wait_ge(zeroed, 1)
            pool.affine_select(out=ident[:, :], in_=ident[:, :], compare_op=ALU.not_equal, fill=1.0,
                               base=0, pattern=[[-1, P]], channel_multiplier=1)


def emit_embedding(nc, x, table, w, bias, h_sb, stats, ident, later):
    mean, var = stats[:, 0, :], stats[:, 1, :]
    WIN = KS * D
    CHUNKS = 5
    starts = [0, 128, 256, 384, WIN - P]
    with ExitStack() as ctx:
        sb = lambda name, shape, dt=F32: ctx.enter_context(nc.sbuf_tensor(name, shape, dt))
        xi = sb("xi", [P, NT], I32)
        rows = sb("rows", [P, NT], I32)
        idx = sb("idx", [P, 2, TILES], I32)
        win = sb("win", [P, TILES, WIN])
        winT = [sb(f"winT{i}", [P, CHUNKS, T]) for i in range(2)]
        w_sb = sb("conv_w", [P, CHUNKS, D])
        b_col = sb("conv_b", [P, 1])
        cT = sb("convT", [P, HALF])
        centred = sb("e_centred", [P, TILES, D])
        psT = [ctx.enter_context(nc.psum_tensor(f"psT{i}", [P, 2 * HALF], F32)) for i in range(2)]
        psC = ctx.enter_context(nc.psum_tensor("psC", [P, HALF], F32))
        psO = ctx.enter_context(nc.psum_tensor("psO", [P, HALF], F32))
        s = lambda name, credits=0: Signal(ctx, nc, name, credits)
        x_loaded = ctx.enter_context(nc.semaphore("x_loaded"))
        w_loaded = s("w_loaded")
        b_loaded = s("b_loaded")
        clipped = ctx.enter_context(nc.semaphore("clipped"))
        rows_ready = ctx.enter_context(nc.semaphore("rows_ready"))
        idx_copied = s("idx_copied")
        landed = [ctx.enter_context(nc.semaphore(f"win_landed{t}")) for t in range(TILES)]
        win_free = s("win_free", TILES)
        t_done = [s("t_done_a"), s("t_done_v")]
        t_read = [s("t_read_a", 1), s("t_read_v", 1)]
        conv_done = s("conv_done")
        cT_ready = s("cT_ready")
        out_done = s("out_done")
        out_read = s("out_read", 1)
        e_chain = s("e_chain")
        centred_done = s("centred_done_e")
        squared = s("squared_e")
        block = ctx.enter_context(nc.Block())

        def turns(eng, body):
            body(0, 0, prev=False)
            with eng.Fori(0, (NB - 2) // 2) as r:
                body(r * 2 + 1, 1, settle=False)
                body(r * 2 + 2, 0)
            body(NB - 1, 1)

        @block.sync
        def _(sp):
            sp.dma_start(xi[:, :].rearrange("p (b t) -> p b t", t=TILES),
                         x.rearrange("b (p t) -> p b t", t=TILES)).then_inc(x_loaded, 16)
            sp.dma_start(w_sb[:, 0:4, :], w[0:4 * P, :].rearrange("(c p) o -> p c o", p=P)).then_inc(w_loaded.sem, 16)
            sp.dma_start(w_sb[D:P, 4, :], w[4 * P:WIN, :]).then_inc(w_loaded.sem, 16)
            for half in (slice(0, D), slice(D, P)):
                sp.dma_start(b_col[half, :], bias.unsqueeze(1)).then_inc(b_loaded.sem, 16)
            for weights in later:
                weights.start(sp)

        @block.gpsimd
        def _(pool):
            win_free.open(pool)
            pool.wait_ge(rows_ready, 1)
            with pool.Fori(0, NB // 2) as b2:
                for par in range(2):
                    pool.tensor_copy(idx[:, par, :], batch(rows, b2 * 2 + par)).then_inc(idx_copied.sem, 1)
                    pool.wait_ge(idx_copied.sem, idx_copied.take())
                    for t in range(TILES):
                        pool.wait_ge(win_free.sem, win_free.take())
                        pool.indirect_dma_start(
                            out=win[:, t, :], out_offset=None, in_=table[:, :],
                            in_offset=bass.IndirectOffsetOnAxis(ap=idx[:, par, t:t + 1], axis=0),
                        ).then_inc(landed[t], 16)
                idx_copied.settle(pool)
                win_free.settle(pool)

        @block.tensor
        def _(pe):
            for q in (*t_read, out_read):
                q.open(pe)
            pe.wait_ge(w_loaded.sem, w_loaded.take(32))

            def transpose(b, t, first):
                pe.wait_ge(landed[t], b * 16 + 16)
                read = t_read[t % 2]
                pe.wait_ge(read.sem, read.take())
                for c in range(CHUNKS):
                    last = nc.tensor.transpose(psT[t % 2][:, c * P:(c + 1) * P],
                                               win[:, t, starts[c]:starts[c] + P], ident[:, :])
                    if c == 0 and not first:
                        last.then_inc(win_free.sem, 1)
                last.then_inc(t_done[t % 2].sem, 1)

            def convolve(par):
                for c in range(CHUNKS):
                    lo = 0 if c < CHUNKS - 1 else D
                    for half in range(2):
                        last = nc.tensor.matmul(psC[half * D:(half + 1) * D, :], w_sb[lo:P, c, :],
                                                winT[par][lo:P, c, half * HALF:(half + 1) * HALF], start=(c == 0),
                                                stop=(c == CHUNKS - 1), skip_group_check=True)
                last.then_inc(conv_done.sem, 1)

            def transpose_back():
                pe.wait_ge(cT_ready.sem, cT_ready.take())
                pe.wait_ge(out_read.sem, out_read.take())
                for j in range(TILES // 2):
                    last = nc.tensor.transpose(psO[:, j * P:(j + 1) * P], cT[:, j * P:(j + 1) * P], ident[:, :])
                last.then_inc(out_done.sem, 1)

            def body(b, par, prev=True, settle=True):
                for t in range(TILES):
                    transpose(b, t, first=(not prev and t == 0))
                    if t == 1 and prev:
                        convolve(1 - par)
                    if t == 4 and prev:
                        transpose_back()
                if settle:
                    for q in (w_loaded, *t_read, cT_ready, out_read):
                        q.settle(pe)
            turns(pe, body)
            for read in t_read:
                pe.wait_ge(read.sem, read.take())
            convolve(1)
            transpose_back()

        @block.scalar
        def _(act):
            act.wait_ge(b_loaded.sem, b_loaded.take(32))

            def copy_conv():
                act.wait_ge(conv_done.sem, conv_done.take())
                nc.scalar.activation(cT[:, :], psC[:, :], ACT.Identity, bias=b_col[:, :],
                                     scale=1.0).then_inc(cT_ready.sem, 1)

            def square():
                act.wait_ge(centred_done.sem, centred_done.take())
                nc.scalar.activation(centred[:, :, :], centred[:, :, :], ACT.Square).then_inc(squared.sem, 1)

            def body(b, par, prev=True, settle=True):
                for t in range(0, TILES, 2):
                    act.wait_ge(t_done[0].sem, t_done[0].take())
                    nc.scalar.activation(winT[par][:, :, t * P:(t + 1) * P],
                                         psT[0][:, 0:CHUNKS * P].rearrange("p (c n) -> p c n", c=CHUNKS),
                                         ACT.Copy).then_inc(t_read[0].sem, 1)
                    if t == 0 and prev:
                        copy_conv()
                if prev:
                    square()
                if settle:
                    for q in (b_loaded, t_done[0], conv_done, centred_done):
                        q.settle(act)
            turns(act, body)
            copy_conv()
            square()

        @block.vector
        def _(dve):
            dve.wait_ge(x_loaded, 16)
            nc.vector.tensor_scalar(rows[:, :], xi[:, :], float(-(KS // 2)), float(VOCAB - 1 + KS // 2),
                                    ALU.max, ALU.min).then_inc(clipped, 1)
            dve.wait_ge(clipped, 1)
            nc.vector.tensor_scalar(xi[:, :], rows[:, :], float(PAD - KS // 2), None, ALU.add).then_inc(clipped, 1)
            dve.wait_ge(clipped, 2)
            nc.vector.tensor_copy(rows[:, :], xi[:, :]).then_inc(rows_ready, 1)

            def link(ins):
                ins.then_inc(e_chain.sem, 1)
                dve.wait_ge(e_chain.sem, e_chain.take())

            def take_output(b):
                dve.wait_ge(out_done.sem, out_done.take())
                nc.vector.tensor_copy(batch(h_sb, b).rearrange("p (g j) d -> p g j d", g=2),
                                      psO[:, :].rearrange("p (j g d) -> p g j d", g=2, d=D)).then_inc(out_read.sem, 1)
                dve.drain()
                link(nc.vector.reduce_sum(batch(mean, b), batch(h_sb, b), AX.X))
                link(nc.vector.tensor_scalar(batch(mean, b), batch(mean, b), 1.0 / D, None, ALU.mult))
                nc.vector.tensor_tensor(centred[:, :, :], batch(h_sb, b), wide(batch(mean, b), D),
                                        ALU.subtract).then_inc(centred_done.sem, 1)

            def measure_variance(b):
                dve.wait_ge(squared.sem, squared.take())
                nc.vector.reduce_sum(batch(var, b), centred[:, :, :], AX.X)

            def body(b, par, prev=True, settle=True):
                for t in range(1, TILES, 2):
                    dve.wait_ge(t_done[1].sem, t_done[1].take())
                    nc.vector.tensor_copy(winT[par][:, :, t * P:(t + 1) * P],
                                          psT[1][:, 0:CHUNKS * P].rearrange("p (c n) -> p c n", c=CHUNKS)
                                          ).then_inc(t_read[1].sem, 1)
                    if t == 5 and prev:
                        take_output(b - 1)
                if prev:
                    measure_variance(b - 1)
                if settle:
                    for q in (t_done[1], out_done, e_chain, squared):
                        q.settle(dve)
            turns(dve, body)
            take_output(NB - 1)
            measure_variance(NB - 1)


def emit_layernorm(nc, tag, h_sb, stats, kind, g=None, measured=False):
    mean, var, r1, r2, s2 = (stats[:, i, :] for i in range(5))
    CH = 4
    n = NT // CH
    chunks = () if measured else range(CH)
    with ExitStack() as ctx:
        centred = ctx.enter_context(nc.sbuf_tensor(f"{tag}_centred", [P, 2, n, D], F32))
        g_sb = ctx.enter_context(nc.sbuf_tensor(f"{tag}_g", [P, 1], F32))
        sem = lambda name: ctx.enter_context(nc.semaphore(f"{tag}_{name}"))
        g_loaded = sem("g_loaded")
        root, chain = sem("root"), sem("chain")
        if chunks:
            summed, meaned, centred_done, squared, var_done = (
                sem(x) for x in ("summed", "meaned", "centred", "squared", "var"))
        block = ctx.enter_context(nc.Block())
        part = lambda t, c: t[:, c * n:(c + 1) * n]

        @block.sync
        def _(sp):
            if kind == "rms":
                sp.dma_start(g_sb[:, :], g.partition_broadcast(P)).then_inc(g_loaded, 16)

        @block.vector
        def _(dve):
            links = [0]

            def link(ins):
                links[0] += 1
                ins.then_inc(chain, 1)
                dve.wait_ge(chain, links[0])

            for c in chunks:
                nc.vector.reduce_sum(part(mean, c), part(h_sb, c), AX.X).then_inc(summed, 1)
                dve.wait_ge(summed, c + 1)
                nc.vector.tensor_scalar(part(mean, c), part(mean, c), 1.0 / D, None, ALU.mult).then_inc(meaned, 1)
            for c in chunks:
                dve.wait_ge(squared, c + 1)
                nc.vector.reduce_sum(part(var, c), centred[:, c % 2], AX.X).then_inc(var_done, 1)
            if chunks:
                dve.wait_ge(var_done, len(chunks))
            link(nc.vector.tensor_scalar(var, var, 1.0 / D, None, ALU.mult))
            nc.vector.tensor_scalar(r2, var, EPS, None, ALU.add).then_inc(root, 1)
            dve.wait_ge(root, 2)
            link(nc.vector.reciprocal(r1, s2))
            link(nc.vector.tensor_tensor(var, var, r1, ALU.mult))
            link(nc.vector.tensor_tensor(var, var, r1, ALU.mult))
            nc.vector.tensor_scalar(r2, var, EPS if kind == "norm" else 0.0, None, ALU.add).then_inc(root, 1)
            dve.wait_ge(root, 4)
            if kind == "rms":
                link(nc.vector.tensor_scalar(s2, s2, EPS, None, ALU.max))
            link(nc.vector.reciprocal(r2, s2))
            if kind == "rms":
                dve.wait_ge(g_loaded, 16)
                link(nc.vector.tensor_scalar(r2, r2, g_sb[:, :], None, ALU.mult))

        @block.gpsimd
        def _(pool):
            for c in chunks:
                pool.wait_ge(meaned, c + 1)
                if c >= 2:
                    pool.wait_ge(var_done, c - 1)
                nc.gpsimd.tensor_tensor(centred[:, c % 2], part(h_sb, c), wide(part(mean, c), D),
                                        ALU.subtract).then_inc(centred_done, 1)

        @block.scalar
        def _(act):
            for c in chunks:
                act.wait_ge(centred_done, c + 1)
                nc.scalar.activation(centred[:, c % 2], centred[:, c % 2], ACT.Square).then_inc(squared, 1)
            act.wait_ge(root, 1)
            nc.scalar.activation(s2, r2, ACT.Sqrt).then_inc(root, 1)
            act.wait_ge(root, 3)
            nc.scalar.activation(s2, r2, ACT.Sqrt).then_inc(root, 1)


RING = 3
EG = 4
UNITS = GROUPS * TILES * HG
LAG = 8


READER = {"score": "act", "q": "act", "k": "act", "gate": "act", "xT": "dve", "v": "dve", "proj": "dve"}
OWN = {8: ("q", 1), 12: ("k", 1), 15: ("high_q", 1), 17: ("low_q", 1), 18: ("high_k", 1), 20: ("low_k", 1),
       27: ("v", 1), 29: ("gate", 1)}
PREV = {14: ("proj", 0), 34: ("proj", 1)}
NEXT = {22: ("stage", 0), 25: ("base", 0), 32: ("xT", 0), 40: ("q", 0), 43: ("high_q", 0), 44: ("low_q", 0),
        48: ("k", 0), 50: ("high_k", 0), 51: ("low_k", 0), 56: ("v", 0), 58: ("gate", 0)}


class Event:

    def __init__(self, kind, n=0, quarter=0, final=False):
        self.kind, self.n, self.quarter, self.final, self.slot = kind, n, quarter, final, None
        self.group, self.tile, self.head = n // (TILES * HG), n // HG % TILES, n % HG
        self.slot_reader = None


def prep_events():
    return [Event("stage"), Event("base"), Event("xT"), Event("q"), Event("high_q"), Event("low_q"),
            Event("k"), Event("high_k"), Event("low_k"), Event("v"), Event("gate")]


def batch_events(has_prev, has_next):
    queries = GROUPS * TILES
    events = []
    for u in range(UNITS + (0 if has_next else LAG)):
        if u < UNITS:
            events.append(Event("score", u))
        k, c = (u - LAG) // HG, (u - LAG) % HG
        if (k, c) in ((0, 0), (TILES, 0)) and (k or has_prev):
            events.append(Event("out", 0 if k else 1))
        if k in (0, TILES):
            quarters = {0: (), 1: (), 2: (0, 1), 3: (2, 3)}[c]
        else:
            quarters = (c,) if k >= 0 or has_prev else ()
        events += [Event("av", k % queries, quarter) for quarter in quarters]
        if u % HG == 2 and (u > HG or has_prev):
            events.append(Event("values", (u // HG - 1) % queries))
        for table, wanted in ((OWN, u < UNITS), (PREV, has_prev), (NEXT, has_next)):
            if u in table and wanted:
                events.append(Event(*table[u]))
    if not has_next:
        events += [Event("out", 1, final=True), Event("proj", 0, final=True), Event("proj", 1)]
    return events


def attention_schedule():
    stretches = [prep_events(), batch_events(False, True), batch_events(True, True), batch_events(True, False)]
    at = 0
    readers = ["act"] * RING
    for n, events in enumerate(stretches):
        start = at
        if n >= 2:
            assert readers == ["act"] * RING
        for e in events:
            if e.kind in READER:
                e.slot = at % RING
                e.slot_reader, readers[e.slot] = readers[e.slot], READER[e.kind]
                at += 1
        assert n != 2 or (at - start) % RING == 0, at - start
    return stretches


def emit_attention0(nc, h_sb, stats, ident, w):
    mean, r1, r2 = stats[:, 0, :], stats[:, 2, :], stats[:, 3, :]
    schedule = attention_schedule()
    with ExitStack() as ctx:
        sb = lambda name, shape, dt=F32: ctx.enter_context(nc.sbuf_tensor(name, shape, dt))
        w_n, w_y, w_f, b_g, b_f, aff = w.w_n, w.w_y, w.w_f, w.b_g, w.b_f, w.aff
        xT = sb("xT", [P, T])
        split_in = [sb(f"split_in{i}", [P, T]) for i in range(2)]
        yn = split_in[0][:, :].rearrange("p (t c) -> p t c", t=TILES)
        hi = [sb(f"split_hi{i}", [P, T], F16) for i in range(2)]
        lo = [sb(f"split_lo{i}", [P, T], F16) for i in range(2)]
        q_st = [sb(f"q_stack{g}", [3 * DH, HG, T], F16) for g in range(GROUPS)]
        k_st = [sb(f"k_stack{g}", [3 * DH, HG, T], F16) for g in range(GROUPS)]
        v_sb = [sb(f"v{g}", [P, TILES, HG * DH]) for g in range(GROUPS)]
        gate = [sb(f"gate{g}", [P, T]) for g in range(GROUPS)]
        gated = [sb(f"gated{g}", [P, T]) for g in range(GROUPS)]
        e_sb = sb("exps", [P, EG, HG, T])
        one = sb("one", [P, 1])
        nmax = sb("nmax", [P, HG])
        zsum = sb("zsum", [P, EG, HG])
        rz = sb("rz", [P, EG, HG])
        vz = sb("vz", [P, EG, HG * DH])
        ring = [ctx.enter_context(nc.psum_tensor(f"ring{i}", [P, T], F32)) for i in range(RING)]
        outT = ctx.enter_context(nc.psum_tensor("outT", [P, T], F32))

        s = lambda name, credits=0: Signal(ctx, nc, name, credits)
        w_scaled = s("w_scaled")
        b_scaled = s("b_scaled")
        slot_free = {"act": s("slot_free_a", RING),
                     "dve": s("slot_free_v")}
        score_done = s("score_done")
        max_done = s("max_done")
        item_done = {"act": s("item_done_a"),
                     "dve": s("item_done_v")}
        exps_ended = s("exps_ended")
        sums_ended = s("sums_ended")
        rz_done = s("rz_done")
        vz_done = s("vz_done")
        e_free = s("e_free", EG)
        out_free = s("out_free", 1)
        staged = s("staged")
        copied = s("copied")
        split_done = s("split_done")
        stacked = [s(f"stacked{g}") for g in range(GROUPS)]
        pool_done = s("pool_done")
        block = ctx.enter_context(nc.Block())
        STACK_DMAS = 2 * 3 * HG

        def turns(eng, body):
            body(None, 0, schedule[0])
            body(0, 1, schedule[1])
            with eng.Fori(1, NB - 1) as b:
                body(b, b + 1, schedule[2])
            body(NB - 1, None, schedule[3])

        @block.sync
        def _(sp):
            def body(b, b_next, events):
                for e in events:
                    if e.kind not in ("low_q", "low_k"):
                        continue
                    i = 0 if e.kind == "low_q" else 1
                    stack = (q_st, k_st)[i][e.n]
                    parts = ((hi[0], lo[0], hi[0]), (hi[1], hi[1], lo[1]))[i]
                    sp.wait_ge(split_done.sem, split_done.take())
                    for n, part in enumerate(parts):
                        for h in range(HG):
                            sp.dma_start(stack[n * DH:(n + 1) * DH, h, :],
                                         part[h * DH:(h + 1) * DH, :]).then_inc(stacked[e.n].sem, 16)
                split_done.settle(sp)
            turns(sp, body)

        @block.tensor
        def _(pe):
            slot_free["act"].open(pe)
            out_free.open(pe)
            w.wait(pe)
            pe.wait_ge(w_scaled.sem, w_scaled.take())

            def body(b, b_next, events):
                unread = 0
                for e in events:
                    if e.kind in READER:
                        tile = ring[e.slot]
                        if e.kind == "score" and e.n % (TILES * HG) == 0:
                            stack = stacked[e.group]
                            pe.wait_ge(stack.sem, stack.take(STACK_DMAS * 16))
                        if e.kind == "xT":
                            pe.wait_ge(staged.sem, staged.take())
                        if e.kind == "proj" and e.final:
                            pe.wait_ge(out_free.sem, out_free.take())
                        free = slot_free[e.slot_reader]
                        unread += (READER[e.kind] == "dve") - (e.slot_reader == "dve")
                        pe.wait_ge(free.sem, free.take())
                        if e.kind == "q" and e.n == 0 and unread:
                            xT_read = slot_free["dve"]
                            pe.wait_ge(xT_read.sem, xT_read.taken + unread)
                    if e.kind == "score":
                        for j in range(2):
                            last = nc.tensor.matmul(tile[:, j * HALF:(j + 1) * HALF],
                                                    q_st[e.group][:, e.head, e.tile * P:(e.tile + 1) * P],
                                                    k_st[e.group][:, e.head, j * HALF:(j + 1) * HALF],
                                                    start=True, stop=True)
                        last.then_inc(score_done.sem, 1)
                    elif e.kind == "av":
                        c, first = e.quarter, e.n % TILES == 0
                        if c == 0:
                            pe.wait_ge(vz_done.sem, vz_done.take())
                        if c == 0 and first:
                            pe.wait_ge(out_free.sem, out_free.take())
                        quarter = slice(c * T // 4, (c + 1) * T // 4)
                        for h in range(HG):
                            last = nc.tensor.matmul(outT[h * DH:(h + 1) * DH, quarter],
                                                    vz[:, e.n % EG, h * DH:(h + 1) * DH],
                                                    e_sb[:, e.n % EG, h, quarter], start=first and c % 2 == 0,
                                                    stop=e.n % TILES == TILES - 1, skip_group_check=True)
                        if c == 3:
                            last.then_inc(e_free.sem, 1)
                    elif e.kind == "xT":
                        for t in range(TILES):
                            last = nc.tensor.transpose(tile[:, t * P:(t + 1) * P], yn[:, t, :], ident[:, :])
                        last.then_inc(item_done["dve"].sem, 1)
                    elif e.kind in ("q", "k", "gate"):
                        col = e.n * P + (HEADS * DH if e.kind == "k" else 0)
                        weight, rows = (w_y, UPPER) if e.kind == "gate" else (w_n, LOWER)
                        for j in range(2):
                            last = nc.tensor.matmul(tile[:, j * HALF:(j + 1) * HALF], weight[rows, col:col + P],
                                                    xT[rows, j * HALF:(j + 1) * HALF], start=True, stop=True)
                        last.then_inc(item_done["act"].sem, 1)
                    elif e.kind == "v":
                        col = 2 * HEADS * DH + e.n * P
                        for t in range(TILES):
                            last = nc.tensor.matmul(tile[:, t * P:(t + 1) * P], xT[D:P, t * P:(t + 1) * P],
                                                    w_n[D:P, col:col + P], start=True, stop=True)
                        last.then_inc(item_done["dve"].sem, 1)
                    elif e.kind == "proj":
                        for i in range(TILES // 2):
                            t = e.n * TILES // 2 + i
                            for g in range(GROUPS):
                                last = nc.tensor.matmul(tile[:, i * D:(i + 1) * D], gated[g][:, t * P:(t + 1) * P],
                                                        w_f[:, g, :], start=(g == 0), stop=(g == 1))
                        last.then_inc(item_done["dve"].sem, 1)
                    elif e.kind == "out" and e.final:
                        pe.drain().then_inc(sums_ended.sem, 1)
                for q in (w_scaled, *slot_free.values(), out_free, vz_done, staged, *stacked):
                    q.settle(pe)
            turns(pe, body)

        @block.vector
        def _(dve):
            w.wait(dve)
            nc.vector.memset(aff[0:D, 0:1], 1.0)
            nc.vector.memset(aff[0:D, 1:2], 0.0)
            nc.vector.tensor_scalar(b_g[:, :], b_g[:, :], 0.5, None, ALU.mult).then_inc(b_scaled.sem, 1)
            nc.vector.tensor_scalar(w_f[:, :, :], w_f[:, :, :], 0.5, None, ALU.mult).then_inc(w_scaled.sem, 1)

            def body(b, b_next, events):
                for n, e in enumerate(events):
                    if e.kind == "score":
                        dve.wait_ge(score_done.sem, score_done.take())
                        nc.vector.tensor_reduce(nmax[:, e.head:e.head + 1], ring[e.slot][:, :], axis=AX.X,
                                                op=ALU.max, negate=True).then_inc(max_done.sem, 1)
                    elif e.kind == "values":
                        if b_next is None and e.n == GROUPS * TILES - 1 and n > len(events) // 2:
                            dve.wait_ge(exps_ended.sem, exps_ended.take())
                        nc.vector.reciprocal(rz[:, e.n % EG, :], zsum[:, e.n % EG, :]).then_inc(rz_done.sem, 1)
                    elif e.kind == "out":
                        if e.final:
                            dve.wait_ge(sums_ended.sem, sums_ended.take())
                        nc.vector.scalar_tensor_tensor(gated[e.n][:, :], gate[e.n][:, :], 1.0, outT[:, :],
                                                       ALU.add, ALU.mult).then_inc(out_free.sem, 1)
                    elif READER.get(e.kind) == "dve":
                        done, free, tile = item_done["dve"], slot_free["dve"], ring[e.slot]
                        dve.wait_ge(done.sem, done.take())
                        if e.kind == "xT":
                            nc.vector.tensor_scalar(xT[:, :], tile[:, :], aff[:, 0:1], aff[:, 1:2], ALU.mult,
                                                    ALU.add).then_inc(free.sem, 1)
                        elif e.kind == "v":
                            nc.vector.tensor_copy(v_sb[e.n][:, :, :].rearrange("p t d -> p (t d)"),
                                                  tile[:, :]).then_inc(free.sem, 1)
                        elif e.kind == "proj":
                            last_batch = b_next is None and n >= len(events) - 2
                            half = TILES // 2
                            at = NB - 1 if last_batch else b - 1
                            h = h_sb[:, bass.ds(at * TILES + e.n * half, half)]
                            nc.vector.tensor_tensor(h, h, tile[:, 0:half * D].rearrange("p (t d) -> p t d", d=D),
                                                    ALU.add).then_inc(free.sem, 1)
                for q in (score_done, item_done["dve"], exps_ended, sums_ended):
                    q.settle(dve)
            turns(dve, body)

        @block.scalar
        def _(act):
            e_free.open(act)
            w.wait(act)
            act.wait_ge(b_scaled.sem, b_scaled.take())

            def body(b, b_next, events):
                for e in events:
                    if READER.get(e.kind) != "act":
                        continue
                    tile, free, done = ring[e.slot], slot_free["act"], item_done["act"]
                    if e.kind == "score":
                        act.wait_ge(max_done.sem, max_done.take())
                        k = e.tile % EG
                        if e.head == 0:
                            act.wait_ge(e_free.sem, e_free.take())
                        nc.scalar.activation(e_sb[:, k, e.head, :], tile[:, :], ACT.Exp,
                                             bias=nmax[:, e.head:e.head + 1], scale=1.0,
                                             accum_out=zsum[:, k, e.head:e.head + 1]).then_inc(free.sem, 1)
                        if e.n == UNITS - 1 and b_next is None:
                            act.drain().then_inc(exps_ended.sem, 1)
                        continue
                    act.wait_ge(done.sem, done.take())
                    if e.kind in ("q", "k"):
                        i = 0 if e.kind == "q" else 1
                        nc.scalar.activation(split_in[i][:, :], tile[:, :], ACT.Copy,
                                             scale=(SCALE0, 1.0)[i]).then_inc(free.sem, 1)
                        act.drain().then_inc(copied.sem, 1)
                    elif e.kind == "gate":
                        nc.scalar.activation(gate[e.n][:, :], tile[:, :], ACT.Tanh, bias=b_g[:, e.n:e.n + 1],
                                             scale=0.5).then_inc(free.sem, 1)
                for q in (b_scaled, max_done, e_free, item_done["act"]):
                    q.settle(act)
            turns(act, body)

        @block.gpsimd
        def _(pool):
            w.wait(pool)
            pool.memset(one[:, :], 1.0).then_inc(pool_done.sem, 1)
            pool.wait_ge(pool_done.sem, pool_done.take())

            def body(b, b_next, events):
                for e in events:
                    if e.kind == "values":
                        pool.wait_ge(rz_done.sem, rz_done.take())
                        k = e.n % EG
                        v = v_sb[e.n // TILES][:, e.n % TILES, :].rearrange("p (h d) -> p h d", h=HG)
                        nc.gpsimd.tensor_tensor(vz[:, k, :].rearrange("p (h d) -> p h d", h=HG), v,
                                                wide(rz[:, k, :], DH), ALU.mult).then_inc(vz_done.sem, 1)
                    elif e.kind in ("high_q", "high_k"):
                        i = 0 if e.kind == "high_q" else 1
                        pool.wait_ge(copied.sem, copied.take())
                        nc.gpsimd.tensor_tensor(hi[i][:, :], split_in[i][:, :], one[:, :].to_broadcast([P, T]),
                                                ALU.mult).then_inc(pool_done.sem, 1)
                        pool.wait_ge(pool_done.sem, pool_done.take())
                    elif e.kind in ("low_q", "low_k"):
                        i = 0 if e.kind == "low_q" else 1
                        nc.gpsimd.tensor_tensor(lo[i][:, :], split_in[i][:, :], hi[i][:, :],
                                                ALU.subtract).then_inc(split_done.sem, 1)
                    elif e.kind == "stage":
                        y = yn[:, :, 0:D]
                        for src, stat, op in ((batch(h_sb, b_next), mean, ALU.subtract), (y, r1, ALU.mult)):
                            nc.gpsimd.tensor_tensor(y, src, wide(batch(stat, b_next), D), op).then_inc(pool_done.sem, 1)
                            pool.wait_ge(pool_done.sem, pool_done.take())
                        nc.gpsimd.tensor_tensor(yn[:, :, D:2 * D], y, wide(batch(r2, b_next), D), ALU.mult)
                    elif e.kind == "base":
                        h = batch(h_sb, b_next)
                        nc.gpsimd.tensor_tensor(h, h, shared(b_f[:, :], TILES), ALU.add).then_inc(pool_done.sem, 1)
                        pool.wait_ge(pool_done.sem, pool_done.take())
                        nc.gpsimd.tensor_tensor(h, h, yn[:, :, 0:D], ALU.add).then_inc(staged.sem, 1)
                for q in (rz_done, copied, pool_done):
                    q.settle(pool)
            turns(pool, body)


WS = 64.0
TE = TILES * EXPERTS
SIDE = {2: ("back", 0), 4: ("tokens", 0), 5: ("tokens", 1), 7: ("router", 0), 12: ("weights", 0)}


def emit_moe0(nc, h_sb, stats, ident, w):
    mean, var, r1, r2, s2 = (stats[:, i, :] for i in range(5))
    with ExitStack() as ctx:
        sb = lambda name, shape, dt=F32: ctx.enter_context(nc.sbuf_tensor(name, shape, dt))
        w1f, lng_sb, lnb_sb, wrf, br_sb, b1_sb, w2_sb, b2_sb = w.w1, w.lng, w.lnb, w.wr, w.br, w.b1, w.w2, w.b2
        w1s = sb("w1s", [P, EXPERTS, HID0])
        w1h = sb("w1h", [P, HT, P], F16)
        w1l = sb("w1l", [P, HT, P], F16)
        wrh = sb("wrh", [P, EXPERTS], F16)
        wrl = sb("wrl", [P, EXPERTS], F16)
        iota_i = sb("iota_i", [P, EXPERTS], I32)
        iota = sb("iota", [P, EXPERTS])
        euler = sb("euler", [P, TILES])
        select = sb("select", [P, TE, D], F16)
        xn = sb("xn", [P, TILES, 2 * D])
        xs = [sb(f"xs{i}", [P, T], F16) for i in range(2)]
        hid = [sb(f"hid{i}", [P, T]) for i in range(2)]
        logits = sb("logits", [P, TILES, EXPERTS])
        top = sb("top", [P, TILES, 8])
        top_i = sb("top_i", [P, TILES, 8], U32)
        top_f = sb("top_f", [P, 2, TILES])
        gap = sb("gap", [P, TILES])
        e2 = sb("e2", [P, TILES])
        tw = sb("tw", [P, 2, TILES])
        den = sb("den", [P, TILES])
        pick = sb("pick", [P, 2, TILES, EXPERTS])
        wt = sb("wt", [P, 2, TE])
        wts = [sb(f"wts{i}", [P, P], F16) for i in range(2)]
        acc = sb("acc", [P, HALF])
        wb = [sb(f"wb{i}", [P, HALF]) for i in range(2)]
        centred = sb("m0_centred", [P, TILES, D])
        term = [sb(f"term{i}", [P, HALF]) for i in range(2)]
        hps = [ctx.enter_context(nc.psum_tensor(f"hps{i}", [P, T], F32)) for i in range(2)]
        yps = [ctx.enter_context(nc.psum_tensor(f"yps{i}", [P, HALF], F32)) for i in range(2)]
        wps = ctx.enter_context(nc.psum_tensor("wps", [P, HALF], F32))
        side = ctx.enter_context(nc.psum_tensor("side", [P, HALF], F32))

        s = lambda name, credits=0: Signal(ctx, nc, name, credits)
        consts = s("consts")
        folded_v = s("folded_v")
        w_ready = s("w_ready")
        select_ready = s("select_ready")
        b1_ready = s("b1_ready")
        xn_ready = s("xn_ready")
        side_done = s("side_done")
        side_read = s("side_read", 1)
        xs_ready = s("xs_ready")
        wt_ready = s("wt_ready")
        wts_ready = s("wts_ready")
        h_done = s("h_done")
        gelu_done = s("gelu_done")
        wps_done = s("wps_done")
        wps_read = s("wps_read", 1)
        wb_ready = s("wb_ready")
        y_done = s("y_done")
        y_read = s("y_read", 1)
        gap_ready = s("gap_ready")
        e2_ready = s("e2_ready")
        term_done = s("term_done")
        term_free = s("term_free", 2)
        acc_ready = s("acc_ready")
        mean_done = s("mean_done0")
        centred_done = s("centred_done0")
        squared = s("squared0")
        chain = s("dve_chain")
        pool_done = s("pool_done0")
        block = ctx.enter_context(nc.Block())

        def turns(eng, body):
            body(0, 0, prev=False)
            with eng.Fori(0, (NB - 2) // 2) as r:
                body(r * 2 + 1, 1, settle=False)
                body(r * 2 + 2, 0)
            body(NB - 1, 1, next=False)

        def due(ht, prev, next):
            kind, n = SIDE.get(ht, (None, 0))
            return (kind, n) if (prev if kind == "back" else next) else (None, 0)

        @block.tensor
        def _(pe):
            side_read.open(pe)
            y_read.open(pe)
            wps_read.open(pe)
            w.wait(pe)

            def fill_side(kind, n, par):
                if kind is None:
                    return
                if kind == "back":
                    pe.wait_ge(acc_ready.sem, acc_ready.take())
                if kind == "tokens" and n == 0:
                    pe.wait_ge(xn_ready.sem, xn_ready.take())
                if kind == "router":
                    pe.wait_ge(xs_ready.sem, xs_ready.take())
                if kind == "weights":
                    pe.wait_ge(wt_ready.sem, wt_ready.take())
                pe.wait_ge(side_read.sem, side_read.take())
                if kind == "back":
                    for j in range(TILES // 2):
                        last = nc.tensor.transpose(side[:, j * P:(j + 1) * P], acc[:, j * P:(j + 1) * P], ident[:, :])
                elif kind == "tokens":
                    for j in range(TILES // 2):
                        last = nc.tensor.transpose(side[:, j * P:(j + 1) * P], xn[:, n * TILES // 2 + j, :], ident[:, :])
                elif kind == "router":
                    for t in range(TILES):
                        out = side[:, t * EXPERTS:(t + 1) * EXPERTS]
                        nc.tensor.matmul(out, xs[par][:, t * P:(t + 1) * P], wrh[:, :], start=True, stop=False)
                        last = nc.tensor.matmul(out, xs[par][0:D, t * P:(t + 1) * P], wrl[0:D, :], start=False, stop=True)
                else:
                    last = nc.tensor.transpose(side[:, 0:P], wt[:, :, :].rearrange("p k i -> p (k i)"), ident[:, :])
                last.then_inc(side_done.sem, 1)

            def layer1(ht, par):
                for j in range(2):
                    cols = slice(j * HALF, (j + 1) * HALF)
                    nc.tensor.matmul(hps[ht % 2][:, cols], w1h[:, ht, :], xs[par][:, cols], start=True, stop=False)
                    last = nc.tensor.matmul(hps[ht % 2][:, cols], w1l[0:D, ht, :], xs[par][0:D, cols],
                                            start=False, stop=True)
                last.then_inc(h_done.sem, 1)

            def layer2(ht, par):
                expert, chunk = divmod(ht, HC)
                if chunk == 0:
                    if expert == 0:
                        pe.wait_ge(wts_ready.sem, wts_ready.take())
                    pe.wait_ge(wps_read.sem, wps_read.take())
                    for i in range(TILES):
                        j, half = divmod(i, 2)
                        t = half * TILES // 2 + j
                        last = nc.tensor.matmul(wps[half * D:(half + 1) * D, j * P:(j + 1) * P],
                                                select[:, t * EXPERTS + expert, :], wts[par][:, :], start=True,
                                                stop=True)
                    last.then_inc(wps_done.sem, 1)
                if chunk == HC - 1:
                    pe.wait_ge(y_read.sem, y_read.take())
                pe.wait_ge(gelu_done.sem, gelu_done.take())
                for half in range(2):
                    last = nc.tensor.matmul(yps[expert % 2][half * D:(half + 1) * D, :], w2_sb[:, ht, :],
                                            hid[ht % 2][:, half * HALF:(half + 1) * HALF], start=(chunk == 0),
                                            stop=(chunk == HC - 1), skip_group_check=True)
                if chunk == HC - 1:
                    last.then_inc(y_done.sem, 1)

            for ht in range(HT):
                expert, chunk = divmod(ht, HC)
                last = nc.tensor.matmul(hps[0][:, ht:ht + 1], w1f[0:D, expert, chunk * P:(chunk + 1) * P],
                                        lnb_sb[0:D, expert:expert + 1], start=True, stop=True)
            last.then_inc(folded_v.sem, 1)
            pe.wait_ge(w_ready.sem, w_ready.take())
            pe.wait_ge(select_ready.sem, select_ready.take())

            def settle_all():
                for q in (xn_ready, w_ready, select_ready, gelu_done, y_read, wps_read, xs_ready, side_read, wt_ready,
                          wts_ready, acc_ready):
                    q.settle(pe)

            for kind, n in SIDE.values():
                if kind != "back":
                    fill_side(kind, n, 0)

            def body(b, par, prev=True, next=True, settle=True):
                for ht in range(HT + 1):
                    if ht < HT:
                        layer1(ht, par)
                    fill_side(*due(ht, prev, next), 1 - par)
                    if ht:
                        layer2(ht - 1, par)
                if settle:
                    settle_all()
            turns(pe, body)
            fill_side("back", 0, 0)

        @block.scalar
        def _(act):
            for rows in (UPPER, LOWER):
                last = nc.scalar.activation(select[rows, :, :], wide(ident[rows, rows], D), ACT.Copy)
            last.then_inc(select_ready.sem, 1)
            act.wait_ge(b1_ready.sem, b1_ready.take())

            def square():
                act.wait_ge(centred_done.sem, centred_done.take())
                nc.scalar.activation(centred[:, :, :], centred[:, :, :], ACT.Square).then_inc(squared.sem, 1)

            def body(b, par, prev=True, next=True, settle=True):
                for ht in range(HT):
                    if ht == 8 and prev:
                        square()
                    act.wait_ge(h_done.sem, h_done.take())
                    nc.scalar.activation(hid[ht % 2][:, :], hps[ht % 2][:, :], ACT.Gelu, bias=b1_sb[:, ht:ht + 1],
                                         scale=1.0 / WS).then_inc(gelu_done.sem, 1)
                    if ht % HC == HC - 1:
                        e = ht // HC
                        act.wait_ge(wps_done.sem, wps_done.take())
                        nc.scalar.activation(wb[e % 2][:, :], wps[:, :], ACT.Copy).then_inc(wps_read.sem, 1)
                        act.drain().then_inc(wb_ready.sem, 1)
                if settle:
                    for q in (h_done, wps_done, centred_done):
                        q.settle(act)
            turns(act, body)
            square()

        @block.gpsimd
        def _(pool):
            pool.memset(euler[:, :], float(np.e))
            pool.iota(iota_i[:, :], pattern=[[1, EXPERTS]], base=0, channel_multiplier=0).then_inc(consts.sem, 1)

            def step(ins):
                ins.then_inc(pool_done.sem, 1)
                pool.wait_ge(pool_done.sem, pool_done.take())

            def stage(b):
                x = xn[:, :, 0:D]
                for src, stat, op in ((batch(h_sb, b), mean, ALU.subtract), (x, r1, ALU.mult), (x, r2, ALU.mult)):
                    step(nc.gpsimd.tensor_tensor(x, src, wide(batch(stat, b), D), op))
                nc.gpsimd.tensor_copy(xn[:, :, D:2 * D], x).then_inc(xn_ready.sem, 1)

            def exp_gap():
                pool.wait_ge(gap_ready.sem, gap_ready.take())
                nc.gpsimd.tensor_tensor(e2[:, :], euler[:, :], gap[:, :], ALU.pow).then_inc(e2_ready.sem, 1)

            def centre(b):
                pool.wait_ge(mean_done.sem, mean_done.take())
                nc.gpsimd.tensor_tensor(centred[:, :, :], batch(h_sb, b), wide(batch(mean, b), D),
                                        ALU.subtract).then_inc(centred_done.sem, 1)

            def settle_all():
                for q in (gap_ready, term_done, mean_done, pool_done):
                    q.settle(pool)

            stage(0)
            exp_gap()

            def body(b, par, prev=True, next=True, settle=True):
                if next:
                    stage(b + 1)
                pool.wait_ge(term_done.sem, term_done.take())
                for e in range(1, EXPERTS):
                    if e == 2 and prev:
                        centre(b - 1)
                    if e == 3 and next:
                        exp_gap()
                    pool.wait_ge(term_done.sem, term_done.take())
                    step(nc.gpsimd.tensor_tensor(acc[:, :], acc[:, :], term[e % 2][:, :], ALU.add))
                    pool.sem_inc(term_free.sem, 1)
                pool.sem_inc(acc_ready.sem, 1)
                if settle:
                    settle_all()
            turns(pool, body)
            centre(NB - 1)

        @block.vector
        def _(dve):
            term_free.open(dve)

            def link(ins):
                ins.then_inc(chain.sem, 1)
                dve.wait_ge(chain.sem, chain.take())

            def read_side(kind, n, par, b):
                if kind is None:
                    return
                dve.wait_ge(side_done.sem, side_done.take())
                if kind == "back":
                    h = batch(h_sb, b).rearrange("p (g j) d -> p g j d", g=2)
                    nc.vector.tensor_tensor(h, h, side[:, :].rearrange("p (j g d) -> p g j d", g=2, d=D),
                                            ALU.add).then_inc(side_read.sem, 1)
                elif kind == "tokens":
                    x = xs[par][:, n * HALF:(n + 1) * HALF]
                    link(nc.vector.tensor_copy(x, side[:, :]))
                    nc.vector.tensor_tensor(x[D:P], side[D:P, :], x[D:P], ALU.subtract).then_inc(side_read.sem, 1)
                    if n == 1:
                        dve.drain().then_inc(xs_ready.sem, 1)
                elif kind == "router":
                    route_logits(b)
                else:
                    link(nc.vector.tensor_copy(wts[par][:, :], side[:, 0:P]))
                    nc.vector.tensor_tensor(wts[par][TE:P, :], side[TE:P, 0:P], wts[par][TE:P, :],
                                            ALU.subtract).then_inc(side_read.sem, 1)
                    dve.drain().then_inc(wts_ready.sem, 1)

            def route_logits(b):
                nc.vector.tensor_tensor(logits[:, :, :], side[:, 0:TE].rearrange("p (t e) -> p t e", e=EXPERTS),
                                        wide(batch(s2, b), EXPERTS), ALU.mult).then_inc(side_read.sem, 1)
                dve.drain()
                link(nc.vector.scalar_tensor_tensor(logits[:, :, :], logits[:, :, :], 1.0 / WS,
                                                    shared(br_sb[:, :], TILES), ALU.mult, ALU.add))
                for t in range(TILES):
                    last = nc.vector.max(top[:, t, :], logits[:, t, :])
                link(last)
                nc.vector.tensor_tensor(gap[:, :], top[:, :, 1], top[:, :, 0], ALU.subtract).then_inc(gap_ready.sem, 1)
                for t in range(TILES):
                    last = nc.vector.max_index(top_i[:, t, :], top[:, t, :], logits[:, t, :])
                link(last)
                link(nc.vector.tensor_copy(top_f[:, :, :], top_i[:, :, 0:2].rearrange("p t k -> p k t")))
                for k in range(2):
                    last = nc.vector.tensor_tensor(pick[:, k], shared(iota[:, :], TILES), wide(top_f[:, k, :], EXPERTS),
                                                   ALU.is_equal)
                link(last)

            def route_weights():
                dve.wait_ge(e2_ready.sem, e2_ready.take())
                link(nc.vector.tensor_scalar(den[:, :], e2[:, :], 1.0, None, ALU.add))
                link(nc.vector.reciprocal(tw[:, 0, :], den[:, :]))
                link(nc.vector.tensor_tensor(tw[:, 1, :], e2[:, :], tw[:, 0, :], ALU.mult))
                for k in range(2):
                    last = nc.vector.tensor_tensor(pick[:, k], pick[:, k], wide(tw[:, k, :], EXPERTS), ALU.mult)
                link(last)
                for k in range(2):
                    last = nc.vector.tensor_tensor(wt[:, k, :].rearrange("p (t e) -> p t e", e=EXPERTS), pick[:, 0],
                                                   pick[:, 1], ALU.add)
                last.then_inc(wt_ready.sem, 1)

            w.wait(dve)
            dve.wait_ge(consts.sem, consts.take())
            nc.vector.tensor_copy(iota[:, :], iota_i[:, :])
            for e in range(EXPERTS):
                last = nc.vector.tensor_scalar(w1s[:, e, :], w1f[:, e, :], lng_sb[:, e:e + 1], WS, ALU.mult, ALU.mult)
            link(last)
            link(nc.vector.tensor_scalar(wrf[:, :], wrf[:, :], WS, None, ALU.mult))
            w1_flat = w1s[:, :, :].rearrange("p e h -> p (e h)")
            flat = lambda w: w[:, :, :].rearrange("p t h -> p (t h)")
            link(nc.vector.tensor_copy(flat(w1h), w1_flat))
            nc.vector.tensor_tensor(flat(w1l), w1_flat, flat(w1h), ALU.subtract)
            link(nc.vector.tensor_copy(wrh[:, :], wrf[:, :]))
            nc.vector.tensor_tensor(wrl[:, :], wrf[:, :], wrh[:, :], ALU.subtract).then_inc(w_ready.sem, 1)
            dve.wait_ge(folded_v.sem, folded_v.take())
            nc.vector.tensor_tensor(b1_sb[:, :], b1_sb[:, :], hps[0][:, 0:HT], ALU.add).then_inc(b1_ready.sem, 1)
            for kind, n in SIDE.values():
                if kind != "back":
                    read_side(kind, n, 0, 0)
                if kind == "router":
                    route_weights()

            def settle_all():
                for q in (consts, folded_v, squared, side_done, e2_ready, wb_ready, y_done, term_free, chain):
                    q.settle(dve)
            settle_all()

            def measure_mean(b):
                dve.drain()
                link(nc.vector.reduce_sum(batch(mean, b), batch(h_sb, b), AX.X))
                nc.vector.tensor_scalar(batch(mean, b), batch(mean, b), 1.0 / D, None, ALU.mult).then_inc(mean_done.sem, 1)

            def measure_variance(b):
                dve.wait_ge(squared.sem, squared.take())
                nc.vector.reduce_sum(batch(var, b), centred[:, :, :], AX.X)

            def body(b, par, prev=True, next=True, settle=True):
                for ht in range(1, HT + 1):
                    if ht == 3 and prev:
                        measure_mean(b - 1)
                    if ht == 13 and prev:
                        measure_variance(b - 1)
                    kind, n = due(ht, prev, next)
                    read_side(kind, n, 1 - par, b - 1 if kind == "back" else b + 1)
                    if ht == 10 and next:
                        route_weights()
                    if ht % HC == 0:
                        e = ht // HC - 1
                        dve.wait_ge(wb_ready.sem, wb_ready.take())
                        dve.wait_ge(y_done.sem, y_done.take())
                        if e:
                            dve.wait_ge(term_free.sem, term_free.take())
                        nc.vector.scalar_tensor_tensor(term[e % 2][:, :] if e else acc[:, :], yps[e % 2][:, :],
                                                       b2_sb[:, e:e + 1], wb[e % 2][:, :], ALU.add,
                                                       ALU.mult).then_inc(term_done.sem, 1)
                        dve.drain().then_inc(y_read.sem, 1)
                if settle:
                    settle_all()
            turns(dve, body)
            read_side("back", 0, 0, NB - 1)
            measure_mean(NB - 1)
            measure_variance(NB - 1)




def emit_attention1(nc, h_sb, stats, ident, w):
    mean, var, r1, r2 = (stats[:, i, :] for i in range(4))
    with ExitStack() as ctx:
        sb = lambda name, shape, dt=F32: ctx.enter_context(nc.sbuf_tensor(name, shape, dt))
        w_sb, gb, wo_sb, bo_sb = w.uv, w.gb, w.wo, w.bo
        xn = sb("xn1", [P, TILES, D])
        xT = sb("xT1", [D + 1, T])
        base = sb("base", [P, T])
        u_sb, v_sb = ([sb(f"{n}1_{i}", [P, T]) for i in range(2)] for n in "uv")
        full = [sb(f"a1_{n}", [P, T]) for n in "qk"]
        high = [[sb(f"a1_{n}h{i}", [P, T], F16) for i in range(2)] for n in "qk"]
        low = [[sb(f"a1_{n}l{i}", [P, T], F16) for i in range(2)] for n in "qk"]
        centred = sb("a1_centred", [P, TILES, D])
        a_sb = [sb(f"a1_{i}", [P, T]) for i in range(2)]
        gated = sb("a1_gated", [P, T])
        proj = sb("a1_proj", [P, TILES, D])
        sps = [ctx.enter_context(nc.psum_tensor(f"sps{i}", [P, T], F32)) for i in range(2)]
        ops_ = ctx.enter_context(nc.psum_tensor("ops", [P, T], F32))
        pps = ctx.enter_context(nc.psum_tensor("pps", [P, T], F32))

        s = lambda name, credits=0: Signal(ctx, nc, name, credits)
        scaled = s("scaled1")
        xn_ready = s("xn_ready1")
        xn_free = s("xn_free1", 1)
        p_done = s("p_done1")
        proj_done = s("proj_done1")
        p_free = s("p_free1", 1)
        base_done = s("base_done1")
        split = s("split1")
        qk_ready = s("qk_ready1")
        mean_done = s("mean_done1")
        centred_done = s("centred_done1")
        squared = s("squared1")
        s_done = s("s_done1")
        relu_done = s("relu_done1")
        a_ready = s("a_ready1")
        o_done = s("o_done1")
        gated_done = s("gated_done1", 1)
        chain = s("dve_chain1")
        pool_done = s("pool_done1")
        block = ctx.enter_context(nc.Block())

        def turns(eng, body):
            body(None, 1, False, True)
            body(0, 0, False, True)
            with eng.Fori(0, (NB - 2) // 2) as i:
                body(i * 2 + 1, 1, True, True, settle=False)
                body(i * 2 + 2, 0, True, True)
            body(NB - 1, 1, True, False)

        @block.gpsimd
        def _(pool):
            xn_free.open(pool)

            def body(b, par, has_prev, has_next, settle=True):
                if has_next:
                    nxt = 0 if b is None else b + 1
                    pool.wait_ge(xn_free.sem, xn_free.take())
                    x = xn[:, :, :]
                    for n, (src, stat, op) in enumerate(((batch(h_sb, nxt), mean, ALU.subtract), (x, r1, ALU.mult),
                                                         (x, r2, ALU.mult))):
                        ins = nc.gpsimd.tensor_tensor(x, src, wide(batch(stat, nxt), D), op)
                        if n < 2:
                            ins.then_inc(pool_done.sem, 1)
                            pool.wait_ge(pool_done.sem, pool_done.take())
                    ins.then_inc(xn_ready.sem, 1)
                    for i in range(2):
                        pool.wait_ge(split.sem, split.take())
                        nc.gpsimd.tensor_tensor(low[i][1 - par][:, :], full[i][:, :], high[i][1 - par][:, :],
                                                ALU.subtract).then_inc(qk_ready.sem, 1)
                for at in ([b - 1] if has_prev else []) + ([b] if b is not None and not has_next else []):
                    pool.wait_ge(mean_done.sem, mean_done.take())
                    nc.gpsimd.tensor_tensor(centred[:, :, :], batch(h_sb, at), wide(batch(mean, at), D),
                                            ALU.subtract).then_inc(centred_done.sem, 1)
                if settle:
                    for q in (xn_free, pool_done, split, mean_done):
                        q.settle(pool)
            turns(pool, body)

        @block.tensor
        def _(pe):
            p_free.open(pe)
            gated_done.open(pe)
            w.wait(pe)
            pe.wait_ge(scaled.sem, scaled.take())

            def scores(par, m):
                if m == 0:
                    pe.wait_ge(qk_ready.sem, qk_ready.take(2))
                for j in range(2):
                    cols = slice(j * HALF, (j + 1) * HALF)
                    for n, (k, q) in enumerate(((high, high), (high, low), (low, high))):
                        last = nc.tensor.matmul(sps[m % 2][:, cols], k[1][par][:, m * P:(m + 1) * P],
                                                q[0][par][:, cols], start=(n == 0), stop=(n == 2))
                last.then_inc(s_done.sem, 1)

            def attend(par, m):
                pe.wait_ge(a_ready.sem, a_ready.take())
                if m == 0:
                    pe.wait_ge(gated_done.sem, gated_done.take())
                    pe.wait_ge(p_free.sem, p_free.taken + 1)
                for j in range(2):
                    cols = slice(j * HALF, (j + 1) * HALF)
                    last = nc.tensor.matmul(ops_[:, cols], v_sb[par][:, m * P:(m + 1) * P], a_sb[m % 2][:, cols],
                                            start=(m == 0), stop=(m == TILES - 1), skip_group_check=True)
                if m == TILES - 1:
                    last.then_inc(o_done.sem, 1)

            def operand(kind):
                if kind == "xT":
                    pe.wait_ge(xn_ready.sem, xn_ready.take())
                pe.wait_ge(p_free.sem, p_free.take())
                if kind == "xT":
                    for t in range(TILES):
                        last = nc.tensor.transpose(pps[0:D, t * P:(t + 1) * P], xn[:, t, :], ident[:, :])
                elif kind == "v":
                    for t in range(TILES):
                        last = nc.tensor.matmul(pps[:, t * P:(t + 1) * P], xT[:, t * P:(t + 1) * P],
                                                w_sb[:, S1:2 * S1], start=True, stop=True)
                else:
                    col = 0 if kind == "u" else 2 * S1
                    for j in range(2):
                        last = nc.tensor.matmul(pps[:, j * HALF:(j + 1) * HALF], w_sb[:, col:col + S1],
                                                xT[:, j * HALF:(j + 1) * HALF], start=True, stop=True)
                        if kind == "base" and j == 0:
                            last.then_inc(xn_free.sem, 1)
                last.then_inc(p_done.sem, 1)

            def project():
                pe.wait_ge(p_free.sem, p_free.take())
                for t in range(TILES):
                    last = nc.tensor.matmul(pps[:, t * D:(t + 1) * D], gated[:, t * P:(t + 1) * P], wo_sb[:, :],
                                            start=True, stop=True)
                last.then_inc(proj_done.sem, 1)

            def body(b, par, has_prev, has_next, settle=True):
                for m in range(TILES):
                    if b is not None:
                        scores(par, m)
                        if m:
                            attend(par, m - 1)
                        elif has_prev:
                            attend(1 - par, TILES - 1)
                    if has_next and 1 <= m <= 4:
                        operand(("xT", "base", "u", "v")[m - 1])
                    if m == 5 and has_prev:
                        project()
                if b is not None and not has_next:
                    attend(par, TILES - 1)
                    pe.wait_ge(gated_done.sem, gated_done.take())
                    project()
                if settle:
                    for q in (scaled, qk_ready, a_ready, gated_done, p_free, xn_ready):
                        q.settle(pe)

            turns(pe, body)

        @block.vector
        def _(dve):
            w.wait(dve)
            nc.vector.memset(xT[D:D + 1, :], 1.0).then_inc(scaled.sem, 1)

            def link(ins):
                ins.then_inc(chain.sem, 1)
                dve.wait_ge(chain.sem, chain.take())

            def gate_output(par):
                dve.wait_ge(o_done.sem, o_done.take())
                nc.vector.tensor_tensor(gated[:, :], ops_[:, :], u_sb[par][:, :], ALU.mult).then_inc(gated_done.sem, 1)

            def add_projection(b):
                dve.wait_ge(proj_done.sem, proj_done.take())
                link(nc.vector.tensor_tensor(proj[:, :, :], pps[:, 0:HALF].rearrange("p (t d) -> p t d", d=D),
                                             shared(bo_sb[:, :], TILES), ALU.add))
                nc.vector.tensor_tensor(batch(h_sb, b), batch(h_sb, b), proj[:, :, :], ALU.add).then_inc(p_free.sem, 1)

            def measure_mean(b):
                dve.drain()
                link(nc.vector.reduce_sum(batch(mean, b), batch(h_sb, b), AX.X))
                nc.vector.tensor_scalar(batch(mean, b), batch(mean, b), 1.0 / D, None, ALU.mult).then_inc(mean_done.sem, 1)

            def measure_variance(b):
                dve.wait_ge(squared.sem, squared.take())
                nc.vector.reduce_sum(batch(var, b), centred[:, :, :], AX.X)

            def body(b, par, has_prev, has_next, settle=True):
                for m in range(TILES):
                    if b is not None:
                        dve.wait_ge(s_done.sem, s_done.take())
                        nc.vector.tensor_scalar(a_sb[m % 2][:, :], sps[m % 2][:, :], 0.0, S1 ** -0.5, ALU.max,
                                                ALU.mult).then_inc(relu_done.sem, 1)
                    if m == 0 and has_prev:
                        gate_output(1 - par)
                    if m == 4 and has_next:
                        dve.wait_ge(base_done.sem, base_done.take())
                        for i in range(2):
                            nc.vector.tensor_scalar(full[i][:, :], base[:, :], gb[:, i:i + 1], gb[:, i + 2:i + 3],
                                                    ALU.mult, ALU.add)
                            nc.vector.tensor_scalar(high[i][1 - par][:, :], base[:, :], gb[:, i:i + 1],
                                                    gb[:, i + 2:i + 3], ALU.mult, ALU.add).then_inc(split.sem, 1)
                    if m == 6 and has_prev:
                        add_projection(b - 1)
                        measure_mean(b - 1)
                if has_prev:
                    measure_variance(b - 1)
                if b is not None and not has_next:
                    gate_output(par)
                    add_projection(b)
                    measure_mean(b)
                    measure_variance(b)
                if settle:
                    for q in (squared, chain, o_done, proj_done, s_done, base_done):
                        q.settle(dve)
            turns(dve, body)

        @block.scalar
        def _(act):
            w.wait(act)

            def body(b, par, has_prev, has_next, settle=True):
                for m in range(TILES):
                    if b is not None:
                        act.wait_ge(relu_done.sem, relu_done.take())
                        nc.scalar.activation(a_sb[m % 2][:, :], a_sb[m % 2][:, :],
                                             ACT.Square).then_inc(a_ready.sem, 1)
                    if has_next and 1 <= m <= 4:
                        act.wait_ge(p_done.sem, p_done.take())
                        if m == 1:
                            nc.scalar.activation(xT[0:D, :], pps[0:D, :], ACT.Copy).then_inc(p_free.sem, 1)
                        elif m == 2:
                            nc.scalar.activation(base[:, :], pps[:, :], ACT.Silu).then_inc(p_free.sem, 1)
                            act.drain().then_inc(base_done.sem, 1)
                        else:
                            nc.scalar.activation((u_sb if m == 3 else v_sb)[1 - par][:, :], pps[:, :],
                                                 ACT.Silu).then_inc(p_free.sem, 1)
                for _ in range(has_prev + (b is not None and not has_next)):
                    act.wait_ge(centred_done.sem, centred_done.take())
                    nc.scalar.activation(centred[:, :, :], centred[:, :, :], ACT.Square).then_inc(squared.sem, 1)
                if settle:
                    for q in (p_done, relu_done, centred_done):
                        q.settle(act)
            turns(act, body)


HID1 = 128
ROW_W2, ROW_B2, ROW_B1 = HID1, HID1 + D, HID1 + 2 * D
ROW = HID1 + 2 * D + 1
CAPACITY = float(-(-NB * T * 5 // (4 * EXPERTS)))


def emit_routing(nc, h_sb, stats, ident, y_all, w, route_i, route_w):
    mean, r1 = stats[:, 0, :], stats[:, 2, :]
    CH = 4
    n, nb = NT // CH, NB // CH
    with ExitStack() as ctx:
        sb = lambda name, shape, dt=F32: ctx.enter_context(nc.sbuf_tensor(name, shape, dt))
        ysum = sb("ysum", [P, NB, D])
        token_share = sb("token_share", [P, 1])
        ones = sb("ones", [NB, P])
        row_i = sb("row_i", [P, 1], I32)
        row_f = sb("row_f", [P, 1])
        tokens_mean = sb("tokens_mean", [D, NB])
        logits, exps, probs, scale = (sb(f"r_{x}", [NB, EXPERTS]) for x in ("logits", "exps", "probs", "scale"))
        top = sb("r_top", [NB, 8])
        top_i = sb("r_top_i", [NB, 8], U32)
        nmax, total, gap, e2, den = (sb(f"r_{x}", [NB, 1]) for x in ("nmax", "total", "gap", "e2", "den"))
        four = sb("r_four", [NB, 4])
        four_diag = sb("r_four_diag", [NB, 4, NB])
        rows = sb("r_rows", [P, NB, 2])
        ps = [ctx.enter_context(nc.psum_tensor(f"r_ps{i}", [P, HALF], F32)) for i in range(4)]
        sem = lambda name: ctx.enter_context(nc.semaphore("r_" + name))
        consts, centred, scaled, summed, means_done, means_ready, logits_done, shifted, exped, \
            probs_ready, loads_done, gap_ready, e2_ready, four_ready, four_done, chain = (
                sem(x) for x in ("consts", "centred", "scaled", "summed", "means_done", "means_ready",
                                 "logits_done", "shifted", "exped", "probs_ready", "loads_done", "gap_ready",
                                 "e2_ready", "four_ready", "four_done", "chain"))
        block = ctx.enter_context(nc.Block())
        part = lambda t, c: t[:, c * n:(c + 1) * n]

        @block.gpsimd
        def _(pool):
            pool.memset(token_share[:, :], 1.0 / T)
            pool.memset(ones[:, :], 1.0)
            pool.iota(row_i[:, :], pattern=[[0, 1]], base=0, channel_multiplier=1).then_inc(consts, 1)
            for c in range(CH):
                pool.wait_ge(centred, c + 1)
                nc.gpsimd.tensor_tensor(part(y_all, c), part(y_all, c), wide(part(r1, c), D), ALU.mult).then_inc(scaled, 1)

        @block.tensor
        def _(pe):
            pe.wait_ge(consts, 1)
            w.wait(pe)
            for b in range(NB):
                if b % nb == 0:
                    pe.wait_ge(summed, b // nb + 1)
                last = nc.tensor.matmul(ps[0][0:D, b:b + 1], ysum[:, b, :], token_share[:, :], start=True, stop=True)
            last.then_inc(means_done, 1)
            pe.wait_ge(means_ready, 1)
            nc.tensor.matmul(ps[1][0:NB, 0:EXPERTS], tokens_mean[:, :], w.wr[:, :], start=True,
                             stop=True).then_inc(logits_done, 1)
            pe.wait_ge(probs_ready, 1)
            nc.tensor.matmul(ps[2][0:NB, 0:EXPERTS], ones[:, 0:NB], probs[:, :], start=True,
                             stop=True).then_inc(loads_done, 1)
            pe.wait_ge(four_ready, 1)
            nc.tensor.matmul(ps[3][:, 0:4 * NB], ones[:, :], four_diag[:, :, :].rearrange("p k b -> p (k b)"),
                             start=True, stop=True).then_inc(four_done, 1)

        @block.scalar
        def _(act):
            for i in range(2):
                act.wait_ge(shifted, i + 1)
                nc.scalar.activation(exps[:, :], logits[:, :], ACT.Exp, bias=nmax[:, :], scale=1.0,
                                     accum_out=total[:, :])
                act.drain().then_inc(exped, 1)
            act.wait_ge(gap_ready, 1)
            nc.scalar.activation(e2[:, :], gap[:, :], ACT.Exp).then_inc(e2_ready, 1)

        @block.vector
        def _(dve):
            links = [0]

            def link(ins):
                links[0] += 1
                ins.then_inc(chain, 1)
                dve.wait_ge(chain, links[0])

            def softmax(i):
                nc.vector.tensor_reduce(nmax[:, :], logits[:, :], axis=AX.X, op=ALU.max, negate=True).then_inc(shifted, 1)
                dve.wait_ge(exped, i + 1)
                link(nc.vector.reciprocal(den[:, :], total[:, :]))
                return nc.vector.tensor_scalar(probs[:, :], exps[:, :], den[:, :], None, ALU.mult)

            def centre(c):
                nc.vector.tensor_tensor(part(y_all, c), part(h_sb, c), wide(part(mean, c), D),
                                        ALU.subtract).then_inc(centred, 1)

            centre(0)
            for c in range(CH):
                if c + 1 < CH:
                    centre(c + 1)
                dve.wait_ge(scaled, c + 1)
                nc.vector.reduce_sum(ysum[:, c * nb:(c + 1) * nb, :],
                                     part(y_all, c).rearrange("p (b t) d -> p b d t", t=TILES), AX.X).then_inc(summed, 1)
            dve.wait_ge(consts, 1)
            w.wait(dve)
            nc.vector.tensor_copy(row_f[:, :], row_i[:, :])
            dve.wait_ge(means_done, 1)
            nc.vector.tensor_copy(tokens_mean[:, :], ps[0][0:D, 0:NB]).then_inc(means_ready, 1)
            dve.wait_ge(logits_done, 1)
            link(nc.vector.tensor_tensor(logits[:, :], ps[1][0:NB, 0:EXPERTS], w.br[:, :], ALU.add))
            softmax(0).then_inc(probs_ready, 1)
            dve.wait_ge(loads_done, 1)
            link(nc.vector.tensor_scalar(scale[:, :], ps[2][0:NB, 0:EXPERTS], float(T), CAPACITY, ALU.mult, ALU.max))
            link(nc.vector.reciprocal(scale[:, :], scale[:, :]))
            link(nc.vector.scalar_tensor_tensor(logits[:, :], scale[:, :], CAPACITY, probs[:, :], ALU.mult, ALU.mult))
            link(softmax(1))
            link(nc.vector.max(top[:, :], probs[:, :]))
            nc.vector.tensor_tensor(gap[:, :], top[:, 1:2], top[:, 0:1], ALU.subtract).then_inc(gap_ready, 1)
            link(nc.vector.max_index(top_i[:, :], top[:, :], probs[:, :]))
            nc.vector.tensor_copy(four[:, 0:2], top_i[:, 0:2])
            dve.wait_ge(e2_ready, 1)
            link(nc.vector.tensor_scalar(den[:, :], e2[:, :], 1.0, None, ALU.add))
            link(nc.vector.reciprocal(four[:, 2:3], den[:, :]))
            link(nc.vector.tensor_tensor(four[:, 3:4], e2[:, :], four[:, 2:3], ALU.mult))
            nc.vector.tensor_tensor(four_diag[:, :, :], wide(four[:, :], NB), shared(ident[0:NB, 0:NB], 4),
                                    ALU.mult).then_inc(four_ready, 1)
            dve.wait_ge(four_done, 1)
            four_all = ps[3][:, 0:4 * NB].rearrange("p (k b) -> p k b", b=NB)
            nc.vector.tensor_copy(route_w[:, :, :], four_all[:, 2:4, :])
            link(nc.vector.tensor_scalar(rows[:, :, :], four_all[:, 0:2, :].rearrange("p k b -> p b k"), float(P),
                                         row_f[:, :], ALU.mult, ALU.add))
            nc.vector.tensor_copy(route_i[:, :, :], rows[:, :, :])


def emit_moe1(nc, h_sb, stats, ident, w, table, out):
    with ExitStack() as outer:
        keep = lambda name, shape, dt=F32: outer.enter_context(nc.sbuf_tensor(name, shape, dt))
        y_all = keep("y_all", [P, NT, D])
        route_i = keep("route_i", [P, NB, 2], I32)
        route_w = keep("route_w", [P, 2, NB])
        emit_routing(nc, h_sb, stats, ident, y_all, w, route_i, route_w)
        emit_experts(nc, h_sb, ident, y_all, route_i, route_w, w, table, out)


def emit_experts(nc, h_sb, ident, y_all, route_i, route_w, weights, table, out):
    with ExitStack() as ctx:
        sb = lambda name, shape, dt=F32: ctx.enter_context(nc.sbuf_tensor(name, shape, dt))
        two = lambda name, shape, dt=F32: [sb(f"{name}_{i}", shape, dt) for i in range(2)]
        idx = two("m1_idx", [P, 2], I32)
        w_g = two("m1_w", [P, 2, ROW])
        w1s = two("m1_w1s", [P, 2, HID1])
        b1s = two("m1_b1s", [P, 2])
        w2s = two("m1_w2s", [P, 2, D])
        b2w = two("m1_b2w", [P, D])
        b2s = two("m1_b2s", [P, D])
        y_b = two("m1_y", [P, TILES, D])
        yT = two("m1_yT", [P, HALF])
        hid = two("m1_hid", [P, 2 * HALF])
        oT = sb("m1_oT", [P, HALF])
        base = two("m1_base", [P, TILES, D])
        z = two("m1_z", [P, TILES, D])
        sq = sb("m1_sq", [P, TILES, D])
        zm = sb("m1_zm", [P, TILES])
        zv = two("m1_zv", [P, TILES])
        rstd = sb("m1_rstd", [P, TILES])
        half = sb("m1_half", [P, TILES])
        yps = [ctx.enter_context(nc.psum_tensor(f"m1_yps{i}", [P, HALF], F32)) for i in range(2)]
        hps = [ctx.enter_context(nc.psum_tensor(f"m1_hps{i}", [P, 2 * HALF], F32)) for i in range(2)]
        oTps = ctx.enter_context(nc.psum_tensor("m1_oTps", [P, HALF], F32))
        xps = ctx.enter_context(nc.psum_tensor("m1_xps", [P, HALF], F32))

        s = lambda name, credits=0: Signal(ctx, nc, "m1_" + name, credits)
        stored = ctx.enter_context(nc.semaphore("m1_stored"))
        landed = [ctx.enter_context(nc.semaphore(f"m1_landed{i}")) for i in range(2)]
        idx_copied = s("idx_copied")
        y_ready = s("y_ready")
        x_done = s("x_done")
        yT_ready = s("yT_ready")
        w_ready = s("w_ready")
        b2_ready = s("b2_ready")
        base_ready = s("base_ready")
        h_done = s("h_done")
        gelu_done = s("gelu_done")
        oT_done = s("oT_done")
        oT_ready = s("oT_ready")
        out_done = s("out_done")
        centred = s("centred")
        squared = s("squared")
        var_ready = s("var_ready")
        rstd_ready = s("rstd_ready")
        z_ready = s("z_ready")
        h_ready = s("h_ready")
        chain = s("chain")
        pool_done = s("pool_done")
        block = ctx.enter_context(nc.Block())

        def turns(eng, body):
            body(-1, 1, 1, prev=False, this=False)
            body(0, 0, 1, prev=False)
            with eng.Fori(0, NB // 2 - 2) as r:
                body(r * 2 + 1, 1, r + 2, settle=False)
                body(r * 2 + 2, 0, r + 2)
            body(NB - 3, 1, NB // 2)
            body(NB - 2, 0, NB // 2, ahead=False)
            body(NB - 1, 1, None, next=False, ahead=False)
            body(NB, 0, None, this=False, next=False, ahead=False, settle=False)

        @block.sync
        def _(sp):
            def body(i, par, count, prev=True, this=True, next=True, ahead=True, settle=True):
                if prev:
                    sp.wait_ge(h_ready.sem, h_ready.take())
                    sp.dma_start(out[bass.ds(i - 1, 1)].rearrange("b (p t) d -> p (b t) d", t=TILES),
                                 batch(h_sb, i - 1)).then_inc(stored, 16)
                if settle:
                    h_ready.settle(sp)
            turns(sp, body)
            sp.wait_ge(stored, NB * 16)

        @block.gpsimd
        def _(pool):
            pool.memset(half[:, :], -0.5).then_inc(pool_done.sem, 1)
            pool.wait_ge(pool_done.sem, pool_done.take())

            def gather(buf, b):
                nc.gpsimd.tensor_copy(idx[buf][:, :], route_i[:, bass.ds(b, 1), :].rearrange("p b k -> p (b k)")
                                      ).then_inc(idx_copied.sem, 1)
                pool.wait_ge(idx_copied.sem, idx_copied.take())
                for k in range(2):
                    pool.indirect_dma_start(
                        out=w_g[buf][:, k, :], out_offset=None, in_=table[:, :],
                        in_offset=bass.IndirectOffsetOnAxis(ap=idx[buf][:, k:k + 1], axis=0),
                    ).then_inc(landed[buf], 16)

            gather(0, 0)

            def body(i, par, count, prev=True, this=True, next=True, ahead=True, settle=True):
                nxt = 1 - par
                if ahead:
                    gather(par, i + 2)
                if prev:
                    pool.wait_ge(var_ready.sem, var_ready.take())
                    nc.gpsimd.tensor_tensor(rstd[:, :], zv[nxt][:, :], half[:, :], ALU.pow).then_inc(rstd_ready.sem, 1)
                    pool.wait_ge(z_ready.sem, z_ready.take())
                    nc.gpsimd.tensor_tensor(batch(h_sb, i - 1), batch(h_sb, i - 1), z[nxt][:, :, :],
                                            ALU.add).then_inc(h_ready.sem, 1)
                if next:
                    pool.wait_ge(b2_ready.sem, b2_ready.take())
                    nc.gpsimd.tensor_tensor(base[nxt][:, :, :], batch(y_all, i + 1), shared(b2s[nxt][:, :], TILES),
                                            ALU.add).then_inc(base_ready.sem, 1)
                if settle:
                    for q in (idx_copied, var_ready, z_ready, b2_ready, pool_done):
                        q.settle(pool)
            turns(pool, body)

        @block.tensor
        def _(pe):
            def body(i, par, count, prev=True, this=True, next=True, ahead=True, settle=True):
                nxt = 1 - par
                if next:
                    pe.wait_ge(y_ready.sem, y_ready.take())
                    if this:
                        pe.wait_ge(yT_ready.sem, yT_ready.take())
                    for j in range(TILES // 2):
                        last = nc.tensor.transpose(xps[:, j * P:(j + 1) * P],
                                                   y_b[nxt][:, 2 * j:2 * j + 2, :].rearrange("p t d -> p (t d)"),
                                                   ident[:, :])
                    last.then_inc(x_done.sem, 1)
                if this and not next:
                    pe.wait_ge(yT_ready.sem, yT_ready.take())
                for k in range(2):
                    if this:
                        if k == 0:
                            pe.wait_ge(w_ready.sem, w_ready.take())
                        for odd in range(2):
                            rows = slice(odd * D, (odd + 1) * D)
                            last = nc.tensor.matmul(hps[k][:, odd * HALF:(odd + 1) * HALF], w1s[par][rows, k, :],
                                                    yT[par][rows, :], start=True, stop=True)
                        last.then_inc(h_done.sem, 1)
                    if k == 0 and prev:
                        if not this:
                            pe.drain()
                        pe.wait_ge(oT_ready.sem, oT_ready.take())
                        for j in range(TILES // 2):
                            last = nc.tensor.transpose(yps[nxt][:, j * P:(j + 1) * P], oT[:, j * P:(j + 1) * P],
                                                       ident[:, :])
                        last.then_inc(out_done.sem, 1)
                if this:
                    for k in range(2):
                        pe.wait_ge(gelu_done.sem, gelu_done.take())
                        for odd in range(2):
                            last = nc.tensor.matmul(oTps[odd * D:(odd + 1) * D, :], w2s[par][:, k, :],
                                                    hid[k][:, odd * HALF:(odd + 1) * HALF], start=(k == 0), stop=(k == 1),
                                                    skip_group_check=True)
                    last.then_inc(oT_done.sem, 1)
                if settle:
                    for q in (y_ready, yT_ready, w_ready, gelu_done, oT_ready):
                        q.settle(pe)
            turns(pe, body)

        @block.scalar
        def _(act):
            nc.scalar.activation(y_b[0][:, :, :], batch(y_all, 0), ACT.Copy).then_inc(y_ready.sem, 1)

            def body(i, par, count, prev=True, this=True, next=True, ahead=True, settle=True):
                nxt = 1 - par
                if prev:
                    act.wait_ge(oT_done.sem, oT_done.take())
                    nc.scalar.activation(oT[:, :], oTps[:, :], ACT.Copy).then_inc(oT_ready.sem, 1)
                if next:
                    act.wait_ge(x_done.sem, x_done.take())
                    nc.scalar.activation(yT[nxt][:, :], xps[:, :], ACT.Copy).then_inc(yT_ready.sem, 1)
                if this:
                    for k in range(2):
                        act.wait_ge(h_done.sem, h_done.take())
                        nc.scalar.activation(hid[k][:, :], hps[k][:, :], ACT.Gelu,
                                             bias=b1s[par][:, k:k + 1], scale=1.0).then_inc(gelu_done.sem, 1)
                if ahead:
                    nc.scalar.activation(y_b[par][:, :, :], batch(y_all, i + 2), ACT.Copy).then_inc(y_ready.sem, 1)
                if prev:
                    act.wait_ge(centred.sem, centred.take())
                    nc.scalar.activation(sq[:, :, :], z[nxt][:, :, :], ACT.Square).then_inc(squared.sem, 1)
                if settle:
                    for q in (x_done, h_done, centred, oT_done):
                        q.settle(act)
            turns(act, body)

        @block.vector
        def _(dve):
            weights.wait(dve)

            def link(ins):
                ins.then_inc(chain.sem, 1)
                dve.wait_ge(chain.sem, chain.take())

            def body(i, par, count, prev=True, this=True, next=True, ahead=True, settle=True):
                nxt = 1 - par
                if prev:
                    zb, mb = z[nxt][:, :, :], zm[:, :]
                    dve.wait_ge(base_ready.sem, base_ready.take())
                    dve.wait_ge(out_done.sem, out_done.take())
                    link(nc.vector.tensor_tensor(zb, yps[nxt][:, :].rearrange("p (t d) -> p t d", d=D),
                                                 base[nxt][:, :, :], ALU.add))
                    link(nc.vector.reduce_sum(mb, zb, AX.X))
                    link(nc.vector.tensor_scalar(mb, mb, 1.0 / D, None, ALU.mult))
                    nc.vector.tensor_tensor(zb, zb, wide(mb, D), ALU.subtract).then_inc(centred.sem, 1)
                if next:
                    dve.wait_ge(landed[nxt], count * 32)
                    w = [route_w[:, k, bass.ds(i + 1, 1)] for k in range(2)]
                    nc.vector.tensor_scalar(b2w[nxt][:, :], w_g[nxt][:, 0, ROW_B2:ROW_B2 + D], w[0], None, ALU.mult)
                    nc.vector.tensor_copy(w1s[nxt][:, :, :], w_g[nxt][:, :, 0:HID1])
                    nc.vector.tensor_copy(b1s[nxt][:, :], w_g[nxt][:, :, ROW_B1])
                    for k in range(2):
                        last = nc.vector.tensor_scalar(w2s[nxt][:, k, :], w_g[nxt][:, k, ROW_W2:ROW_W2 + D], w[k], None,
                                                       ALU.mult)
                    last.then_inc(w_ready.sem, 1)
                    link(dve.drain())
                    nc.vector.scalar_tensor_tensor(b2s[nxt][:, :], w_g[nxt][:, 1, ROW_B2:ROW_B2 + D], w[1], b2w[nxt][:, :],
                                                   ALU.mult, ALU.add).then_inc(b2_ready.sem, 1)
                if prev:
                    dve.wait_ge(squared.sem, squared.take())
                    link(nc.vector.reduce_sum(zv[nxt][:, :], sq[:, :, :], AX.X))
                    nc.vector.tensor_scalar(zv[nxt][:, :], zv[nxt][:, :], 1.0 / D, EPS, ALU.mult,
                                            ALU.add).then_inc(var_ready.sem, 1)
                    link(nc.vector.tensor_tensor(zb, zb, shared(weights.gamma[:, :], TILES), ALU.mult))
                    dve.wait_ge(rstd_ready.sem, rstd_ready.take())
                    link(nc.vector.tensor_tensor(zb, zb, wide(rstd[:, :], D), ALU.mult))
                    nc.vector.tensor_tensor(zb, zb, shared(weights.beta[:, :], TILES), ALU.add).then_inc(z_ready.sem, 1)
                if settle:
                    for q in (base_ready, out_done, squared, rstd_ready, chain):
                        q.settle(dve)
            turns(dve, body)


INS = {
    "x": ((NB, T), I32), "table": ((VOCAB + 2 * PAD, D), F32), "conv_w": ((KS * D, D), F32), "conv_b": ((D,), F32),
    "qkv_w": ((D, 3 * HEADS * DH), F32), "gate_w": ((D, HEADS * DH), F32), "gate_b": ((P, GROUPS), F32),
    "fin_w": ((HEADS * DH, D), F32), "fin_b": ((D,), F32), "ln_gamma": ((D,), F32), "ln_beta": ((D,), F32),
    "m0_wr": ((D, EXPERTS), F32), "m0_br": ((EXPERTS,), F32), "m0_lng": ((D, EXPERTS), F32),
    "m0_lnb": ((D, EXPERTS), F32), "m0_w1": ((EXPERTS, D, HID0), F32), "m0_b1": ((P, HT), F32),
    "m0_w2": ((EXPERTS, HID0, D), F32), "m0_b2": ((D, EXPERTS), F32),
    "a1_g": ((1,), F32), "a1_wuv": ((D, 3 * S1), F32), "a1_buv": ((3 * S1,), F32), "a1_gamma": ((S1, 2), F32),
    "a1_beta": ((S1, 2), F32), "a1_wo": ((S1, D), F32), "a1_bo": ((D,), F32),
    "m1_wr": ((D, EXPERTS), F32), "m1_br": ((EXPERTS,), F32), "m1_table": ((EXPERTS * P, ROW), F32),
    "m1_gamma": ((D,), F32), "m1_beta": ((D,), F32),
}


def build(nc, a, out):
    with ExitStack() as ctx:
        h_sb = ctx.enter_context(nc.sbuf_tensor("h", [P, NT, D], F32))
        stats = ctx.enter_context(nc.sbuf_tensor("stats", [P, 5, NT], F32))
        ident = ctx.enter_context(nc.sbuf_tensor("ident", [P, P], F32))
        emit_identity(nc, ctx, ident)
        part = lambda prefix, names: [a[prefix + n] for n in names.split()]
        w_a0 = attention0_weights(ctx, nc, *part("", "qkv_w gate_w gate_b fin_w fin_b ln_gamma ln_beta"))
        w_m0 = moe0_weights(ctx, nc, *part("m0_", "wr br lng lnb w1 b1 w2 b2"))
        w_a1 = attention1_weights(ctx, nc, *part("a1_", "wuv buv gamma beta wo bo"))
        w_m1 = moe1_weights(ctx, nc, *part("m1_", "wr br gamma beta"))
        emit_embedding(nc, a["x"], a["table"], a["conv_w"], a["conv_b"], h_sb, stats, ident, (w_a0, w_m0, w_a1, w_m1))
        emit_layernorm(nc, "ln1", h_sb, stats, "norm", measured=True)
        emit_attention0(nc, h_sb, stats, ident, w_a0)
        emit_layernorm(nc, "ln2", h_sb, stats, "norm")
        emit_moe0(nc, h_sb, stats, ident, w_m0)
        emit_layernorm(nc, "ln3", h_sb, stats, "rms", a["a1_g"], measured=True)
        emit_attention1(nc, h_sb, stats, ident, w_a1)
        emit_layernorm(nc, "ln4", h_sb, stats, "norm", measured=True)
        emit_moe1(nc, h_sb, stats, ident, w_m1, a["m1_table"], out)


def kernel(**inputs):
    import concourse.bacc as bacc
    from concourse.bass_utils import run_bass_kernel_spmd

    g = {k: np.asarray(v) for k, v in inputs.items()}
    arrays = {
        "x": g["x"], "table": np.pad(g["L0_tok_emb"], ((PAD, PAD), (0, 0)), mode="edge"),
        "conv_w": g["L0_tok_W"].transpose(2, 1, 0).reshape(KS * D, D), "conv_b": g["L0_tok_b"],
        "qkv_w": g["L0_attn_W_qkv"].T, "gate_w": g["L0_attn_W_gate"].T, "gate_b": g["L0_attn_b_gate"].reshape(GROUPS, P).T,
        "fin_w": g["L0_attn_W_final"].T, "fin_b": g["L0_attn_b_final"], "ln_gamma": g["L0_attn_ln_gamma"],
        "ln_beta": g["L0_attn_ln_beta"],
        "m0_wr": g["L0_ffn_Wr"], "m0_br": g["L0_ffn_br"], "m0_lng": g["L0_ffn_ln_g"].T, "m0_lnb": g["L0_ffn_ln_b"].T,
        "m0_w1": g["L0_ffn_W1"], "m0_b1": g["L0_ffn_b1"].reshape(HT, P).T, "m0_w2": g["L0_ffn_W2"],
        "m0_b2": g["L0_ffn_b2"].T,
        "a1_g": g["L1_attn_g"].reshape(1), "a1_wuv": g["L1_attn_W_uv"], "a1_buv": g["L1_attn_b_uv"],
        "a1_gamma": g["L1_attn_gamma"].T, "a1_beta": g["L1_attn_beta"].T, "a1_wo": g["L1_attn_W_o"],
        "a1_bo": g["L1_attn_b_o"],
        "m1_wr": g["L1_ffn_Wr"], "m1_br": g["L1_ffn_br"], "m1_gamma": g["L1_ffn_gamma"], "m1_beta": g["L1_ffn_beta"],
        "m1_table": np.concatenate([
            np.tile(g["L1_ffn_W1"], (1, P // D, 1)), g["L1_ffn_W2"],
            np.broadcast_to(g["L1_ffn_b2"][:, None, :], (EXPERTS, P, D)), g["L1_ffn_b1"][:, :, None],
        ], axis=2).reshape(EXPERTS * P, ROW),
    }
    nc = bacc.Bacc("TRN2", target_bir_lowering=False, num_devices=1)
    aps = {n: nc.dram_tensor(f"in_{n}", shape, dt, kind="ExternalInput").ap() for n, (shape, dt) in INS.items()}
    out = nc.dram_tensor("out_h", (NB, T, D), F32, kind="ExternalOutput").ap()
    build(nc, aps, out)
    r = run_bass_kernel_spmd(nc, [{f"in_{n}": np.ascontiguousarray(arrays[n]) for n in INS}], core_ids=[0])
    return r.results[0]["out_h"]
```
